# Optimizing a Trainium2 kernel written in Bass

```python
import numpy as np
import jax
import jax.numpy as jnp

def _softmax(x, axis=-1):
    return jax.nn.softmax(x, axis=axis)

def _gelu(x):
    return jax.nn.gelu(x, approximate=True)

def _silu(x):
    return jax.nn.silu(x)

def _sigmoid(x):
    return jax.nn.sigmoid(x)

def _layernorm(x, axis=-1, eps=1e-05):
    m = jnp.mean(x, axis=axis, keepdims=True)
    v = jnp.var(x, axis=axis, keepdims=True)
    return (x - m) / jnp.sqrt(v + eps)

def _scatter_add(tgt, idx, src, axis=0):
    return tgt.at[idx].add(src)

def _segment_sum(src, seg, n):
    return jax.ops.segment_sum(src, seg, n)
kernel_name = 'mk_cond_seq_d2_seqx_r4_4bc551'

def setup_inputs(seed: int=0):
    np.random.seed(seed)
    _w = jnp.asarray

    def _rec_inputs():
        import jax
        import jax.numpy as jnp
        _rk = jax.random.key(seed)
        x = 1.648e-05 + 1 * jax.random.normal(jax.random.fold_in(_rk, 1), (2, 1024, 288), jnp.float32)
        _lenS = 1024 - jax.random.randint(jax.random.fold_in(_rk, 7), (2,), 0, max(1, 1024 // 4) + 1, jnp.int32)
        _lenS2 = 1024 - jax.random.randint(jax.random.fold_in(_rk, 8), (2,), 0, max(1, 1024 // 4) + 1, jnp.int32)
        cond_1152 = 0.00914911 + 1.00357 * jax.random.normal(jax.random.fold_in(_rk, 11), (2, 288), jnp.float32)
        return (x, cond_1152)
    x, cond_1152 = _rec_inputs()

    def _L0_cond_setup():
        import jax, jax.numpy as jnp
        import numpy as np
        B, L, C = (8, 256, 288)
        H = 16
        D = C // H
        FF = int(C * 4.0)
        EPS = 1e-06

        def _layernorm(x):
            mu = jnp.mean(x, axis=-1, keepdims=True)
            var = jnp.mean(jnp.square(x - mu), axis=-1, keepdims=True)
            return (x - mu) * jax.lax.rsqrt(var + EPS)

        def _modulate(x, shift, scale):
            return x * (1.0 + scale) + shift

        def _attention(h, W_qkv, b_qkv, W_proj, b_proj):
            b, l, c = h.shape
            qkv = h @ W_qkv + b_qkv
            qkv = qkv.reshape(b, l, 3, H, D)
            q, k, v = (qkv[:, :, 0], qkv[:, :, 1], qkv[:, :, 2])
            scale = D ** (-0.5)
            scores = jnp.einsum('blhd,bmhd->bhlm', q * scale, k)
            attn = jax.nn.softmax(scores, axis=-1)
            o = jnp.einsum('bhlm,bmhd->blhd', attn, v).reshape(b, l, c)
            return o @ W_proj + b_proj
        key = jax.random.key(seed)
        ks = jax.random.split(key, 12)
        s = 0.02
        return {'x': jax.random.normal(ks[0], (B, L, C), jnp.float32), 'c': jax.random.normal(ks[1], (B, 1, C), jnp.float32), 'W_qkv': jax.random.normal(ks[2], (C, 3 * C), jnp.float32) * s, 'b_qkv': jnp.zeros((3 * C,), jnp.float32), 'W_proj': jax.random.normal(ks[3], (C, C), jnp.float32) * s, 'b_proj': jnp.zeros((C,), jnp.float32), 'W_fc1': jax.random.normal(ks[4], (C, FF), jnp.float32) * s, 'b_fc1': jnp.zeros((FF,), jnp.float32), 'W_fc2': jax.random.normal(ks[5], (FF, C), jnp.float32) * s, 'b_fc2': jnp.zeros((C,), jnp.float32), 'W_ada': jax.random.normal(ks[6], (C, 6 * C), jnp.float32) * s, 'b_ada': jnp.zeros((6 * C,), jnp.float32)}
    _L0_cond_all = _L0_cond_setup()
    _L0_cond_in = {k: v for k, v in _L0_cond_all.items() if k in ('W_qkv', 'b_qkv', 'W_proj', 'b_proj', 'W_fc1', 'b_fc1', 'W_fc2', 'b_fc2', 'W_ada', 'b_ada')}
    del _L0_cond_all

    def _L1_cond_setup():
        import jax, jax.numpy as jnp
        import numpy as np
        N, T, D, H = (32, 256, 288, 16)
        DH = D // H
        MLP = int(D * 4.0)
        EPS = 1e-06

        def _layernorm(x):
            m = jnp.mean(x, axis=-1, keepdims=True)
            v = jnp.var(x, axis=-1, keepdims=True)
            return (x - m) * jax.lax.rsqrt(v + EPS)

        def _modulate(x, shift, scale):
            return x * (1.0 + scale[:, None, :]) + shift[:, None, :]

        def _attention(x, qkv_w, qkv_b, proj_w, proj_b):
            n, t, d = x.shape
            scale = DH ** (-0.5)
            qkv = x @ qkv_w + qkv_b
            qkv = qkv.reshape(n, t, 3, H, DH)
            q, k, v = (qkv[:, :, 0], qkv[:, :, 1], qkv[:, :, 2])
            attn = jnp.einsum('nthd,ntkd->nthk', q * scale, k)
            attn = jax.nn.softmax(attn, axis=-1)
            out = jnp.einsum('nthk,ntkd->nthd', attn, v)
            out = out.transpose(0, 2, 1, 3).reshape(n, t, d)
            return out @ proj_w + proj_b

        def _mlp(x, fc1_w, fc1_b, fc2_w, fc2_b):
            h = jax.nn.gelu(x @ fc1_w + fc1_b, approximate=False)
            return h @ fc2_w + fc2_b
        key = jax.random.key(seed)
        ks = jax.random.split(key, 14)
        s = 0.02
        return {'x': jax.random.normal(ks[0], (N, T, D), jnp.float32), 'c': jax.random.normal(ks[1], (N, D), jnp.float32), 'qkv_w': jax.random.normal(ks[2], (D, 3 * D), jnp.float32) * s, 'qkv_b': jax.random.normal(ks[3], (3 * D,), jnp.float32) * s, 'proj_w': jax.random.normal(ks[4], (D, D), jnp.float32) * s, 'proj_b': jax.random.normal(ks[5], (D,), jnp.float32) * s, 'fc1_w': jax.random.normal(ks[6], (D, MLP), jnp.float32) * s, 'fc1_b': jax.random.normal(ks[7], (MLP,), jnp.float32) * s, 'fc2_w': jax.random.normal(ks[8], (MLP, D), jnp.float32) * s, 'fc2_b': jax.random.normal(ks[9], (D,), jnp.float32) * s, 'ada_w': jax.random.normal(ks[10], (D, 6 * D), jnp.float32) * s, 'ada_b': jax.random.normal(ks[11], (6 * D,), jnp.float32) * s}
    _L1_cond_all = _L1_cond_setup()
    _L1_cond_in = {k: v for k, v in _L1_cond_all.items() if k in ('qkv_w', 'qkv_b', 'proj_w', 'proj_b', 'fc1_w', 'fc1_b', 'fc2_w', 'fc2_b', 'ada_w', 'ada_b')}
    del _L1_cond_all
    return {'x': x, 'cond_1152': cond_1152, 'L0_cond_W_qkv': _L0_cond_in['W_qkv'], 'L0_cond_b_qkv': _L0_cond_in['b_qkv'], 'L0_cond_W_proj': _L0_cond_in['W_proj'], 'L0_cond_b_proj': _L0_cond_in['b_proj'], 'L0_cond_W_fc1': _L0_cond_in['W_fc1'], 'L0_cond_b_fc1': _L0_cond_in['b_fc1'], 'L0_cond_W_fc2': _L0_cond_in['W_fc2'], 'L0_cond_b_fc2': _L0_cond_in['b_fc2'], 'L0_cond_W_ada': _L0_cond_in['W_ada'], 'L0_cond_b_ada': _L0_cond_in['b_ada'], 'L1_cond_qkv_w': _L1_cond_in['qkv_w'], 'L1_cond_qkv_b': _L1_cond_in['qkv_b'], 'L1_cond_proj_w': _L1_cond_in['proj_w'], 'L1_cond_proj_b': _L1_cond_in['proj_b'], 'L1_cond_fc1_w': _L1_cond_in['fc1_w'], 'L1_cond_fc1_b': _L1_cond_in['fc1_b'], 'L1_cond_fc2_w': _L1_cond_in['fc2_w'], 'L1_cond_fc2_b': _L1_cond_in['fc2_b'], 'L1_cond_ada_w': _L1_cond_in['ada_w'], 'L1_cond_ada_b': _L1_cond_in['ada_b']}

def reference(x, cond_1152, L0_cond_W_qkv, L0_cond_b_qkv, L0_cond_W_proj, L0_cond_b_proj, L0_cond_W_fc1, L0_cond_b_fc1, L0_cond_W_fc2, L0_cond_b_fc2, L0_cond_W_ada, L0_cond_b_ada, L1_cond_qkv_w, L1_cond_qkv_b, L1_cond_proj_w, L1_cond_proj_b, L1_cond_fc1_w, L1_cond_fc1_b, L1_cond_fc2_w, L1_cond_fc2_b, L1_cond_ada_w, L1_cond_ada_b):
    import jax
    import jax.numpy as jnp

    def _L0_cond_ref(x, c, W_qkv, b_qkv, W_proj, b_proj, W_fc1, b_fc1, W_fc2, b_fc2, W_ada, b_ada):
        import jax, jax.numpy as jnp
        import numpy as np
        B, L, C = (8, 256, 288)
        H = 16
        D = C // H
        FF = int(C * 4.0)
        EPS = 1e-06

        def _layernorm(x):
            mu = jnp.mean(x, axis=-1, keepdims=True)
            var = jnp.mean(jnp.square(x - mu), axis=-1, keepdims=True)
            return (x - mu) * jax.lax.rsqrt(var + EPS)

        def _modulate(x, shift, scale):
            return x * (1.0 + scale) + shift

        def _attention(h, W_qkv, b_qkv, W_proj, b_proj):
            b, l, c = h.shape
            qkv = h @ W_qkv + b_qkv
            qkv = qkv.reshape(b, l, 3, H, D)
            q, k, v = (qkv[:, :, 0], qkv[:, :, 1], qkv[:, :, 2])
            scale = D ** (-0.5)
            scores = jnp.einsum('blhd,bmhd->bhlm', q * scale, k)
            attn = jax.nn.softmax(scores, axis=-1)
            o = jnp.einsum('bhlm,bmhd->blhd', attn, v).reshape(b, l, c)
            return o @ W_proj + b_proj
        ada = jax.nn.silu(c) @ W_ada + b_ada
        shift_msa, scale_msa, gate_msa, shift_mlp, scale_mlp, gate_mlp = jnp.split(ada, 6, axis=-1)
        h = _modulate(_layernorm(x), shift_msa, scale_msa)
        x = x + gate_msa * _attention(h, W_qkv, b_qkv, W_proj, b_proj)
        h = _modulate(_layernorm(x), shift_mlp, scale_mlp)
        mlp = jax.nn.gelu(h @ W_fc1 + b_fc1, approximate=True) @ W_fc2 + b_fc2
        x = x + gate_mlp * mlp
        return x

    def _L1_cond_ref(x, c, qkv_w, qkv_b, proj_w, proj_b, fc1_w, fc1_b, fc2_w, fc2_b, ada_w, ada_b):
        import jax, jax.numpy as jnp
        import numpy as np
        N, T, D, H = (32, 256, 288, 16)
        DH = D // H
        MLP = int(D * 4.0)
        EPS = 1e-06

        def _layernorm(x):
            m = jnp.mean(x, axis=-1, keepdims=True)
            v = jnp.var(x, axis=-1, keepdims=True)
            return (x - m) * jax.lax.rsqrt(v + EPS)

        def _modulate(x, shift, scale):
            return x * (1.0 + scale[:, None, :]) + shift[:, None, :]

        def _attention(x, qkv_w, qkv_b, proj_w, proj_b):
            n, t, d = x.shape
            scale = DH ** (-0.5)
            qkv = x @ qkv_w + qkv_b
            qkv = qkv.reshape(n, t, 3, H, DH)
            q, k, v = (qkv[:, :, 0], qkv[:, :, 1], qkv[:, :, 2])
            attn = jnp.einsum('nthd,ntkd->nthk', q * scale, k)
            attn = jax.nn.softmax(attn, axis=-1)
            out = jnp.einsum('nthk,ntkd->nthd', attn, v)
            out = out.transpose(0, 2, 1, 3).reshape(n, t, d)
            return out @ proj_w + proj_b

        def _mlp(x, fc1_w, fc1_b, fc2_w, fc2_b):
            h = jax.nn.gelu(x @ fc1_w + fc1_b, approximate=False)
            return h @ fc2_w + fc2_b
        ada = jax.nn.silu(c) @ ada_w + ada_b
        shift_msa, scale_msa, gate_msa, shift_mlp, scale_mlp, gate_mlp = jnp.split(ada, 6, axis=1)
        x = x + gate_msa[:, None, :] * _attention(_modulate(_layernorm(x), shift_msa, scale_msa), qkv_w, qkv_b, proj_w, proj_b)
        x = x + gate_mlp[:, None, :] * _mlp(_modulate(_layernorm(x), shift_mlp, scale_mlp), fc1_w, fc1_b, fc2_w, fc2_b)
        return x
    x = _L0_cond_ref(x, cond_1152[:, None, :], L0_cond_W_qkv, L0_cond_b_qkv, L0_cond_W_proj, L0_cond_b_proj, L0_cond_W_fc1, L0_cond_b_fc1, L0_cond_W_fc2, L0_cond_b_fc2, L0_cond_W_ada, L0_cond_b_ada)
    x = _L1_cond_ref(x, cond_1152, L1_cond_qkv_w, L1_cond_qkv_b, L1_cond_proj_w, L1_cond_proj_b, L1_cond_fc1_w, L1_cond_fc1_b, L1_cond_fc2_w, L1_cond_fc2_b, L1_cond_ada_w, L1_cond_ada_b)
    return x

_drawn_inputs = setup_inputs


def setup_inputs(seed=0):
    import zlib

    import numpy as np

    out = dict(_drawn_inputs(seed))
    spreads = {'L0_cond_b_qkv': (0.0, 0.8),
     'L0_cond_b_proj': (0.0, 0.345),
     'L0_cond_b_fc1': (0.0, 0.8),
     'L0_cond_b_fc2': (0.0, 0.363),
     'L0_cond_b_ada': (0.0, 0.391)}
    factors = {'L0_cond_W_qkv': 8.0,
     'L0_cond_W_proj': 5.406,
     'L1_cond_qkv_w': 8.0,
     'L1_cond_qkv_b': 8.0,
     'L1_cond_proj_w': 8.0,
     'L1_cond_proj_b': 33.222,
     'L1_cond_fc1_b': 64.0,
     'L1_cond_fc2_b': 34.661,
     'L1_cond_ada_b': 8.0,
     'L1_cond_fc1_w': 5.627,
     'L1_cond_fc2_w': 5.133}
    for name, (base, spread) in spreads.items():
        noise = np.random.default_rng([zlib.crc32(name.encode()), seed]).standard_normal(out[name].shape)
        drawn = base * np.exp(spread * noise) if base else spread * noise
        out[name] = jnp.asarray(drawn.astype(out[name].dtype))
    for name, factor in factors.items():
        out[name] = (out[name] * factor).astype(out[name].dtype)
    return out
```

```python
from contextlib import ExitStack

import concourse.bass as bass
from concourse import mybir

F32 = mybir.dt.float32
F16 = mybir.dt.float16
BF16 = mybir.dt.bfloat16
ALU = mybir.AluOpType
ACT = mybir.ActivationFunctionType
AX = mybir.AxisListType

P = 128
B, L, C = 2, 1024, 288
H, D = 16, 18
FF = 4 * C
NT = B * L // P
TB = L // P
KB = 2
R = C - KB * P
EPS = 1e-6
HS, WS = 16.0, 64.0
UN = 1.0 / (HS * WS)
HG = 4
NG = B * H // HG
PARTS = 6
MR = 96
MROWS = 3 * HG
SK = PARTS * D + MROWS
KT = L // P
QC = 2
FT = FF // P
VW = 32
NW_QKV, NW_FC1, NW_FC2 = 3 * C, FF, C


def hidden_blocks_kernel(nc, x, cond, qkv_w, qkv_b, proj_w, proj_b, fc1_w, fc1_b, fc2_w, fc2_b,
                         ada_w, ada_b, identity, ones_rows, lo_rows, max_rows, zeros, out):
    gelus = [ACT.Gelu_apprx_tanh, ACT.Gelu]
    with ExitStack() as ctx:
        def sb(name, shape, dt=F32):
            return ctx.enter_context(nc.sbuf_tensor(name, shape, dt))

        def sem(name):
            return ctx.enter_context(nc.semaphore(name))

        x_sb = sb("x_sb", [P, NT, C])
        qk_sb = sb("qk_sb", [P, NT, 2 * C])
        v_sb = sb("v_sb", [P, NT, H, D + 1])
        stacks = sb("stacks", [P, 2, 2, HG, L], BF16)
        stage = sb("stage", [P, 2, TB, HG, SK], BF16)
        resid = sb("resid", [P, TB, HG * D])
        v_group = sb("v_group", [P, 2, KT, HG, VW])
        probs = sb("probs", [P, 2, HG, 512])
        w_qkv = sb("w_qkv", [P, 5, NW_QKV], F16)
        w_proj = sb("w_proj", [P, 5, C], F16)
        w_fc1 = sb("w_fc1", [P, 5, NW_FC1], F16)
        w_fc2 = sb("w_fc2", [P, 2, FT, NW_FC2], F16)
        w_raw = sb("w_raw", [P, FF])
        w_mask = sb("w_mask", [P, FF], F16)
        ada = sb("ada", [P, B, 6, C])
        o_cols = sb("o_cols", [P, QC, 512])
        fc2_bias = sb("fc2_bias", [P, C])
        ident = sb("ident", [P, P])
        ident16 = sb("ident16", [P, P], F16)
        identb = sb("identb", [P, P], BF16)
        ones_raw = sb("ones_raw", [P, R])
        ones_blk = sb("ones_blk", [P, R], F16)
        max_raw = sb("max_raw", [P, HG * MROWS])
        lo_row = sb("lo_row", [P, 1])
        zero_col = sb("zero_col", [P, 1])
        power = sb("power", [P, 1])
        eps_pair = sb("eps_pair", [P, 2])
        bn = sb("bn", [P, 2, 6])
        mv = sb("mv", [P, 2, 2])
        mean_var = sb("mean_var", [P, NT, 2])
        rstd = sb("rstd", [P, NT])
        carrier = sb("carrier", [P, 1])
        row_max = sb("row_max", [P, HG, TB, 2])
        neg_max = sb("neg_max", [P, HG * TB])
        max_rest = sb("max_rest", [P, HG * TB])
        max_parts = sb("max_parts", [P, TB, MROWS], BF16)
        o_recip = sb("o_recip", [P, QC, TB // QC * HG])
        cond_t = sb("cond_t", [96, 3 * B])
        silu_t = sb("silu_t", [96, 3 * B])

        free = probs[:].rearrange("p a h n -> p (a h n)")
        xn = [free[:, C * i:C * (i + 1)] for i in range(2)]
        hn = [free[:, 2 * C + C * i:2 * C + C * (i + 1)] for i in range(2)]
        hs = [free[:, 4 * C + C * i:5 * C + C * i].bitcast(F16).rearrange("p (s n) -> p s n", s=2)
              for i in range(2)]
        hT = [free[:, 6 * C + 320 * i:6 * C + 320 * (i + 1)].bitcast(F16).rearrange("p (k n) -> p k n", k=5)
              for i in range(2)]
        hs4 = hs + [free[:, 6 * C + C * i:7 * C + C * i].bitcast(F16).rearrange("p (s n) -> p s n", s=2)
                    for i in range(2)]
        y_sb = free[:, 2560:2560 + 2 * C].rearrange("p (a n) -> p a n", a=2)
        cond_bc = free[0:96, 3200:3200 + 6 * P].rearrange("p (k n) -> p k n", n=P)
        free2 = stacks[:].rearrange("p a m h n -> p (a m h n)")
        h2T = free2[:, 0:2560].bitcast(F16).rearrange("p (k n) -> p k n", k=5)
        gs = free2[:, 2560:2560 + 2 * FT * 512].bitcast(F16).rearrange("p (f s n) -> p f s n", f=FT, s=2)
        g_sb = [free2[:, 11776 + 1024 * i:11776 + 1024 * (i + 1)].bitcast(F32) for i in range(2)]
        free3 = qk_sb[:].rearrange("p t n -> p (t n)")
        ada_w_sb = free3[0:96, 0:3 * 6 * C].rearrange("p (k n) -> p k n", k=3)
        ada_b_sb = free3[:, 3 * 6 * C:4 * 6 * C]

        ps = ctx.enter_context(nc.psum_tensor("ps", [P, 8, 512], F32))

        def bank(i):
            return ps[:, i, :]

        def bank16(i, dt):
            return ps[:, i, :].bitcast(dt)

        prod = free2[:, 0:2 * H * H * D].bitcast(F32)
        head_s = free2[:, 2 * H * H * D:2 * H * H * D + 2 * H * H].bitcast(F32).rearrange("p (h k) -> p h k", h=H)
        head_e = free2[:, 10240:10240 + 2 * H * H].bitcast(F32).rearrange("p (h k) -> p h k", h=H)
        head_1 = free2[:, 11264:11264 + 2 * H].bitcast(F32)
        head_2 = free2[:, 11392:11392 + 2 * H].bitcast(F32)
        head_out = free2[:, 11520:11520 + 2 * C].bitcast(F32).rearrange("p (h d) -> p h d", h=H)
        turned_out = nc.dram_tensor("turned_out", (B, H, L, D), F32, kind="Internal").ap()

        head_step, head_sub, head_exp, head_o = sem("head_step"), sem("head_sub"), sem("head_exp"), sem("head_o")
        o_stored, o_loaded = sem("o_stored"), sem("o_loaded")
        const_in, const_ready = sem("const_in"), sem("const_ready")
        x_in, ada_in, fc2_bias_in = sem("x_in"), sem("ada_in"), sem("fc2_bias_in")
        w_in, w_ready, w_step = sem("w_in"), sem("w_ready"), sem("w_step")
        silu_ready, cond_ready = sem("silu_ready"), sem("cond_ready")
        ada_mm, ada_sum, ada_ready = sem("ada_mm"), sem("ada_sum"), sem("ada_ready")
        stat_raw, stat_agg, stat_ready, rstd_ready = (sem("stat_raw"), sem("stat_agg"), sem("stat_ready"),
                                                      sem("rstd_ready"))
        xn_done = [sem(f"xn_done{i}") for i in range(3)]
        xs_done = [sem(f"xs_done{i}") for i in range(3)]
        h_ready = [sem(f"h_ready{i}") for i in range(3)]
        hi_ready = [sem(f"hi_ready{i}") for i in range(3)]
        lo_ready = [sem(f"lo_ready{i}") for i in range(3)]
        turned = [sem(f"turned{i}") for i in range(3)]
        hT_ready = [sem(f"hT_ready{i}") for i in range(3)]
        qkv_mm, qk_ready, v_ready = sem("qkv_mm"), sem("qk_ready"), sem("v_ready")
        part_step, vg_ready = sem("part_step"), sem("vg_ready")
        stack_turned, stack_ready = sem("stack_turned"), sem("stack_ready")
        max_mm, max_done, neg_done, split_done = (sem("max_mm"), sem("max_done"), sem("neg_done"),
                                                  sem("split_done"))
        parts_ready, max_turned, max_row = sem("parts_ready"), sem("max_turned"), sem("max_row")
        scores_ready, probs_ready, pv_done = sem("scores_ready"), sem("probs_ready"), sem("pv_done")
        o_copied, o_turned, recip_done, o_ready = (sem("o_copied"), sem("o_turned"), sem("recip_done"),
                                                   sem("o_ready"))
        proj_mm, proj_y, x_mid = sem("proj_mm"), sem("proj_y"), sem("x_mid")
        fc1_mm, g_ready, g_hi, g_split = sem("fc1_mm"), sem("g_ready"), sem("g_hi"), sem("g_split")
        fc2_mm, fc2_y, fc2_g, x_new = sem("fc2_mm"), sem("fc2_y"), sem("fc2_g"), sem("x_new")
        out_done = sem("out_done")

        N_CONST = 8
        CONSTS = 16 * 4
        FULL, MIXED = 1, 6

        def weight_jobs(l):
            jobs = []
            for w, b, dst, n, done in ((qkv_w[l], qkv_b[l], w_qkv, NW_QKV, (qkv_mm, NT * l)),
                                       (proj_w[l], proj_b[l], w_proj, C, (proj_mm, NT * l)),
                                       (fc1_w[l], fc1_b[l], w_fc1, NW_FC1, (fc1_mm, 4 * FT * l))):
                for k in range(KB):
                    jobs.append(([(slice(0, P), w[k * P:(k + 1) * P, :])], n, dst[:, k, :], dst[:, KB + k, :], done))
                src = [(slice(R * i, R * i + R), w[KB * P:C, :]) for i in range(3)]
                src += [(slice(3 * R + i, 3 * R + i + 1), b.rearrange("(a n) -> a n", a=1)) for i in range(2)]
                src += [(slice(3 * R + 2, P), zeros[0:R - 2, 0:n])]
                jobs.append((src, n, dst[:, 4, :], None, done))
            fc2_v = fc2_w[l].rearrange("(f p) n -> p f n", p=P)
            for f0, f1 in ((0, 4), (4, 8), (8, 9)):
                n = (f1 - f0) * C
                jobs.append(([(slice(0, P), fc2_v[:, f0:f1, :])], n,
                             w_fc2[:, 0, f0:f1, :].rearrange("p f n -> p (f n)"),
                             w_fc2[:, 1, f0:f1, :].rearrange("p f n -> p (f n)"), (fc2_mm, NT * l)))
            return jobs

        JOBS = [weight_jobs(l) for l in range(2)]
        NJ = len(JOBS[0])
        QKV_JOBS, PROJ_JOBS, FC1_JOBS = 3, 6, 9

        side = [("T", 0, 0), ("T", 1, 0), ("T", 0, 1), ("T", 1, 1)]
        for j in range(HG):
            for i in range(2 * TB):
                if i == TB and j < 2:
                    side += [("T", 0, j + 2), ("T", 1, j + 2)]
                side.append(("S", j, i // 2, i % 2))
        SLOTS = 2 * KT
        SIDE_SLOTS = SLOTS - 3
        cut = [len(side) * n // SIDE_SLOTS for n in range(SIDE_SLOTS + 1)]

        def slot_side(n):
            if n < SIDE_SLOTS:
                s = side[cut[n]:cut[n + 1]]
                return s[:len(s) // 2], s[len(s) // 2:]
            return ([("M",)], []) if n == SIDE_SLOTS + 1 else ([], [])

        PSTEPS = 5
        NT_STEPS = 2 * HG
        NS_STEPS = 2 * TB * HG
        O_SLOT = 9

        block = ctx.enter_context(nc.Block())

        @block.sync
        def _(sp):
            sp.dma_start(ident[:], identity).then_inc(const_in, 16)
            sp.dma_start(ones_raw[:], ones_rows).then_inc(const_in, 16)
            sp.dma_start(max_raw[:], max_rows).then_inc(const_in, 16)
            sp.dma_start(lo_row[:], lo_rows).then_inc(const_in, 16)
            with nc.allow_non_contiguous_dma(reason="576 numbers"):
                for b in range(B):
                    sp.dma_start(cond_t[:].rearrange("p (k b) -> p k b", b=B)[:, :, b],
                                 cond[b].rearrange("(k p) -> p k", p=96)).then_inc(x_in, 16)
            x_v = x.rearrange("b (t p) n -> p (b t) n", p=P)
            for q in range(4):
                sp.dma_start(x_sb[:, 4 * q:4 * q + 4, :], x_v[:, 4 * q:4 * q + 4, :]).then_inc(x_in, 16)

            def load_ada(l):
                if l:
                    sp.wait_ge(part_step, 2 * PSTEPS * NG * l)
                sp.dma_start(ada_w_sb, ada_w[l].rearrange("(k p) n -> p k n", p=96)).then_inc(ada_in, 16)
                sp.dma_start(ada_b_sb, ada_b[l].rearrange("(a n) -> a n", a=1).to_broadcast([P, 6 * C])
                             ).then_inc(ada_in, 16)

            def load_weights(l, lo, hi):
                for i in range(lo, hi):
                    if NJ * l + i:
                        sp.wait_ge(w_ready, NJ * l + i)
                    for rows, src in JOBS[l][i][0]:
                        n = JOBS[l][i][1]
                        dst = w_raw[rows, 0:n]
                        if len(src.shape) == 3:
                            dst = dst.rearrange("p (f n) -> p f n", n=C)
                        sp.dma_start(dst, src).then_inc(w_in, 16)

            load_weights(0, 0, 1)
            load_ada(0)
            sp.dma_start(fc2_bias[:], fc2_b[0].rearrange("(a n) -> a n", a=1).to_broadcast([P, C])
                         ).then_inc(fc2_bias_in, 16)
            load_weights(0, 1, NJ)
            load_weights(1, 0, QKV_JOBS)
            load_ada(1)
            load_weights(1, QKV_JOBS, QKV_JOBS + 1)
            sp.wait_ge(fc2_y, NT)
            sp.dma_start(fc2_bias[:], fc2_b[1].rearrange("(a n) -> a n", a=1).to_broadcast([P, C])
                         ).then_inc(fc2_bias_in, 16)
            load_weights(1, QKV_JOBS + 1, NJ)
            for b in range(B):
                for t in range(TB):
                    sp.wait_ge(head_o, TB * b + t + 1)
                    sp.dma_start(turned_out[b, :, t * P:(t + 1) * P, :].rearrange("h p d -> p h d"),
                                 v_sb[:, TB * b + t, :, 0:D]).then_inc(o_stored, 16)
                sp.wait_ge(o_stored, 16 * TB * (b + 1))
                rows = turned_out[b].rearrange("h (a r) d -> (h a) (r d)", r=H).rearrange(
                    "(t p) (h d) -> p t h d", p=P, h=H)
                for t in range(TB):
                    sp.dma_start(v_sb[:, TB * b + t, :, 0:D], rows[:, t]).then_inc(o_loaded, 16)
            o_v = out.rearrange("b (t p) n -> p (b t) n", p=P)
            for c in range(4):
                sp.wait_ge(x_new, NT + 4 * c + 4)
                sp.dma_start(o_v[:, 4 * c:4 * c + 4, :], x_sb[:, 4 * c:4 * c + 4, :]).then_inc(out_done, 16)
            sp.wait_ge(out_done, 64)

        @block.gpsimd
        def _(pool):
            steps = [0]
            loaded = [0]

            def chain(ins):
                steps[0] += 1
                ins.then_inc(w_step, 1)
                pool.wait_ge(w_step, steps[0])

            def split_weights(l, first, end):
                for i in range(first, end):
                    src, n, dst_hi, dst_lo, (done, count) = JOBS[l][i]
                    loaded[0] += 16 * len(src)
                    pool.wait_ge(w_in, loaded[0])
                    if l:
                        pool.wait_ge(done, count)
                    chain(nc.gpsimd.tensor_scalar(w_raw[:, 0:n], w_raw[:, 0:n], WS, None, ALU.mult))
                    chain(nc.gpsimd.tensor_copy(dst_hi, w_raw[:, 0:n]))
                    if dst_lo is None:
                        chain(nc.gpsimd.tensor_scalar(w_mask[:, 0:n], dst_hi, lo_row[:, 0:1], None, ALU.mult))
                        last = nc.gpsimd.tensor_tensor(dst_hi, w_raw[:, 0:n], w_mask[:, 0:n], ALU.subtract)
                    else:
                        last = nc.gpsimd.tensor_tensor(dst_lo, w_raw[:, 0:n], dst_hi, ALU.subtract)
                    last.then_inc(w_ready, 1)

            def invert(t, n):
                pool.wait_ge(stat_ready, n + 1)
                nc.gpsimd.tensor_tensor(rstd[:, bass.ds(t, 1)], mean_var[:, t, 1:2],
                                        power[:], ALU.pow).then_inc(rstd_ready, 1)

            def cut_parts(src, m, order, n):
                st = stage[:, m].rearrange("p t h s -> p (t h) s")
                src4 = src.rearrange("p t (h d) -> p t h d", d=D)
                rs = resid[:].rearrange("p t (h d) -> p (t h) d", d=D)
                rs4 = resid[:].rearrange("p t (h d) -> p t h d", d=D)
                z4 = zero_col[:].unsqueeze(1).unsqueeze(1).to_broadcast([P, TB, HG, D])
                z3 = zero_col[:].unsqueeze(1).to_broadcast([P, TB * HG, D])
                first = [order.index(i) for i in (1, 2, 3)]

                def at(part, lo=0, hi=D):
                    off = part * D + lo + (MROWS if part * D + lo >= MR else 0)
                    return st[:, :, off:off + hi - lo]

                pool.wait_ge(part_step, PSTEPS * n)
                nc.gpsimd.tensor_tensor(rs4, src4, z4, ALU.add).then_inc(part_step, 1)
                pool.wait_ge(part_step, PSTEPS * n + 1)
                nc.gpsimd.tensor_tensor(at(first[0]), rs, z3, ALU.add).then_inc(part_step, 1)
                pool.wait_ge(part_step, PSTEPS * n + 2)
                nc.gpsimd.tensor_tensor(rs, rs, at(first[0]), ALU.subtract).then_inc(part_step, 1)
                pool.wait_ge(part_step, PSTEPS * n + 3)
                nc.gpsimd.tensor_tensor(at(first[1]), rs, z3, ALU.add).then_inc(part_step, 1)
                pool.wait_ge(part_step, PSTEPS * n + 4)
                last = nc.gpsimd.tensor_tensor(at(first[2]), rs, at(first[1]), ALU.subtract)
                for part in range(PARTS):
                    if part in first:
                        continue
                    f = first[order[part] - 1]
                    pieces = [(0, D)] if part < PARTS - 1 else [(0, MR - part * D), (MR - part * D, D)]
                    for lo, hi in pieces:
                        zeros_in = zero_col[:].unsqueeze(1).to_broadcast([P, TB * HG, hi - lo])
                        last = nc.gpsimd.tensor_tensor(at(part, lo, hi), at(f, lo, hi), zeros_in, ALU.add)
                last.then_inc(part_step, 1)

            def group_parts(l, p, u, first_round):
                n = NG * l + 2 * p + u
                if first_round:
                    pool.wait_ge(qk_ready, NT * l + TB * (u + 1))
                if first_round and l == 0 and u == 0:
                    pool.wait_ge(const_ready, 1)
                else:
                    pool.wait_ge(stack_turned, NT_STEPS * n)
                for m, order in ((0, (1, 1, 2, 1, 3, 2)), (1, (1, 2, 1, 3, 1, 2))):
                    cols = bass.ds(p * (HG * D) + (1 - m) * C, HG * D)
                    cut_parts(qk_sb[:, TB * u:TB * (u + 1), cols], m, order, 2 * n + m)
                if first_round:
                    pool.wait_ge(v_ready, NT * l + TB * (u + 1))
                else:
                    pool.wait_ge(pv_done, SLOTS * (n - 1))
                nc.gpsimd.tensor_tensor(v_group[:, u, :, :, 0:D + 1],
                                        v_sb[:, TB * u:TB * (u + 1), bass.ds(p * HG, HG), :],
                                        zero_col[:].unsqueeze(1).unsqueeze(1).to_broadcast([P, TB, HG, D + 1]),
                                        ALU.add).then_inc(vg_ready, 1)

            chain(nc.gpsimd.memset(power[:], -0.5))
            chain(nc.gpsimd.memset(zero_col[:], 0.0))
            pool.wait_ge(const_in, CONSTS)
            with pool.Fori(0, NT) as t:
                invert(t, t)
            split_weights(0, 0, QKV_JOBS)
            for l in range(2):
                if l == 0:
                    for u in range(2):
                        group_parts(l, 0, u, True)
                    with pool.Fori(1, HG) as p:
                        for u in range(2):
                            group_parts(l, p, u, False)
                    split_weights(0, QKV_JOBS, NJ)
                else:
                    split_weights(1, QKV_JOBS, NJ)
                stats = 2 * NT * l + NT

                def add_projection(t):
                    pool.wait_ge(proj_y, NT * l + t + 1)
                    nc.gpsimd.tensor_tensor(x_sb[:, t, :], x_sb[:, t, :], y_sb[:, t % 2, :],
                                            ALU.add).then_inc(x_mid, 1)

                add_projection(0)
                with pool.Fori(1, NT) as t:
                    add_projection(t)
                    invert(t - 1, stats + t - 1)
                invert(NT - 1, stats + NT - 1)
                if l == 0:
                    split_weights(1, 0, QKV_JOBS)

                def add_mlp(t):
                    n = NT * l + t
                    pool.wait_ge(fc2_y, n + 1)
                    nc.gpsimd.tensor_tensor(y_sb[:, t % 2, :], y_sb[:, t % 2, :], ada[:, t // TB, 5, :],
                                            ALU.mult).then_inc(fc2_g, 1)
                    pool.wait_ge(fc2_g, n + 1)
                    nc.gpsimd.tensor_tensor(x_sb[:, t, :], x_sb[:, t, :], y_sb[:, t % 2, :],
                                            ALU.add).then_inc(x_new, 1)

                add_mlp(0)
                with pool.Fori(1, NT) as t:
                    add_mlp(t)
                    if l == 0:
                        invert(t - 1, stats + NT + t - 1)
                if l == 0:
                    invert(NT - 1, stats + 2 * NT - 1)

        @block.vector
        def _(dve):
            dve.wait_ge(const_in, CONSTS)
            nc.vector.tensor_copy(ident16[:], ident[:])
            nc.vector.tensor_copy(identb[:], ident[:])
            nc.vector.tensor_copy(ones_blk[:], ones_raw[:])
            nc.vector.memset(eps_pair[:, 0:1], 0.0)
            nc.vector.memset(eps_pair[:, 1:2], EPS)
            nc.vector.memset(v_sb[:, :, :, D:D + 1], 1.0)
            nc.vector.memset(v_group[:].rearrange("p u k h d -> p (u k h) d")[:, :, D + 1:VW], 0.0)
            nc.vector.memset(stage[:, 1, :, :, MR:MR + MROWS], 0.0)
            nc.vector.tensor_copy(stage[:, 0, :, :, MR:MR + MROWS],
                                  max_raw[:].rearrange("p (h s) -> p h s", h=HG).unsqueeze(1).to_broadcast(
                                      [P, TB, HG, MROWS])).then_inc(const_ready, 1)
            dve.wait_ge(const_ready, 1)

            def statistics(t, n):
                nc.vector.bn_stats(bn[:, 0, :], x_sb[:, t, :]).then_inc(stat_raw, 1)
                dve.wait_ge(stat_raw, n + 1)
                nc.vector.memset(carrier[:], 0.0)
                nc.vector.bn_aggr(mv[:, 0, :], bn[:, 0, :]).then_inc(stat_agg, 1)
                dve.wait_ge(stat_agg, n + 1)
                nc.vector.tensor_tensor(mean_var[:, t, :], mv[:, 0, :], eps_pair[:], ALU.add
                                        ).then_inc(stat_ready, 1)

            def normalise(ph, t, u, n, k, b, s):
                dve.wait_ge(rstd_ready, k + 1)
                nc.vector.tensor_scalar(xn[u], x_sb[:, t, :], mean_var[:, t, 0:1], rstd[:, bass.ds(t, 1)],
                                        ALU.subtract, ALU.mult).then_inc(xn_done[ph], 1)
                dve.wait_ge(xn_done[ph], n + 1)
                nc.vector.tensor_tensor(xn[u], xn[u], ada[:, b, s + 1, :], ALU.mult).then_inc(xs_done[ph], 1)
                dve.wait_ge(xs_done[ph], n + 1)
                nc.vector.tensor_tensor(hn[u], xn[u], ada[:, b, s, :], ALU.add).then_inc(h_ready[ph], 1)

            def low_part(ph, i, n):
                dve.wait_ge(hi_ready[ph], n + 1)
                nc.vector.tensor_tensor(hs4[i][:, 1, :], hn[i % 2], hs4[i][:, 0, :], ALU.subtract
                                        ).then_inc(lo_ready[ph], 1)

            def conditioning(l):
                if l:
                    dve.wait_ge(x_new, NT)
                dve.wait_ge(silu_ready, 1)
                nc.vector.tensor_copy(cond_bc, silu_t[:].unsqueeze(2).to_broadcast([96, 3 * B, P])
                                      ).then_inc(cond_ready, 1)
                dve.wait_ge(ada_in, 32 * (l + 1))
                for i in range(4 * B):
                    b, q = divmod(i, 4)
                    cols = slice(q * 6 * C // 4, (q + 1) * 6 * C // 4)
                    dve.wait_ge(ada_mm, 4 * B * l + i + 1)
                    nc.vector.tensor_tensor(ada[:, b].rearrange("p s n -> p (s n)")[:, cols],
                                            bank(6 + i % 2)[:, 0:6 * C // 4], ada_b_sb[:, cols], ALU.add
                                            ).then_inc(ada_sum, 1)
                dve.wait_ge(ada_sum, 4 * B * (l + 1))
                shift, scale = ada[:, :, 0:4:3, :], ada[:, :, 1:5:3, :]
                nc.vector.tensor_scalar(shift, shift, HS, None, ALU.mult)
                nc.vector.tensor_scalar(scale, scale, 1.0, HS, ALU.add, ALU.mult).then_inc(ada_ready, 1)
                dve.wait_ge(ada_ready, l + 1)

            def take_v(l, t, u):
                dve.wait_ge(qkv_mm, NT * l + t + 1)
                nc.vector.tensor_scalar(v_sb[:, t, :, 0:D], bank(4 + 3 * u)[:, 0:C].rearrange(
                    "p (h d) -> p h d", d=D), UN, None, ALU.mult).then_inc(v_ready, 1)

            def qkv_tile(l, t, u, peeled):
                normalise(0, t, u, NT * l + t, 2 * NT * l + t, t // TB, 0)
                if not peeled:
                    take_v(l, t - 2, u)
                low_part(0, u, NT * l + t)

            def reduce_scores(g, k, bk):
                j, i = divmod(k, 2 * TB)
                dve.wait_ge(max_mm, NS_STEPS * g + k + 1)
                nc.vector.reduce_max(row_max[:, j, i // 2, i % 2:i % 2 + 1], bank(bk), AX.X
                                     ).then_inc(max_done, 1)

            def split_maxima(g):
                at = max_parts[:].rearrange("p t (h s) -> p h t s", s=3)
                neg = neg_max[:].rearrange("p (h t) -> p h t", h=HG)
                rest = max_rest[:].rearrange("p (h t) -> p h t", h=HG)
                dve.wait_ge(max_done, NS_STEPS * (g + 1))
                nc.vector.tensor_reduce(neg_max[:], row_max[:].rearrange("p h t s -> p (h t) s"), AX.X,
                                        ALU.max, negate=True).then_inc(neg_done, 1)
                dve.wait_ge(neg_done, g + 1)
                nc.vector.tensor_copy(at[:, :, :, 0], neg).then_inc(split_done, 1)
                dve.wait_ge(split_done, 3 * g + 1)
                nc.vector.tensor_tensor(rest, neg, at[:, :, :, 0], ALU.subtract).then_inc(split_done, 1)
                dve.wait_ge(split_done, 3 * g + 2)
                nc.vector.tensor_copy(at[:, :, :, 1], rest).then_inc(split_done, 1)
                dve.wait_ge(split_done, 3 * g + 3)
                nc.vector.tensor_tensor(at[:, :, :, 2], rest, at[:, :, :, 1], ALU.subtract
                                        ).then_inc(parts_ready, 1)

            def place_maxima(g, par, bk):
                dve.wait_ge(max_turned, g + 1)
                for j in range(HG):
                    nc.vector.tensor_copy(stacks[MR:MR + MROWS, par, 1, j, :],
                                          bank16(bk, BF16)[MR:MR + MROWS, :]).then_inc(max_row, 1)

            def normalise_o(g, p, u, c, bk):
                o = bank(bk).rearrange("p (k d) -> p k d", d=VW)
                dve.wait_ge(o_turned, QC * g + c + 1)
                nc.vector.reciprocal(o_recip[:, c].unsqueeze(2), o[:, :, D:D + 1]).then_inc(recip_done, 1)
                dve.wait_ge(recip_done, QC * g + c + 1)
                t0, n = TB * u + TB // QC * c, TB // QC
                nc.vector.tensor_tensor(
                    v_sb[:, t0:t0 + n, bass.ds(p * HG, HG), 0:D],
                    o[:, :, 0:D].rearrange("p (t h) d -> p t h d", h=HG),
                    o_recip[:, c].rearrange("p (t h) -> p t h", h=HG).unsqueeze(3).to_broadcast([P, n, HG, D]),
                    ALU.mult).then_inc(o_ready, 1)

            def side_slot(g, par, n, bk, done):
                for step in sum(slot_side(n), []):
                    if step[0] == "S":
                        reduce_scores(g, done, bk % 2)
                        done += 1
                        if done == NS_STEPS:
                            split_maxima(g)
                    elif step[0] == "M":
                        place_maxima(g, par, bk % 2)
                    bk += 1
                return bk, done

            def attention_half(l, p, u, bk, with_side):
                g, done = NG * l + 2 * p + u, 0
                for n in range(SLOTS):
                    if n == O_SLOT:
                        normalise_o(g, p, u, 0, bk % 2)
                        bk += 1
                    if with_side:
                        bk, done = side_slot(g + 1, 1 - u, n, bk, done)
                normalise_o(g, p, u, 1, bk % 2)
                return bk + 1

            def attention(l):
                bk, done = 0, 0
                for n in range(SLOTS):
                    bk, done = side_slot(NG * l, 0, n, bk, done)
                with dve.Fori(0, HG - 1) as p:
                    bk = attention_half(l, p, 0, 0, True)
                    attention_half(l, p, 1, bk, True)
                bk = attention_half(l, HG - 1, 0, 0, True)
                attention_half(l, HG - 1, 1, bk, False)

            def take_projection(l, t, u, peeled):
                n = NT * l + t
                dve.wait_ge(proj_mm, n + 1)
                if not peeled:
                    dve.wait_ge(x_mid, n - 1)
                nc.vector.scalar_tensor_tensor(y_sb[:, u, :], bank(2 + u)[:, 0:C], UN, ada[:, t // TB, 2, :],
                                               ALU.mult, ALU.mult).then_inc(proj_y, 1)

            def proj_low(l, t, u):
                dve.wait_ge(hi_ready[1], NT * l + t + 1)
                nc.vector.scalar_tensor_tensor(hs[u][:, 1, :].rearrange("p (h d) -> p h d", d=D),
                                               v_sb[:, t, :, 0:D], HS,
                                               hs[u][:, 0, :].rearrange("p (h d) -> p h d", d=D),
                                               ALU.mult, ALU.subtract).then_inc(lo_ready[1], 1)

            def mid_statistics(l, t):
                dve.wait_ge(x_mid, NT * l + t + 1)
                statistics(t, 2 * NT * l + NT + t)

            def mlp_normalise(l, t, i):
                normalise(2, t, i % 2, NT * l + t, 2 * NT * l + NT + t, t // TB, 3)

            def mlp_chunk(l, c, last):
                for f in range(FT):
                    n = FT * (4 * l + c) + f
                    dve.wait_ge(g_ready, n + 1)
                    nc.vector.tensor_scalar(gs[:, f, 0, :], g_sb[f % 2], HS, None, ALU.mult).then_inc(g_hi, 1)
                    if not last and f < 8:
                        i = f // 2
                        if f % 2 == 0:
                            mlp_normalise(l, 4 * (c + 1) + i, i)
                        else:
                            low_part(2, i, NT * l + 4 * (c + 1) + i)
                    dve.wait_ge(g_hi, n + 1)
                    nc.vector.scalar_tensor_tensor(gs[:, f, 1, :], g_sb[f % 2], HS, gs[:, f, 0, :],
                                                   ALU.mult, ALU.subtract).then_inc(g_split, 1)
                for i in range(4 + 2):
                    if i < 4:
                        n = NT * l + 4 * c + i
                        dve.wait_ge(fc2_mm, n + 1)
                        if i > 1 or l or not isinstance(c, int) or c:
                            dve.wait_ge(x_new, n - 1)
                        nc.vector.scalar_tensor_tensor(y_sb[:, i % 2, :], bank(4 + i % 2)[:, 0:C], UN,
                                                       fc2_bias[:], ALU.mult, ALU.add).then_inc(fc2_y, 1)
                    if i > 1 and l == 0:
                        t = 4 * c + i - 2
                        dve.wait_ge(x_new, NT * l + t + 1)
                        statistics(t, 2 * NT * (l + 1) + t)

            def attend_heads(t):
                q = qk_sb[:, t, 0:C].rearrange("p (h d) -> p h d", d=D)
                k = qk_sb[:, t, C:2 * C].rearrange("p (k d) -> p k d", d=D)

                def then(ins, i):
                    ins.then_inc(head_step, 1)
                    dve.wait_ge(head_step, 7 * t + i)

                dve.wait_ge(qk_ready, NT + t + 1)
                qb = q.unsqueeze(2).to_broadcast([P, H, H, D])
                kb = k.unsqueeze(1).to_broadcast([P, H, H, D])
                then(nc.vector.tensor_tensor(prod.rearrange("p (h k d) -> p h k d", h=H, k=H), qb, kb, ALU.mult), 1)
                then(nc.vector.tensor_reduce(head_s, prod.rearrange("p (h k d) -> p h k d", h=H, k=H),
                                             AX.X, ALU.add), 2)
                then(nc.vector.tensor_reduce(head_1, head_s, AX.X, ALU.max), 3)
                nc.vector.tensor_tensor(head_s, head_s, head_1.unsqueeze(2).to_broadcast([P, H, H]),
                                        ALU.subtract).then_inc(head_sub, 1)
                dve.wait_ge(head_exp, t + 1)
                then(nc.vector.tensor_reduce(head_2, head_e, AX.X, ALU.add), 4)
                then(nc.vector.reciprocal(head_1, head_2), 5)
                eb = head_e.unsqueeze(2).to_broadcast([P, H, D, H])
                for h0 in range(0, H, 4):
                    vb = v_sb[:, t, :, 0:D].rearrange("p k d -> p d k").unsqueeze(1).to_broadcast([P, 4, D, H])
                    last = nc.vector.tensor_tensor(
                        prod[:, h0 * D * H:(h0 + 4) * D * H].rearrange("p (h d k) -> p h d k", h=4, d=D),
                        eb[:, h0:h0 + 4], vb, ALU.mult)
                then(last, 6)
                then(nc.vector.tensor_reduce(head_out,
                                             prod.rearrange("p (h d k) -> p h d k", h=H, d=D),
                                             AX.X, ALU.add), 7)
                nc.vector.tensor_tensor(v_sb[:, t, :, 0:D], head_out, head_1.unsqueeze(2).to_broadcast([P, H, D]),
                                        ALU.mult).then_inc(head_o, 1)

            dve.wait_ge(x_in, 16 * 6)
            with dve.Fori(0, NT) as t:
                statistics(t, t)
            for l in range(2):
                conditioning(l)
                for t in range(2):
                    qkv_tile(l, t, t, True)
                with dve.Fori(1, TB) as i:
                    for u in range(2):
                        qkv_tile(l, 2 * i + u, u, False)
                for u in range(2):
                    take_v(l, NT - 2 + u, u)
                if l == 0:
                    attention(l)
                else:
                    with dve.Fori(0, NT) as t:
                        attend_heads(t)
                    dve.wait_ge(o_loaded, 16 * NT)
                for t in range(4):
                    proj_low(l, t, t % 2)
                    if t >= 2:
                        take_projection(l, t - 2, t % 2, True)
                    if t >= 3:
                        mid_statistics(l, t - 3)
                with dve.Fori(2, TB) as i:
                    for u in range(2):
                        proj_low(l, 2 * i + u, u)
                        take_projection(l, 2 * i + u - 2, u, False)
                        mid_statistics(l, 2 * i + u - 3)
                for t in (NT - 2, NT - 1):
                    take_projection(l, t, t % 2, False)
                    mid_statistics(l, t - 1)
                mid_statistics(l, NT - 1)
                dve.wait_ge(fc2_bias_in, 16 * (l + 1))
                for i in range(4):
                    mlp_normalise(l, i, i)
                    low_part(2, i, NT * l + i)
                mlp_chunk(l, 0, False)
                with dve.Fori(1, 3) as c:
                    mlp_chunk(l, c, False)
                mlp_chunk(l, 3, True)

        @block.scalar
        def _(act):
            act.wait_ge(x_in, 16 * 6)
            nc.scalar.activation(silu_t[:], cond_t[:], ACT.Silu).then_inc(silu_ready, 1)

            def high_part(ph, i, n, gap):
                act.wait_ge(h_ready[ph], n + 1)
                if gap:
                    act.wait_ge(turned[ph], n + 1 - gap)
                nc.scalar.activation(hs4[i][:, 0, :], hn[i % 2], ACT.Copy).then_inc(hi_ready[ph], 1)

            def take_hT(ph, u, n, dst):
                act.wait_ge(turned[ph], n + 1)
                nc.scalar.activation(dst, bank16(u, F16)[:, 0:5 * P].rearrange("p (k n) -> p k n", k=5),
                                     ACT.Copy).then_inc(hT_ready[ph], 1)

            def take_qk(l, t, u):
                act.wait_ge(qkv_mm, NT * l + t + 1)
                nc.scalar.activation(qk_sb[:, t, 0:C], bank(2 + 3 * u)[:, 0:C], ACT.Copy, scale=UN * D ** -0.5)
                nc.scalar.activation(qk_sb[:, t, C:2 * C], bank(3 + 3 * u)[:, 0:C], ACT.Copy, scale=UN
                                     ).then_inc(qk_ready, 1)

            def qkv_tile(l, t, u, peeled):
                high_part(0, u, NT * l + t, 0 if peeled and l == 0 else 2)
                if not peeled:
                    take_qk(l, t - 2, u)
                take_hT(0, u, NT * l + t, hT[u])

            def take_stack(g, par, step, k, bk):
                act.wait_ge(stack_turned, NT_STEPS * g + k + 1)
                nc.scalar.activation(stacks[0:SK, par, step[1], step[2], :], bank16(bk, BF16)[0:SK, :],
                                     ACT.Copy).then_inc(stack_ready, 1)

            def side_slot(g, par, n, bk, k):
                for step in sum(slot_side(n), []):
                    if step[0] == "T":
                        take_stack(g, par, step, k, bk % 2)
                        k += 1
                    bk += 1
                return bk, k

            def exponents(g, n, first):
                s = SLOTS * g + n
                if not first:
                    act.wait_ge(pv_done, s - 1)
                for pair in range(2):
                    act.wait_ge(scores_ready, 2 * s + pair + 1)
                    nc.scalar.activation(
                        probs[:, n % 2, 2 * pair:2 * pair + 2, :].rearrange("p h n -> p (h n)"),
                        ps[:, 2 + 2 * pair:4 + 2 * pair, :].rearrange("p b n -> p (b n)"),
                        ACT.Exp).then_inc(probs_ready, 1)

            def copy_o(g, c, first):
                act.wait_ge(pv_done, SLOTS * g + KT * (c + 1))
                if not first:
                    act.wait_ge(o_turned, QC * (g - 1) + c + 1)
                nc.scalar.activation(o_cols[:, c, :], bank(6 + c), ACT.Copy).then_inc(o_copied, 1)

            def attention_half(l, p, u, bk, with_side, first):
                g, k = NG * l + 2 * p + u, 0
                for n in range(SLOTS):
                    exponents(g, n, first and n < 2)
                    if n == KT:
                        copy_o(g, 0, first)
                    if n == O_SLOT:
                        bk += 1
                    if with_side:
                        bk, k = side_slot(g + 1, 1 - u, n, bk, k)
                copy_o(g, 1, first)
                return bk + 1

            def attention(l):
                bk, k = 0, 0
                for n in range(SLOTS):
                    bk, k = side_slot(NG * l, 0, n, bk, k)
                bk = attention_half(l, 0, 0, 0, True, l == 0)
                attention_half(l, 0, 1, bk, True, False)
                with act.Fori(1, HG - 1) as p:
                    bk = attention_half(l, p, 0, 0, True, False)
                    attention_half(l, p, 1, bk, True, False)
                bk = attention_half(l, HG - 1, 0, 0, True, False)
                attention_half(l, HG - 1, 1, bk, False, False)

            def proj_tile(l, t, u, first):
                n = NT * l + t
                if not first:
                    act.wait_ge(turned[1], n - 1)
                nc.scalar.activation(hs[u][:, 0, :].rearrange("p (h d) -> p h d", d=D), v_sb[:, t, :, 0:D],
                                     ACT.Copy, scale=HS).then_inc(hi_ready[1], 1)
                take_hT(1, u, n, hT[u])

            def mlp_chunk(l, c, last):
                t1 = 4 * (c + 1)
                for f in range(FT):
                    n = FT * (4 * l + c) + f
                    act.wait_ge(fc1_mm, n + 1)
                    if l or not isinstance(c, int) or c or f > 1:
                        act.wait_ge(g_split, n if f == 0 else n - 1)
                    nc.scalar.activation(g_sb[f % 2], bank(2 + f % 2), gelus[l], scale=UN).then_inc(g_ready, 1)
                    if not last and f < 8 and f % 2 == 0:
                        high_part(2, f // 2, NT * l + t1 + f // 2, 4)
                if not last:
                    for i in range(4):
                        take_hT(2, i % 2, NT * l + t1 + i, h2T[:, :, P * i:P * (i + 1)])

            for l in range(2):
                for t in range(2):
                    qkv_tile(l, t, t, True)
                with act.Fori(1, TB) as i:
                    for u in range(2):
                        qkv_tile(l, 2 * i + u, u, False)
                for u in range(2):
                    take_qk(l, NT - 2 + u, u)
                if l == 0:
                    attention(l)
                    act.wait_ge(o_ready, QC * NG)
                else:
                    with act.Fori(0, NT) as t:
                        act.wait_ge(head_sub, t + 1)
                        nc.scalar.activation(head_e.rearrange("p h k -> p (h k)"),
                                             head_s.rearrange("p h k -> p (h k)"), ACT.Exp).then_inc(head_exp, 1)
                    act.wait_ge(o_loaded, 16 * NT)
                for t in range(2):
                    proj_tile(l, t, t, l == 0)
                with act.Fori(1, TB) as i:
                    for u in range(2):
                        proj_tile(l, 2 * i + u, u, False)
                for i in range(4):
                    high_part(2, i, NT * l + i, 4 if l else 0)
                    take_hT(2, i % 2, NT * l + i, h2T[:, :, P * i:P * (i + 1)])
                mlp_chunk(l, 0, False)
                with act.Fori(1, 3) as c:
                    mlp_chunk(l, c, False)
                mlp_chunk(l, 3, True)

        @block.tensor
        def _(pe):
            def turn(ph, u, n, first, parts=None):
                pe.wait_ge(lo_ready[ph], n + 1)
                if not first:
                    pe.wait_ge(hT_ready[ph], n - 1)
                at = bank16(u, F16)
                both = parts or hs[u]
                for s in range(2):
                    for k in range(KB):
                        blk = KB * s + k
                        nc.tensor.transpose(at[:, blk * P:(blk + 1) * P], both[:, s, k * P:(k + 1) * P], ident16[:])
                for i, part in enumerate((both[:, 0, KB * P:C], both[:, 1, KB * P:C], both[:, 0, KB * P:C],
                                          ones_blk[:])):
                    mm = nc.tensor.transpose(at[R * i:R * (i + 1), 4 * P:5 * P], part, ident16[:])
                mm.then_inc(turned[ph], 1)

            PRODUCTS = [(0, 0), (2, 0), (0, 2), (1, 1), (3, 1), (1, 3), (4, 4)]

            def qkv_mms(l, t, u, first):
                n = NT * l + t
                pe.wait_ge(hT_ready[0], n + 1)
                if not first:
                    pe.wait_ge(qk_ready, n - 1)
                    pe.wait_ge(v_ready, n - 1)
                for i, (a, w) in enumerate(PRODUCTS):
                    for o in range(3):
                        mm = nc.tensor.matmul(bank(2 + 3 * u + o)[:, 0:C], hT[u][:, a, :],
                                              w_qkv[:, w, o * C:(o + 1) * C],
                                              start=(i == 0), stop=(i == len(PRODUCTS) - 1))
                mm.then_inc(qkv_mm, 1)

            def side_step(g, par, step, count, bk, freed):
                sem_freed, value = freed
                pe.wait_ge(sem_freed, value)
                if step[0] == "T":
                    _, m, j = step
                    k = count["T"]
                    if k == 0:
                        pe.wait_ge(part_step, 2 * PSTEPS * (g + 1))
                    for t in range(TB):
                        mm = nc.tensor.transpose(bank16(bk, BF16)[0:SK, t * P:(t + 1) * P],
                                                 stage[:, m, t, j, :], identb[:])
                    mm.then_inc(stack_turned, 1)
                    count["T"] += 1
                    return stack_ready, NT_STEPS * g + k + 1
                if step[0] == "S":
                    _, j, t, half = step
                    k = count["S"]
                    if k % (2 * TB) == 0:
                        pe.wait_ge(stack_ready, NT_STEPS * g + 2 * (j + 1))
                    nc.tensor.matmul(bank(bk), stacks[0:SK, par, 1, j, t * P:(t + 1) * P],
                                     stacks[0:SK, par, 0, j, half * 512:(half + 1) * 512],
                                     start=True, stop=True).then_inc(max_mm, 1)
                    count["S"] += 1
                    return max_done, NS_STEPS * g + k + 1
                pe.wait_ge(parts_ready, g + 1)
                for t in range(TB):
                    mm = nc.tensor.transpose(bank16(bk, BF16)[MR:MR + MROWS, t * P:(t + 1) * P],
                                             max_parts[:, t, :], identb[:])
                mm.then_inc(max_turned, 1)
                return max_row, HG * (g + 1)

            def scores(g, u, n, pair, first):
                c, kt = divmod(n, KT)
                s = SLOTS * g + n
                if not first:
                    pe.wait_ge(probs_ready, 2 * (s - 1) + pair + 1)
                if n == 0:
                    pe.wait_ge(max_row, HG * g + 2 * pair + 2)
                for j in (2 * pair, 2 * pair + 1):
                    mm = nc.tensor.matmul(bank(2 + j), stacks[0:SK, u, 0, j, kt * P:(kt + 1) * P],
                                          stacks[0:SK, u, 1, j, c * 512:(c + 1) * 512], start=True, stop=True)
                mm.then_inc(scores_ready, 1)

            def weigh(g, u, n, first):
                c, kt = divmod(n, KT)
                pe.wait_ge(probs_ready, 2 * (SLOTS * g + n) + 2)
                if n == 0:
                    pe.wait_ge(vg_ready, g + 1)
                if kt == 0 and not first:
                    pe.wait_ge(o_copied, QC * (g - 1) + c + 1)
                for j in range(HG):
                    mm = nc.tensor.matmul(bank(6 + c)[VW * j:VW * (j + 1), :], v_group[:, u, kt, j, :],
                                          probs[:, n % 2, j, :], start=(kt == 0), stop=(kt == KT - 1))
                mm.then_inc(pv_done, 1)

            def turn_o(g, c, bk, freed):
                sem_freed, value = freed
                pe.wait_ge(sem_freed, value)
                pe.wait_ge(o_copied, QC * g + c + 1)
                for q in range(TB // QC):
                    mm = nc.tensor.transpose(bank(bk)[:, q * P:(q + 1) * P], o_cols[:, c, q * P:(q + 1) * P],
                                             ident[:])
                mm.then_inc(o_turned, 1)
                return o_ready, QC * g + c + 1

            def attention_half(l, p, u, bk, recent, with_side, last, first):
                g, count = NG * l + 2 * p + u, {"T": 0, "S": 0}

                def side(steps, bk):
                    for step in steps:
                        freed = side_step(g + 1, 1 - u, step, count, bk % 2, recent.pop(0))
                        recent.append(freed)
                        bk += 1
                    return bk

                for n in range(SLOTS):
                    a, b = slot_side(n) if with_side else ([], [])
                    if n == O_SLOT:
                        recent.append(turn_o(g, 0, bk % 2, recent.pop(0)))
                        bk += 1
                    if n < SLOTS - 1:
                        scores(g, u, n + 1, 0, False)
                        bk = side(a, bk)
                        scores(g, u, n + 1, 1, False)
                        bk = side(b, bk)
                        weigh(g, u, n, first)
                    else:
                        if not last:
                            scores(g + 1, 1 - u, 0, 0, False)
                        weigh(g, u, n, first)
                        if not last:
                            scores(g + 1, 1 - u, 0, 1, False)
                recent.append(turn_o(g, 1, bk % 2, recent.pop(0)))
                return bk + 1

            def attention(l):
                g0, bk, count = NG * l, 0, {"T": 0, "S": 0}
                recent = [(hT_ready[0], NT * (l + 1) - 1), (hT_ready[0], NT * (l + 1))]
                for n in range(SLOTS):
                    for step in sum(slot_side(n), []):
                        recent.append(side_step(g0, 0, step, count, bk % 2, recent.pop(0)))
                        bk += 1
                pe.wait_ge(qk_ready, NT * (l + 1))
                pe.wait_ge(v_ready, NT * (l + 1))
                scores(g0, 0, 0, 0, True)
                scores(g0, 0, 0, 1, True)

                def at_start(p):
                    g = g0 + 2 * p
                    return [(max_row, HG * (g + 1)), (o_ready, QC * g)]

                recent = [(max_row, HG * (g0 + 1)), (max_row, HG * (g0 + 1))]
                bk = attention_half(l, 0, 0, 0, recent, True, False, l == 0)
                attention_half(l, 0, 1, bk, recent, True, False, False)
                with pe.Fori(1, HG - 1) as p:
                    recent = at_start(p)
                    bk = attention_half(l, p, 0, 0, recent, True, False, False)
                    attention_half(l, p, 1, bk, recent, True, False, False)
                recent = at_start(HG - 1)
                bk = attention_half(l, HG - 1, 0, 0, recent, True, False, False)
                attention_half(l, HG - 1, 1, bk, recent, False, True, False)

            def proj_mms(l, t, u, first):
                n = NT * l + t
                pe.wait_ge(hT_ready[1], n + 1)
                if not first:
                    pe.wait_ge(proj_y, n - 1)
                for i, (a, w) in enumerate(PRODUCTS):
                    mm = nc.tensor.matmul(bank(2 + u)[:, 0:C], hT[u][:, a, :], w_proj[:, w, :],
                                          start=(i == 0), stop=(i == len(PRODUCTS) - 1))
                mm.then_inc(proj_mm, 1)

            def mlp_chunk(l, c, last):
                pe.wait_ge(hT_ready[2], NT * l + 4 * (c + 1))
                for f in range(FT):
                    n = FT * (4 * l + c) + f
                    if l or not isinstance(c, int) or c or f > 1:
                        pe.wait_ge(g_ready, n if f == 0 else n - 1)
                    for i, (a, w) in enumerate(PRODUCTS):
                        mm = nc.tensor.matmul(bank(2 + f % 2), w_fc1[:, w, f * P:(f + 1) * P], h2T[:, a, :],
                                              start=(i == 0), stop=(i == len(PRODUCTS) - 1))
                    mm.then_inc(fc1_mm, 1)
                if not last:
                    for i in range(4):
                        turn(2, i % 2, NT * l + 4 * (c + 1) + i, False, hs4[i])
                pe.wait_ge(g_split, FT * (4 * l + c + 1))
                for i in range(4):
                    n = NT * l + 4 * c + i
                    if l or not isinstance(c, int) or c or i > 1:
                        pe.wait_ge(fc2_y, n - 1)
                    for f in range(FT):
                        for a, w in ((0, 0), (1, 0), (0, 1)):
                            mm = nc.tensor.matmul(bank(4 + i % 2)[:, 0:C], gs[:, f, a, i * P:(i + 1) * P],
                                                  w_fc2[:, w, f, :], start=(f == 0 and (a, w) == (0, 0)),
                                                  stop=(f == FT - 1 and (a, w) == (0, 1)))
                    mm.then_inc(fc2_mm, 1)

            def conditioning(l):
                pe.wait_ge(cond_ready, l + 1)
                pe.wait_ge(ada_in, 32 * (l + 1))
                for i in range(4 * B):
                    b, q = divmod(i, 4)
                    if i > 1:
                        pe.wait_ge(ada_sum, 4 * B * l + i - 1)
                    for k in range(3):
                        mm = nc.tensor.matmul(bank(6 + i % 2)[:, 0:6 * C // 4], cond_bc[:, k * B + b, :],
                                              ada_w_sb[:, k, q * 6 * C // 4:(q + 1) * 6 * C // 4],
                                              start=(k == 0), stop=(k == 2))
                    mm.then_inc(ada_mm, 1)

            pe.wait_ge(const_ready, 1)
            for l in range(2):
                conditioning(l)
                if l:
                    pe.wait_ge(fc2_y, NT * l)
                turn(0, 0, NT * l, True)
                turn(0, 1, NT * l + 1, True)
                pe.wait_ge(w_ready, NJ * l + QKV_JOBS)
                qkv_mms(l, 0, 0, True)
                turn(0, 0, NT * l + 2, False)
                qkv_mms(l, 1, 1, True)
                turn(0, 1, NT * l + 3, False)
                with pe.Fori(2, TB) as i:
                    for u in range(2):
                        qkv_mms(l, 2 * i + u - 2, u, False)
                        turn(0, u, NT * l + 2 * i + u, False)
                for u in range(2):
                    qkv_mms(l, NT - 2 + u, u, False)
                if l == 0:
                    attention(l)
                pe.wait_ge(w_ready, NJ * l + PROJ_JOBS)
                for t in range(2):
                    turn(1, t, NT * l + t, True)
                for t in range(2):
                    proj_mms(l, t, t, True)
                    turn(1, t, NT * l + t + 2, False)
                with pe.Fori(2, TB) as i:
                    for u in range(2):
                        proj_mms(l, 2 * i + u - 2, u, False)
                        turn(1, u, NT * l + 2 * i + u, False)
                for u in range(2):
                    proj_mms(l, NT - 2 + u, u, False)
                pe.wait_ge(proj_y, NT * (l + 1))
                for i in range(4):
                    turn(2, i % 2, NT * l + i, i < 2, hs4[i])
                pe.wait_ge(w_ready, NJ * (l + 1))
                mlp_chunk(l, 0, False)
                with pe.Fori(1, 3) as c:
                    mlp_chunk(l, c, False)
                mlp_chunk(l, 3, True)


_LAYER = [("L0_cond_W_qkv", "L1_cond_qkv_w"), ("L0_cond_b_qkv", "L1_cond_qkv_b"),
          ("L0_cond_W_proj", "L1_cond_proj_w"), ("L0_cond_b_proj", "L1_cond_proj_b"),
          ("L0_cond_W_fc1", "L1_cond_fc1_w"), ("L0_cond_b_fc1", "L1_cond_fc1_b"),
          ("L0_cond_W_fc2", "L1_cond_fc2_w"), ("L0_cond_b_fc2", "L1_cond_fc2_b"),
          ("L0_cond_W_ada", "L1_cond_ada_w"), ("L0_cond_b_ada", "L1_cond_ada_b")]


def kernel(**inputs):
    import numpy as _np
    import concourse.bacc as _bacc
    from concourse import mybir as _mybir
    from concourse.bass_utils import run_bass_kernel_spmd as _run

    nc = _bacc.Bacc("TRN2", target_bir_lowering=False, num_devices=1)
    arrays = {}

    def given(name, a):
        a = _np.ascontiguousarray(a)
        arrays[name] = a
        return nc.dram_tensor(name, a.shape, _mybir.dt.from_np(a.dtype), kind="ExternalInput").ap()

    ones_rows = _np.zeros((P, R), _np.float32)
    ones_rows[:, 0:2] = HS
    lo_rows = _np.zeros((P, 1), _np.float32)
    lo_rows[2 * R:3 * R] = 1.0
    lo_rows[3 * R + 1] = 1.0
    max_rows = _np.zeros((P, HG, MROWS), _np.float32)
    for j in range(HG):
        max_rows[:, j, 3 * j:3 * j + 3] = 1.0
    args = [given("in_x", inputs["x"]), given("in_cond", inputs["cond_1152"])]
    for pair in _LAYER:
        args.append([given("in_" + name, inputs[name]) for name in pair])
    args += [given("c_identity", _np.eye(P, dtype=_np.float32)), given("c_ones_rows", ones_rows),
             given("c_lo_rows", lo_rows), given("c_max_rows", max_rows.reshape(P, HG * MROWS)),
             given("c_zeros", _np.zeros((R, FF), _np.float32))]
    out = nc.dram_tensor("out_0", (B, L, C), F32, kind="ExternalOutput").ap()
    hidden_blocks_kernel(nc, *args, out)
    r = _run(nc, [arrays], core_ids=[0])
    return r.results[0]["out_0"]
```

```python
from contextlib import ExitStack

import concourse.bass as bass
from concourse import mybir

F32 = mybir.dt.float32
F16 = mybir.dt.float16
BF16 = mybir.dt.bfloat16
ALU = mybir.AluOpType
ACT = mybir.ActivationFunctionType
AX = mybir.AxisListType

P = 128
B, L, C = 2, 1024, 288
H, D = 16, 18
FF = 4 * C
NT = B * L // P
TB = L // P
KB = 2
R = C - KB * P
EPS = 1e-6
HS, WS = 16.0, 64.0
UN = 1.0 / (HS * WS)
HG = 4
NG = B * H // HG
PARTS = 6
MR = 96
MROWS = 3 * HG
SK = PARTS * D + MROWS
KT = L // P
QC = 2
FT = FF // P
VW = 32
NW_QKV, NW_FC1, NW_FC2 = 3 * C, FF, C


def hidden_blocks_kernel(nc, x, cond, qkv_w, qkv_b, proj_w, proj_b, fc1_w, fc1_b, fc2_w, fc2_b,
                         ada_w, ada_b, identity, ones_rows, lo_rows, max_rows, zeros, out):
    gelus = [ACT.Gelu_apprx_tanh, ACT.Gelu]
    with ExitStack() as ctx:
        def sb(name, shape, dt=F32):
            return ctx.enter_context(nc.sbuf_tensor(name, shape, dt))

        def sem(name):
            return ctx.enter_context(nc.semaphore(name))

        x_sb = sb("x_sb", [P, NT, C])
        qk_sb = sb("qk_sb", [P, NT, 2 * C])
        v_sb = sb("v_sb", [P, NT, H, D + 1])
        stacks = sb("stacks", [P, 2, 2, HG, L], BF16)
        stage = sb("stage", [P, 2, TB, HG, SK], BF16)
        resid = sb("resid", [P, TB, HG * D])
        v_group = sb("v_group", [P, 2, KT, HG, VW])
        probs = sb("probs", [P, 2, HG, 512])
        w_qkv = sb("w_qkv", [P, 5, NW_QKV], F16)
        w_proj = sb("w_proj", [P, 5, C], F16)
        w_fc1 = sb("w_fc1", [P, 5, NW_FC1], F16)
        w_fc2 = sb("w_fc2", [P, 2, FT, NW_FC2], F16)
        w_raw = sb("w_raw", [P, FF])
        w_mask = sb("w_mask", [P, FF], F16)
        ada = sb("ada", [P, B, 6, C])
        o_cols = sb("o_cols", [P, QC, 512])
        fc2_bias = sb("fc2_bias", [P, C])
        ident = sb("ident", [P, P])
        ident16 = sb("ident16", [P, P], F16)
        identb = sb("identb", [P, P], BF16)
        ones_raw = sb("ones_raw", [P, R])
        ones_blk = sb("ones_blk", [P, R], F16)
        max_raw = sb("max_raw", [P, HG * MROWS])
        lo_row = sb("lo_row", [P, 1])
        zero_col = sb("zero_col", [P, 1])
        power = sb("power", [P, 1])
        eps_pair = sb("eps_pair", [P, 2])
        bn = sb("bn", [P, 2, 6])
        mv = sb("mv", [P, 2, 2])
        mean_var = sb("mean_var", [P, NT, 2])
        rstd = sb("rstd", [P, NT])
        carrier = sb("carrier", [P, 1])
        row_max = sb("row_max", [P, HG, TB, 2])
        neg_max = sb("neg_max", [P, HG * TB])
        max_rest = sb("max_rest", [P, HG * TB])
        max_parts = sb("max_parts", [P, TB, MROWS], BF16)
        o_recip = sb("o_recip", [P, QC, TB // QC * HG])
        cond_t = sb("cond_t", [96, 3 * B])
        silu_t = sb("silu_t", [96, 3 * B])

        free = probs[:].rearrange("p a h n -> p (a h n)")
        xn = [free[:, C * i:C * (i + 1)] for i in range(2)]
        hn = [free[:, 2 * C + C * i:2 * C + C * (i + 1)] for i in range(2)]
        hs = [free[:, 4 * C + C * i:5 * C + C * i].bitcast(F16).rearrange("p (s n) -> p s n", s=2)
              for i in range(2)]
        hT = [free[:, 6 * C + 320 * i:6 * C + 320 * (i + 1)].bitcast(F16).rearrange("p (k n) -> p k n", k=5)
              for i in range(2)]
        hs4 = hs + [free[:, 6 * C + C * i:7 * C + C * i].bitcast(F16).rearrange("p (s n) -> p s n", s=2)
                    for i in range(2)]
        y_sb = free[:, 2560:2560 + 2 * C].rearrange("p (a n) -> p a n", a=2)
        cond_bc = free[0:96, 3200:3200 + 6 * P].rearrange("p (k n) -> p k n", n=P)
        free2 = stacks[:].rearrange("p a m h n -> p (a m h n)")
        h2T = free2[:, 0:2560].bitcast(F16).rearrange("p (k n) -> p k n", k=5)
        gs = free2[:, 2560:2560 + 2 * FT * 512].bitcast(F16).rearrange("p (f s n) -> p f s n", f=FT, s=2)
        g_sb = [free2[:, 11776 + 1024 * i:11776 + 1024 * (i + 1)].bitcast(F32) for i in range(2)]
        free3 = qk_sb[:].rearrange("p t n -> p (t n)")
        ada_w_sb = free3[0:96, 0:3 * 6 * C].rearrange("p (k n) -> p k n", k=3)
        ada_b_sb = free3[:, 3 * 6 * C:4 * 6 * C]

        ps = ctx.enter_context(nc.psum_tensor("ps", [P, 8, 512], F32))

        def bank(i):
            return ps[:, i, :]

        HALF = 3 * C // 2

        def bank16(i, dt):
            return ps[:, i, :].bitcast(dt)

        free4 = stage[:].rearrange("p m t h s -> p (m t h s)").bitcast(F32)
        free5 = v_group[:].rearrange("p u k h d -> p (u k h d)")
        qk_prod = free2[:, 0:2 * D * H * H].bitcast(F32)
        qk_pair = free2[:, 2 * D * H * H:3 * D * H * H].bitcast(F32)
        ev_low = free4[:, 0:H // 2 * C]
        ev_high = [free4[:, H // 2 * C:H // 2 * C + H // 4 * C],
                   free5[:, 0:H // 4 * C]]
        head_s = free5[:, H // 4 * C:H // 4 * C + H * H].rearrange("p (h k) -> p h k", h=H)
        head_e = [o_cols[:, i, 0:H * H].rearrange("p (h k) -> p h k", h=H) for i in range(2)]
        head_max = o_cols[:, 0, H * H:H * H + H]
        head_sum = [o_cols[:, 0, H * H + H * (i + 1):H * H + H * (i + 2)] for i in range(2)]
        head_rec = [o_cols[:, 1, H * H + H * i:H * H + H * (i + 1)] for i in range(2)]
        turned_out = nc.dram_tensor("turned_out", (B, H, L, D), F32, kind="Internal").ap()

        qk_mult, qk_paired, qk_summed = sem("qk_mult"), sem("qk_paired"), sem("qk_summed")
        head_top, head_sub, head_exp = sem("head_top"), sem("head_sub"), sem("head_exp")
        head_total, head_inv = sem("head_total"), sem("head_inv")
        ev_mult, ev_paired, ev_summed, head_o = sem("ev_mult"), sem("ev_paired"), sem("ev_summed"), sem("head_o")
        o_stored, o_loaded = sem("o_stored"), sem("o_loaded")
        const_in, const_ready = sem("const_in"), sem("const_ready")
        x_in, ada_in, fc2_bias_in = sem("x_in"), sem("ada_in"), sem("fc2_bias_in")
        w_in, w_ready, w_step, w_scaled = sem("w_in"), sem("w_ready"), sem("w_step"), sem("w_scaled")
        silu_ready, cond_ready = sem("silu_ready"), sem("cond_ready")
        ada_mm, ada_sum, ada_ready = sem("ada_mm"), sem("ada_sum"), sem("ada_ready")
        stat_raw, stat_agg, stat_ready, rstd_ready = (sem("stat_raw"), sem("stat_agg"), sem("stat_ready"),
                                                      sem("rstd_ready"))
        xn_done = [sem(f"xn_done{i}") for i in range(3)]
        xs_done = [sem(f"xs_done{i}") for i in range(3)]
        h_ready = [sem(f"h_ready{i}") for i in range(3)]
        hi_ready = [sem(f"hi_ready{i}") for i in range(3)]
        lo_ready = [sem(f"lo_ready{i}") for i in range(3)]
        turned = [sem(f"turned{i}") for i in range(3)]
        hT_ready = [sem(f"hT_ready{i}") for i in range(3)]
        qkv_mm, qk_ready, v_ready = sem("qkv_mm"), sem("qk_ready"), sem("v_ready")
        part_step, vg_ready = sem("part_step"), sem("vg_ready")
        stack_turned, stack_ready = sem("stack_turned"), sem("stack_ready")
        max_mm, max_done, neg_done, split_done = (sem("max_mm"), sem("max_done"), sem("neg_done"),
                                                  sem("split_done"))
        parts_ready, max_turned, max_row = sem("parts_ready"), sem("max_turned"), sem("max_row")
        scores_ready, probs_ready, pv_done = sem("scores_ready"), sem("probs_ready"), sem("pv_done")
        o_copied, o_turned, recip_done, o_ready = (sem("o_copied"), sem("o_turned"), sem("recip_done"),
                                                   sem("o_ready"))
        proj_mm, proj_y, x_mid = sem("proj_mm"), sem("proj_y"), sem("x_mid")
        fc1_mm, g_ready, g_hi, g_split = sem("fc1_mm"), sem("g_ready"), sem("g_hi"), sem("g_split")
        fc2_mm, fc2_y, fc2_g, x_new = sem("fc2_mm"), sem("fc2_y"), sem("fc2_g"), sem("x_new")
        out_done = sem("out_done")

        N_CONST = 8
        CONSTS = 16 * 4
        FULL, MIXED = 1, 6

        def weight_jobs(l):
            jobs = []
            for w, b, dst, n, done in ((qkv_w[l], qkv_b[l], w_qkv, NW_QKV, (qkv_mm, NT * l)),
                                       (proj_w[l], proj_b[l], w_proj, C, (proj_mm, NT * l)),
                                       (fc1_w[l], fc1_b[l], w_fc1, NW_FC1, (fc1_mm, 4 * FT * l))):
                for k in range(KB):
                    jobs.append(([(slice(0, P), w[k * P:(k + 1) * P, :])], n, dst[:, k, :], dst[:, KB + k, :], done))
                src = [(slice(R * i, R * i + R), w[KB * P:C, :]) for i in range(3)]
                src += [(slice(3 * R + i, 3 * R + i + 1), b.rearrange("(a n) -> a n", a=1)) for i in range(2)]
                src += [(slice(3 * R + 2, P), zeros[0:R - 2, 0:n])]
                jobs.append((src, n, dst[:, 4, :], None, done))
            fc2_v = fc2_w[l].rearrange("(f p) n -> p f n", p=P)
            for f0, f1 in ((0, 4), (4, 8), (8, 9)):
                n = (f1 - f0) * C
                jobs.append(([(slice(0, P), fc2_v[:, f0:f1, :])], n,
                             w_fc2[:, 0, f0:f1, :].rearrange("p f n -> p (f n)"),
                             w_fc2[:, 1, f0:f1, :].rearrange("p f n -> p (f n)"), (fc2_mm, NT * l)))
            return jobs

        JOBS = [weight_jobs(l) for l in range(2)]
        NJ = len(JOBS[0])
        QKV_JOBS, PROJ_JOBS, FC1_JOBS = 3, 6, 9

        ACT_JOBS = [(0, i) for i in range(QKV_JOBS)] + [(1, i) for i in range(QKV_JOBS, NJ)]
        LAG = 6
        FIRST, LAST = 8, NT
        PEELED = [n for n in range(NT + LAG + 1) if n < FIRST or n >= LAST]
        JOB_AT = {PEELED[i + 1]: QKV_JOBS + i for i in range(NJ - QKV_JOBS)}

        def loaded(l, i):
            jobs = (JOBS[0] + JOBS[1])[0:NJ * l + i + 1]
            return 16 * sum(len(job[0]) for job in jobs)

        def scaled(l, i):
            return sum(2 + (JOBS[a][b][3] is None) for a, b in ACT_JOBS[0:ACT_JOBS.index((l, i)) + 1])

        side = [("T", 0, 0), ("T", 1, 0), ("T", 0, 1), ("T", 1, 1)]
        for j in range(HG):
            for i in range(2 * TB):
                if i == TB and j < 2:
                    side += [("T", 0, j + 2), ("T", 1, j + 2)]
                side.append(("S", j, i // 2, i % 2))
        SLOTS = 2 * KT
        SIDE_SLOTS = SLOTS - 3
        cut = [len(side) * n // SIDE_SLOTS for n in range(SIDE_SLOTS + 1)]

        def slot_side(n):
            if n < SIDE_SLOTS:
                s = side[cut[n]:cut[n + 1]]
                return s[:len(s) // 2], s[len(s) // 2:]
            return ([("M",)], []) if n == SIDE_SLOTS + 1 else ([], [])

        PSTEPS = 5
        NT_STEPS = 2 * HG
        NS_STEPS = 2 * TB * HG
        O_SLOT = 9

        block = ctx.enter_context(nc.Block())

        @block.sync
        def _(sp):
            sp.dma_start(ident[:], identity).then_inc(const_in, 16)
            sp.dma_start(ones_raw[:], ones_rows).then_inc(const_in, 16)
            sp.dma_start(max_raw[:], max_rows).then_inc(const_in, 16)
            sp.dma_start(lo_row[:], lo_rows).then_inc(const_in, 16)
            with nc.allow_non_contiguous_dma(reason="576 numbers"):
                for b in range(B):
                    sp.dma_start(cond_t[:].rearrange("p (k b) -> p k b", b=B)[:, :, b],
                                 cond[b].rearrange("(k p) -> p k", p=96)).then_inc(x_in, 16)
            x_v = x.rearrange("b (t p) n -> p (b t) n", p=P)
            for q in range(4):
                sp.dma_start(x_sb[:, 4 * q:4 * q + 4, :], x_v[:, 4 * q:4 * q + 4, :]).then_inc(x_in, 16)

            def load_ada(l):
                if l:
                    sp.wait_ge(part_step, 2 * PSTEPS * NG * l)
                sp.dma_start(ada_w_sb, ada_w[l].rearrange("(k p) n -> p k n", p=96)).then_inc(ada_in, 16)
                sp.dma_start(ada_b_sb, ada_b[l].rearrange("(a n) -> a n", a=1).to_broadcast([P, 6 * C])
                             ).then_inc(ada_in, 16)

            def load_weights(l, lo, hi):
                for i in range(lo, hi):
                    if NJ * l + i:
                        sp.wait_ge(w_ready, NJ * l + i)
                    for rows, src in JOBS[l][i][0]:
                        n = JOBS[l][i][1]
                        dst = w_raw[rows, 0:n]
                        if len(src.shape) == 3:
                            dst = dst.rearrange("p (f n) -> p f n", n=C)
                        sp.dma_start(dst, src).then_inc(w_in, 16)

            load_weights(0, 0, 1)
            load_ada(0)
            sp.dma_start(fc2_bias[:], fc2_b[0].rearrange("(a n) -> a n", a=1).to_broadcast([P, C])
                         ).then_inc(fc2_bias_in, 16)
            load_weights(0, 1, NJ)
            load_weights(1, 0, QKV_JOBS)
            load_ada(1)
            load_weights(1, QKV_JOBS, QKV_JOBS + 1)
            sp.wait_ge(fc2_y, NT)
            sp.dma_start(fc2_bias[:], fc2_b[1].rearrange("(a n) -> a n", a=1).to_broadcast([P, C])
                         ).then_inc(fc2_bias_in, 16)
            load_weights(1, QKV_JOBS + 1, NJ)
            for b in range(B):
                for t in range(TB):
                    sp.wait_ge(head_o, TB * b + t + 1)
                    sp.dma_start(turned_out[b, :, t * P:(t + 1) * P, :].rearrange("h p d -> p h d"),
                                 v_sb[:, TB * b + t, :, 0:D]).then_inc(o_stored, 16)
                sp.wait_ge(o_stored, 16 * TB * (b + 1))
                rows = turned_out[b].rearrange("h (a r) d -> (h a) (r d)", r=H).rearrange(
                    "(t p) (h d) -> p t h d", p=P, h=H)
                for t in range(TB):
                    sp.dma_start(v_sb[:, TB * b + t, :, 0:D], rows[:, t]).then_inc(o_loaded, 16)
            o_v = out.rearrange("b (t p) n -> p (b t) n", p=P)
            for c in range(4):
                sp.wait_ge(x_new, NT + 4 * c + 4)
                sp.dma_start(o_v[:, 4 * c:4 * c + 4, :], x_sb[:, 4 * c:4 * c + 4, :]).then_inc(out_done, 16)
            sp.wait_ge(out_done, 64)

        @block.gpsimd
        def _(pool):
            steps = [0]

            def chain(ins):
                steps[0] += 1
                ins.then_inc(w_step, 1)
                pool.wait_ge(w_step, steps[0])

            def split_weights(l, first, end):
                for i in range(first, end):
                    src, n, dst_hi, dst_lo, (done, count) = JOBS[l][i]
                    pool.wait_ge(w_in, loaded(l, i))
                    if l:
                        pool.wait_ge(done, count)
                    chain(nc.gpsimd.tensor_scalar(w_raw[:, 0:n], w_raw[:, 0:n], WS, None, ALU.mult))
                    chain(nc.gpsimd.tensor_copy(dst_hi, w_raw[:, 0:n]))
                    if dst_lo is None:
                        chain(nc.gpsimd.tensor_scalar(w_mask[:, 0:n], dst_hi, lo_row[:, 0:1], None, ALU.mult))
                        last = nc.gpsimd.tensor_tensor(dst_hi, w_raw[:, 0:n], w_mask[:, 0:n], ALU.subtract)
                    else:
                        last = nc.gpsimd.tensor_tensor(dst_lo, w_raw[:, 0:n], dst_hi, ALU.subtract)
                    last.then_inc(w_ready, 1)

            def finish_weights(l, i):
                _, n, dst_hi, dst_lo, _ = JOBS[l][i]
                pool.wait_ge(w_scaled, scaled(l, i))
                if dst_lo is None:
                    last = nc.gpsimd.tensor_tensor(dst_hi, w_raw[:, 0:n], w_mask[:, 0:n], ALU.subtract)
                else:
                    last = nc.gpsimd.tensor_tensor(dst_lo, w_raw[:, 0:n], dst_hi, ALU.subtract)
                last.then_inc(w_ready, 1)

            def head_step(s):
                if not isinstance(s, int) or 0 <= s - 6 < NT:
                    t = s - 6
                    pool.wait_ge(ev_mult, t + 1)
                    for i in range(2):
                        low = ev_low[:, H // 4 * C * i:H // 4 * C * (i + 1)]
                        nc.gpsimd.tensor_tensor(low, low, ev_high[i], ALU.add).then_inc(ev_paired, 1)
                if not isinstance(s, int) or 0 <= s - 3 < NT:
                    t = s - 3
                    if not isinstance(s, int) or t > 0:
                        pool.wait_ge(qk_summed, t)
                    pool.wait_ge(qk_mult, t + 1)
                    half = D // 2 * H * H
                    nc.gpsimd.tensor_tensor(qk_pair, qk_prod[:, 0:half], qk_prod[:, half:2 * half], ALU.add
                                            ).then_inc(qk_paired, 1)

            def invert(t, n):
                pool.wait_ge(stat_ready, n + 1)
                nc.gpsimd.tensor_tensor(rstd[:, bass.ds(t, 1)], mean_var[:, t, 1:2],
                                        power[:], ALU.pow).then_inc(rstd_ready, 1)

            def cut_parts(src, m, order, n):
                st = stage[:, m].rearrange("p t h s -> p (t h) s")
                src4 = src.rearrange("p t (h d) -> p t h d", d=D)
                rs = resid[:].rearrange("p t (h d) -> p (t h) d", d=D)
                rs4 = resid[:].rearrange("p t (h d) -> p t h d", d=D)
                z4 = zero_col[:].unsqueeze(1).unsqueeze(1).to_broadcast([P, TB, HG, D])
                z3 = zero_col[:].unsqueeze(1).to_broadcast([P, TB * HG, D])
                first = [order.index(i) for i in (1, 2, 3)]

                def at(part, lo=0, hi=D):
                    off = part * D + lo + (MROWS if part * D + lo >= MR else 0)
                    return st[:, :, off:off + hi - lo]

                pool.wait_ge(part_step, PSTEPS * n)
                nc.gpsimd.tensor_tensor(rs4, src4, z4, ALU.add).then_inc(part_step, 1)
                pool.wait_ge(part_step, PSTEPS * n + 1)
                nc.gpsimd.tensor_tensor(at(first[0]), rs, z3, ALU.add).then_inc(part_step, 1)
                pool.wait_ge(part_step, PSTEPS * n + 2)
                nc.gpsimd.tensor_tensor(rs, rs, at(first[0]), ALU.subtract).then_inc(part_step, 1)
                pool.wait_ge(part_step, PSTEPS * n + 3)
                nc.gpsimd.tensor_tensor(at(first[1]), rs, z3, ALU.add).then_inc(part_step, 1)
                pool.wait_ge(part_step, PSTEPS * n + 4)
                last = nc.gpsimd.tensor_tensor(at(first[2]), rs, at(first[1]), ALU.subtract)
                for part in range(PARTS):
                    if part in first:
                        continue
                    f = first[order[part] - 1]
                    pieces = [(0, D)] if part < PARTS - 1 else [(0, MR - part * D), (MR - part * D, D)]
                    for lo, hi in pieces:
                        zeros_in = zero_col[:].unsqueeze(1).to_broadcast([P, TB * HG, hi - lo])
                        last = nc.gpsimd.tensor_tensor(at(part, lo, hi), at(f, lo, hi), zeros_in, ALU.add)
                last.then_inc(part_step, 1)

            def group_parts(l, p, u, first_round):
                n = NG * l + 2 * p + u
                if first_round:
                    pool.wait_ge(qk_ready, NT * l + TB * (u + 1))
                if first_round and l == 0 and u == 0:
                    pool.wait_ge(const_ready, 1)
                else:
                    pool.wait_ge(stack_turned, NT_STEPS * n)
                for m, order in ((0, (1, 1, 2, 1, 3, 2)), (1, (1, 2, 1, 3, 1, 2))):
                    cols = bass.ds(p * (HG * D) + (1 - m) * C, HG * D)
                    cut_parts(qk_sb[:, TB * u:TB * (u + 1), cols], m, order, 2 * n + m)
                if first_round:
                    pool.wait_ge(v_ready, NT * l + TB * (u + 1))
                else:
                    pool.wait_ge(pv_done, SLOTS * (n - 1))
                nc.gpsimd.tensor_tensor(v_group[:, u, :, :, 0:D + 1],
                                        v_sb[:, TB * u:TB * (u + 1), bass.ds(p * HG, HG), :],
                                        zero_col[:].unsqueeze(1).unsqueeze(1).to_broadcast([P, TB, HG, D + 1]),
                                        ALU.add).then_inc(vg_ready, 1)

            chain(nc.gpsimd.memset(power[:], -0.5))
            chain(nc.gpsimd.memset(zero_col[:], 0.0))
            pool.wait_ge(const_in, CONSTS)
            with pool.Fori(0, NT) as t:
                invert(t, t)
            for i in range(QKV_JOBS):
                finish_weights(0, i)
            for l in range(2):
                if l == 0:
                    for u in range(2):
                        group_parts(l, 0, u, True)
                    with pool.Fori(1, HG) as p:
                        for u in range(2):
                            group_parts(l, p, u, False)
                    split_weights(0, QKV_JOBS, NJ)
                else:
                    for s in range(NT + LAG + 1):
                        if s == FIRST:
                            with pool.Fori(FIRST, LAST) as n:
                                head_step(n)
                        if s not in PEELED:
                            continue
                        head_step(s)
                        if s in JOB_AT:
                            finish_weights(1, JOB_AT[s])
                stats = 2 * NT * l + NT

                def add_projection(t):
                    pool.wait_ge(proj_y, NT * l + t + 1)
                    nc.gpsimd.tensor_tensor(x_sb[:, t, :], x_sb[:, t, :], y_sb[:, t % 2, :],
                                            ALU.add).then_inc(x_mid, 1)

                add_projection(0)
                with pool.Fori(1, NT) as t:
                    add_projection(t)
                    invert(t - 1, stats + t - 1)
                invert(NT - 1, stats + NT - 1)
                if l == 0:
                    split_weights(1, 0, QKV_JOBS)

                def add_mlp(t):
                    n = NT * l + t
                    pool.wait_ge(fc2_y, n + 1)
                    nc.gpsimd.tensor_tensor(y_sb[:, t % 2, :], y_sb[:, t % 2, :], ada[:, t // TB, 5, :],
                                            ALU.mult).then_inc(fc2_g, 1)
                    pool.wait_ge(fc2_g, n + 1)
                    nc.gpsimd.tensor_tensor(x_sb[:, t, :], x_sb[:, t, :], y_sb[:, t % 2, :],
                                            ALU.add).then_inc(x_new, 1)

                add_mlp(0)
                with pool.Fori(1, NT) as t:
                    add_mlp(t)
                    if l == 0:
                        invert(t - 1, stats + NT + t - 1)
                if l == 0:
                    invert(NT - 1, stats + 2 * NT - 1)

        @block.vector
        def _(dve):
            dve.wait_ge(const_in, CONSTS)
            nc.vector.tensor_copy(ident16[:], ident[:])
            nc.vector.tensor_copy(identb[:], ident[:])
            nc.vector.tensor_copy(ones_blk[:], ones_raw[:])
            nc.vector.memset(eps_pair[:, 0:1], 0.0)
            nc.vector.memset(eps_pair[:, 1:2], EPS)
            nc.vector.memset(v_sb[:, :, :, D:D + 1], 1.0)
            nc.vector.memset(v_group[:].rearrange("p u k h d -> p (u k h) d")[:, :, D + 1:VW], 0.0)
            nc.vector.memset(stage[:, 1, :, :, MR:MR + MROWS], 0.0)
            nc.vector.tensor_copy(stage[:, 0, :, :, MR:MR + MROWS],
                                  max_raw[:].rearrange("p (h s) -> p h s", h=HG).unsqueeze(1).to_broadcast(
                                      [P, TB, HG, MROWS])).then_inc(const_ready, 1)
            dve.wait_ge(const_ready, 1)

            def statistics(t, n):
                nc.vector.bn_stats(bn[:, 0, :], x_sb[:, t, :]).then_inc(stat_raw, 1)
                dve.wait_ge(stat_raw, n + 1)
                nc.vector.memset(carrier[:], 0.0)
                nc.vector.bn_aggr(mv[:, 0, :], bn[:, 0, :]).then_inc(stat_agg, 1)
                dve.wait_ge(stat_agg, n + 1)
                nc.vector.tensor_tensor(mean_var[:, t, :], mv[:, 0, :], eps_pair[:], ALU.add
                                        ).then_inc(stat_ready, 1)

            def normalise(ph, t, u, n, k, b, s):
                dve.wait_ge(rstd_ready, k + 1)
                nc.vector.tensor_scalar(xn[u], x_sb[:, t, :], mean_var[:, t, 0:1], rstd[:, bass.ds(t, 1)],
                                        ALU.subtract, ALU.mult).then_inc(xn_done[ph], 1)
                dve.wait_ge(xn_done[ph], n + 1)
                nc.vector.tensor_tensor(xn[u], xn[u], ada[:, b, s + 1, :], ALU.mult).then_inc(xs_done[ph], 1)
                dve.wait_ge(xs_done[ph], n + 1)
                nc.vector.tensor_tensor(hn[u], xn[u], ada[:, b, s, :], ALU.add).then_inc(h_ready[ph], 1)

            def low_part(ph, i, n):
                dve.wait_ge(hi_ready[ph], n + 1)
                nc.vector.tensor_tensor(hs4[i][:, 1, :], hn[i % 2], hs4[i][:, 0, :], ALU.subtract
                                        ).then_inc(lo_ready[ph], 1)

            def conditioning(l):
                if l:
                    dve.wait_ge(x_new, NT)
                dve.wait_ge(silu_ready, 1)
                nc.vector.tensor_copy(cond_bc, silu_t[:].unsqueeze(2).to_broadcast([96, 3 * B, P])
                                      ).then_inc(cond_ready, 1)
                dve.wait_ge(ada_in, 32 * (l + 1))
                for i in range(4 * B):
                    b, q = divmod(i, 4)
                    cols = slice(q * 6 * C // 4, (q + 1) * 6 * C // 4)
                    dve.wait_ge(ada_mm, 4 * B * l + i + 1)
                    nc.vector.tensor_tensor(ada[:, b].rearrange("p s n -> p (s n)")[:, cols],
                                            bank(6 + i % 2)[:, 0:6 * C // 4], ada_b_sb[:, cols], ALU.add
                                            ).then_inc(ada_sum, 1)
                dve.wait_ge(ada_sum, 4 * B * (l + 1))
                shift, scale = ada[:, :, 0:4:3, :], ada[:, :, 1:5:3, :]
                nc.vector.tensor_scalar(shift, shift, HS, None, ALU.mult)
                nc.vector.tensor_scalar(scale, scale, 1.0, HS, ALU.add, ALU.mult).then_inc(ada_ready, 1)
                dve.wait_ge(ada_ready, l + 1)

            def qkv_tile(l, t, u):
                normalise(0, t, u, NT * l + t, 2 * NT * l + t, t // TB, 0)
                low_part(0, u, NT * l + t)

            def reduce_scores(g, k, bk):
                j, i = divmod(k, 2 * TB)
                dve.wait_ge(max_mm, NS_STEPS * g + k + 1)
                nc.vector.reduce_max(row_max[:, j, i // 2, i % 2:i % 2 + 1], bank(bk), AX.X
                                     ).then_inc(max_done, 1)

            def split_maxima(g):
                at = max_parts[:].rearrange("p t (h s) -> p h t s", s=3)
                neg = neg_max[:].rearrange("p (h t) -> p h t", h=HG)
                rest = max_rest[:].rearrange("p (h t) -> p h t", h=HG)
                dve.wait_ge(max_done, NS_STEPS * (g + 1))
                nc.vector.tensor_reduce(neg_max[:], row_max[:].rearrange("p h t s -> p (h t) s"), AX.X,
                                        ALU.max, negate=True).then_inc(neg_done, 1)
                dve.wait_ge(neg_done, g + 1)
                nc.vector.tensor_copy(at[:, :, :, 0], neg).then_inc(split_done, 1)
                dve.wait_ge(split_done, 3 * g + 1)
                nc.vector.tensor_tensor(rest, neg, at[:, :, :, 0], ALU.subtract).then_inc(split_done, 1)
                dve.wait_ge(split_done, 3 * g + 2)
                nc.vector.tensor_copy(at[:, :, :, 1], rest).then_inc(split_done, 1)
                dve.wait_ge(split_done, 3 * g + 3)
                nc.vector.tensor_tensor(at[:, :, :, 2], rest, at[:, :, :, 1], ALU.subtract
                                        ).then_inc(parts_ready, 1)

            def place_maxima(g, par, bk):
                dve.wait_ge(max_turned, g + 1)
                for j in range(HG):
                    nc.vector.tensor_copy(stacks[MR:MR + MROWS, par, 1, j, :],
                                          bank16(bk, BF16)[MR:MR + MROWS, :]).then_inc(max_row, 1)

            def normalise_o(g, p, u, c, bk):
                o = bank(bk).rearrange("p (k d) -> p k d", d=VW)
                dve.wait_ge(o_turned, QC * g + c + 1)
                nc.vector.reciprocal(o_recip[:, c].unsqueeze(2), o[:, :, D:D + 1]).then_inc(recip_done, 1)
                dve.wait_ge(recip_done, QC * g + c + 1)
                t0, n = TB * u + TB // QC * c, TB // QC
                nc.vector.tensor_tensor(
                    v_sb[:, t0:t0 + n, bass.ds(p * HG, HG), 0:D],
                    o[:, :, 0:D].rearrange("p (t h) d -> p t h d", h=HG),
                    o_recip[:, c].rearrange("p (t h) -> p t h", h=HG).unsqueeze(3).to_broadcast([P, n, HG, D]),
                    ALU.mult).then_inc(o_ready, 1)

            def side_slot(g, par, n, bk, done):
                for step in sum(slot_side(n), []):
                    if step[0] == "S":
                        reduce_scores(g, done, bk % 2)
                        done += 1
                        if done == NS_STEPS:
                            split_maxima(g)
                    elif step[0] == "M":
                        place_maxima(g, par, bk % 2)
                    bk += 1
                return bk, done

            def attention_half(l, p, u, bk, with_side):
                g, done = NG * l + 2 * p + u, 0
                for n in range(SLOTS):
                    if n == O_SLOT:
                        normalise_o(g, p, u, 0, bk % 2)
                        bk += 1
                    if with_side:
                        bk, done = side_slot(g + 1, 1 - u, n, bk, done)
                normalise_o(g, p, u, 1, bk % 2)
                return bk + 1

            def attention(l):
                bk, done = 0, 0
                for n in range(SLOTS):
                    bk, done = side_slot(NG * l, 0, n, bk, done)
                with dve.Fori(0, HG - 1) as p:
                    bk = attention_half(l, p, 0, 0, True)
                    attention_half(l, p, 1, bk, True)
                bk = attention_half(l, HG - 1, 0, 0, True)
                attention_half(l, HG - 1, 1, bk, False)

            def take_projection(l, t, u, peeled):
                n = NT * l + t
                dve.wait_ge(proj_mm, n + 1)
                if not peeled:
                    dve.wait_ge(x_mid, n - 1)
                nc.vector.scalar_tensor_tensor(y_sb[:, u, :], bank(2 + u)[:, 0:C], UN, ada[:, t // TB, 2, :],
                                               ALU.mult, ALU.mult).then_inc(proj_y, 1)

            def proj_low(l, t, u):
                dve.wait_ge(hi_ready[1], NT * l + t + 1)
                nc.vector.scalar_tensor_tensor(hs[u][:, 1, :].rearrange("p (h d) -> p h d", d=D),
                                               v_sb[:, t, :, 0:D], HS,
                                               hs[u][:, 0, :].rearrange("p (h d) -> p h d", d=D),
                                               ALU.mult, ALU.subtract).then_inc(lo_ready[1], 1)

            def mid_statistics(l, t):
                dve.wait_ge(x_mid, NT * l + t + 1)
                statistics(t, 2 * NT * l + NT + t)

            def mlp_normalise(l, t, i):
                normalise(2, t, i % 2, NT * l + t, 2 * NT * l + NT + t, t // TB, 3)

            def mlp_chunk(l, c, last):
                for f in range(FT):
                    n = FT * (4 * l + c) + f
                    dve.wait_ge(g_ready, n + 1)
                    nc.vector.tensor_scalar(gs[:, f, 0, :], g_sb[f % 2], HS, None, ALU.mult).then_inc(g_hi, 1)
                    if not last and f < 8:
                        i = f // 2
                        if f % 2 == 0:
                            mlp_normalise(l, 4 * (c + 1) + i, i)
                        else:
                            low_part(2, i, NT * l + 4 * (c + 1) + i)
                    dve.wait_ge(g_hi, n + 1)
                    nc.vector.scalar_tensor_tensor(gs[:, f, 1, :], g_sb[f % 2], HS, gs[:, f, 0, :],
                                                   ALU.mult, ALU.subtract).then_inc(g_split, 1)
                for i in range(4 + 2):
                    if i < 4:
                        n = NT * l + 4 * c + i
                        dve.wait_ge(fc2_mm, n + 1)
                        if i > 1 or l or not isinstance(c, int) or c:
                            dve.wait_ge(x_new, n - 1)
                        nc.vector.scalar_tensor_tensor(y_sb[:, i % 2, :], bank(4 + i % 2)[:, 0:C], UN,
                                                       fc2_bias[:], ALU.mult, ALU.add).then_inc(fc2_y, 1)
                    if i > 1 and l == 0:
                        t = 4 * c + i - 2
                        dve.wait_ge(x_new, NT * l + t + 1)
                        statistics(t, 2 * NT * (l + 1) + t)

            def multiply_qk(t):
                q = qk_sb[:, t, 0:C].rearrange("p (h d) -> p d h", d=D)
                k = qk_sb[:, t, C:2 * C].rearrange("p (k d) -> p d k", d=D)
                if not isinstance(t, int) or t:
                    dve.wait_ge(qk_paired, t)
                dve.wait_ge(qk_ready, NT + t + 1)
                nc.vector.tensor_tensor(qk_prod.rearrange("p (d h k) -> p d h k", d=D, h=H),
                                        q.unsqueeze(3).to_broadcast([P, D, H, H]),
                                        k.unsqueeze(2).to_broadcast([P, D, H, H]), ALU.mult).then_inc(qk_mult, 1)

            def subtract_maxima(t):
                sums = bank(6)[:, 0:H * H].rearrange("p (h k) -> p h k", h=H)
                dve.wait_ge(qk_summed, t + 1)
                nc.vector.tensor_reduce(head_max, sums, AX.X, ALU.max).then_inc(head_top, 1)
                if not isinstance(t, int) or t:
                    dve.wait_ge(head_exp, t)
                dve.wait_ge(head_top, t + 1)
                nc.vector.tensor_tensor(head_s, sums, head_max.unsqueeze(2).to_broadcast([P, H, H]),
                                        ALU.subtract).then_inc(head_sub, 1)

            def weigh_v(t, u):
                e = head_e[u].rearrange("p h k -> p k h")
                dve.wait_ge(v_ready, NT + t + 1)
                dve.wait_ge(head_exp, t + 1)
                nc.vector.tensor_reduce(head_sum[u], head_e[u], AX.X, ALU.add).then_inc(head_total, 1)

                def part(dst, k0, k1):
                    n = k1 - k0
                    return nc.vector.tensor_tensor(
                        dst.rearrange("p (k h d) -> p k h d", k=n, h=H),
                        e[:, k0:k1].unsqueeze(3).to_broadcast([P, n, H, D]),
                        v_sb[:, t, k0:k1, 0:D].unsqueeze(2).to_broadcast([P, n, H, D]), ALU.mult)

                if not isinstance(t, int) or t:
                    dve.wait_ge(ev_paired, 2 * t)
                part(ev_high[0], H // 2, 3 * H // 4)
                part(ev_high[1], 3 * H // 4, H)
                dve.wait_ge(head_total, t + 1)
                nc.vector.reciprocal(head_rec[u], head_sum[u]).then_inc(head_inv, 1)
                if not isinstance(t, int) or t:
                    dve.wait_ge(ev_summed, t)
                part(ev_low, 0, H // 2).then_inc(ev_mult, 1)

            def normalise_heads(t, u):
                dve.wait_ge(head_inv, t + 1)
                dve.wait_ge(ev_summed, t + 1)
                nc.vector.tensor_tensor(v_sb[:, t, :, 0:D], bank(7)[:, 0:C].rearrange("p (h d) -> p h d", d=D),
                                        head_rec[u].unsqueeze(2).to_broadcast([P, H, D]), ALU.mult
                                        ).then_inc(head_o, 1)

            def head_step(s, u):
                def inside(lag):
                    return not isinstance(s, int) or 0 <= s - lag < NT

                if inside(0):
                    normalise(0, s, u, NT + s, 2 * NT + s, s // TB, 0)
                if inside(3):
                    multiply_qk(s - 3)
                if inside(0):
                    low_part(0, u, NT + s)
                if inside(4):
                    subtract_maxima(s - 4)
                if inside(5):
                    weigh_v(s - 5, 1 - u)
                if inside(6):
                    normalise_heads(s - 6, u)

            dve.wait_ge(x_in, 16 * 6)
            with dve.Fori(0, NT) as t:
                statistics(t, t)
            for l in range(2):
                conditioning(l)
                if l == 0:
                    for t in range(2):
                        qkv_tile(l, t, t)
                    with dve.Fori(1, TB) as i:
                        for u in range(2):
                            qkv_tile(l, 2 * i + u, u)
                    attention(l)
                else:
                    for s in range(FIRST):
                        head_step(s, s % 2)
                    with dve.Fori(FIRST // 2, LAST // 2) as i:
                        for u in range(2):
                            head_step(2 * i + u, u)
                    for s in range(LAST, NT + LAG + 1):
                        head_step(s, s % 2)
                    dve.wait_ge(o_loaded, 16 * NT)
                for t in range(4):
                    proj_low(l, t, t % 2)
                    if t >= 2:
                        take_projection(l, t - 2, t % 2, True)
                    if t >= 3:
                        mid_statistics(l, t - 3)
                with dve.Fori(2, TB) as i:
                    for u in range(2):
                        proj_low(l, 2 * i + u, u)
                        take_projection(l, 2 * i + u - 2, u, False)
                        mid_statistics(l, 2 * i + u - 3)
                for t in (NT - 2, NT - 1):
                    take_projection(l, t, t % 2, False)
                    mid_statistics(l, t - 1)
                mid_statistics(l, NT - 1)
                dve.wait_ge(fc2_bias_in, 16 * (l + 1))
                for i in range(4):
                    mlp_normalise(l, i, i)
                    low_part(2, i, NT * l + i)
                mlp_chunk(l, 0, False)
                with dve.Fori(1, 3) as c:
                    mlp_chunk(l, c, False)
                mlp_chunk(l, 3, True)

        @block.scalar
        def _(act):
            act.wait_ge(x_in, 16 * 6)
            nc.scalar.activation(silu_t[:], cond_t[:], ACT.Silu).then_inc(silu_ready, 1)

            steps = [0]

            def scale_weights(l, i):
                src, n, dst_hi, dst_lo, (done, count) = JOBS[l][i]

                def chain(ins):
                    steps[0] += 1
                    ins.then_inc(w_scaled, 1)
                    act.wait_ge(w_scaled, steps[0])

                act.wait_ge(w_in, loaded(l, i))
                if l:
                    act.wait_ge(done, count)
                chain(nc.scalar.activation(w_raw[:, 0:n], w_raw[:, 0:n], ACT.Copy, scale=WS))
                chain(nc.scalar.activation(dst_hi, w_raw[:, 0:n], ACT.Copy))
                if dst_lo is None:
                    chain(nc.scalar.activation(w_mask[:, 0:n], dst_hi, ACT.Copy, scale=lo_row[:, 0:1]))

            def head_step(s, u):
                def inside(lag):
                    return not isinstance(s, int) or 0 <= s - lag < NT

                if inside(0):
                    high_part(0, u, NT + s, 2)
                if inside(2):
                    take_qkv(1, s - 2, u)
                if inside(0):
                    take_hT(0, u, NT + s, hT[u])
                if inside(4):
                    t = s - 4
                    if not isinstance(s, int) or t > 1:
                        act.wait_ge(ev_mult, t - 1)
                    act.wait_ge(head_sub, t + 1)
                    nc.scalar.activation(head_e[u].rearrange("p h k -> p (h k)"),
                                         head_s.rearrange("p h k -> p (h k)"), ACT.Exp).then_inc(head_exp, 1)

            act.wait_ge(const_in, CONSTS)
            for i in range(QKV_JOBS):
                scale_weights(0, i)

            def high_part(ph, i, n, gap):
                act.wait_ge(h_ready[ph], n + 1)
                if gap:
                    act.wait_ge(turned[ph], n + 1 - gap)
                nc.scalar.activation(hs4[i][:, 0, :], hn[i % 2], ACT.Copy).then_inc(hi_ready[ph], 1)

            def take_hT(ph, u, n, dst):
                act.wait_ge(turned[ph], n + 1)
                nc.scalar.activation(dst, bank16(u, F16)[:, 0:5 * P].rearrange("p (k n) -> p k n", k=5),
                                     ACT.Copy).then_inc(hT_ready[ph], 1)

            def take_qkv(l, t, u):
                act.wait_ge(qkv_mm, NT * l + t + 1)
                nc.scalar.activation(qk_sb[:, t, 0:C], bank(2 + 2 * u)[:, 0:C], ACT.Copy, scale=UN * D ** -0.5)
                k = ps[:, 2 + 2 * u:4 + 2 * u, :].rearrange("p b n -> p (b n)")[:, C:C + 2 * (512 - C)]
                nc.scalar.activation(qk_sb[:, t, C:2 * C].rearrange("p (x n) -> p x n", x=2),
                                     k.rearrange("p (x n) -> p x n", x=2)[:, :, 0:C // 2], ACT.Copy, scale=UN
                                     ).then_inc(qk_ready, 1)
                nc.scalar.activation(v_sb[:, t, :, 0:D], bank(3 + 2 * u)[:, C // 2:HALF].rearrange(
                    "p (h d) -> p h d", d=D), ACT.Copy, scale=UN).then_inc(v_ready, 1)

            def qkv_tile(l, t, u, peeled):
                high_part(0, u, NT * l + t, 0 if peeled and l == 0 else 2)
                if not peeled:
                    take_qkv(l, t - 2, u)
                take_hT(0, u, NT * l + t, hT[u])

            def take_stack(g, par, step, k, bk):
                act.wait_ge(stack_turned, NT_STEPS * g + k + 1)
                nc.scalar.activation(stacks[0:SK, par, step[1], step[2], :], bank16(bk, BF16)[0:SK, :],
                                     ACT.Copy).then_inc(stack_ready, 1)

            def side_slot(g, par, n, bk, k):
                for step in sum(slot_side(n), []):
                    if step[0] == "T":
                        take_stack(g, par, step, k, bk % 2)
                        k += 1
                    bk += 1
                return bk, k

            def exponents(g, n, first):
                s = SLOTS * g + n
                if not first:
                    act.wait_ge(pv_done, s - 1)
                for pair in range(2):
                    act.wait_ge(scores_ready, 2 * s + pair + 1)
                    nc.scalar.activation(
                        probs[:, n % 2, 2 * pair:2 * pair + 2, :].rearrange("p h n -> p (h n)"),
                        ps[:, 2 + 2 * pair:4 + 2 * pair, :].rearrange("p b n -> p (b n)"),
                        ACT.Exp).then_inc(probs_ready, 1)

            def copy_o(g, c, first):
                act.wait_ge(pv_done, SLOTS * g + KT * (c + 1))
                if not first:
                    act.wait_ge(o_turned, QC * (g - 1) + c + 1)
                nc.scalar.activation(o_cols[:, c, :], bank(6 + c), ACT.Copy).then_inc(o_copied, 1)

            def attention_half(l, p, u, bk, with_side, first):
                g, k = NG * l + 2 * p + u, 0
                for n in range(SLOTS):
                    exponents(g, n, first and n < 2)
                    if n == KT:
                        copy_o(g, 0, first)
                    if n == O_SLOT:
                        bk += 1
                    if with_side:
                        bk, k = side_slot(g + 1, 1 - u, n, bk, k)
                copy_o(g, 1, first)
                return bk + 1

            def attention(l):
                bk, k = 0, 0
                for n in range(SLOTS):
                    bk, k = side_slot(NG * l, 0, n, bk, k)
                bk = attention_half(l, 0, 0, 0, True, l == 0)
                attention_half(l, 0, 1, bk, True, False)
                with act.Fori(1, HG - 1) as p:
                    bk = attention_half(l, p, 0, 0, True, False)
                    attention_half(l, p, 1, bk, True, False)
                bk = attention_half(l, HG - 1, 0, 0, True, False)
                attention_half(l, HG - 1, 1, bk, False, False)

            def proj_tile(l, t, u, first):
                n = NT * l + t
                if not first:
                    act.wait_ge(turned[1], n - 1)
                nc.scalar.activation(hs[u][:, 0, :].rearrange("p (h d) -> p h d", d=D), v_sb[:, t, :, 0:D],
                                     ACT.Copy, scale=HS).then_inc(hi_ready[1], 1)
                take_hT(1, u, n, hT[u])

            def mlp_chunk(l, c, last):
                t1 = 4 * (c + 1)
                for f in range(FT):
                    n = FT * (4 * l + c) + f
                    act.wait_ge(fc1_mm, n + 1)
                    if l or not isinstance(c, int) or c or f > 1:
                        act.wait_ge(g_split, n if f == 0 else n - 1)
                    nc.scalar.activation(g_sb[f % 2], bank(2 + f % 2), gelus[l], scale=UN).then_inc(g_ready, 1)
                    if not last and f < 8 and f % 2 == 0:
                        high_part(2, f // 2, NT * l + t1 + f // 2, 4)
                if not last:
                    for i in range(4):
                        take_hT(2, i % 2, NT * l + t1 + i, h2T[:, :, P * i:P * (i + 1)])

            for l in range(2):
                if l == 0:
                    for t in range(2):
                        qkv_tile(l, t, t, True)
                    with act.Fori(1, TB) as i:
                        for u in range(2):
                            qkv_tile(l, 2 * i + u, u, False)
                    for u in range(2):
                        take_qkv(l, NT - 2 + u, u)
                    attention(l)
                    act.wait_ge(o_ready, QC * NG)
                else:
                    for s in range(NT + LAG + 1):
                        if s == FIRST:
                            with act.Fori(FIRST // 2, LAST // 2) as i:
                                for u in range(2):
                                    head_step(2 * i + u, u)
                        if s not in PEELED:
                            continue
                        head_step(s, s % 2)
                        if s in JOB_AT:
                            scale_weights(1, JOB_AT[s])
                    act.wait_ge(o_loaded, 16 * NT)
                for t in range(2):
                    proj_tile(l, t, t, l == 0)
                with act.Fori(1, TB) as i:
                    for u in range(2):
                        proj_tile(l, 2 * i + u, u, False)
                for i in range(4):
                    high_part(2, i, NT * l + i, 4 if l else 0)
                    take_hT(2, i % 2, NT * l + i, h2T[:, :, P * i:P * (i + 1)])
                mlp_chunk(l, 0, False)
                with act.Fori(1, 3) as c:
                    mlp_chunk(l, c, False)
                mlp_chunk(l, 3, True)

        @block.tensor
        def _(pe):
            def turn(ph, u, n, first, parts=None):
                pe.wait_ge(lo_ready[ph], n + 1)
                if not first:
                    pe.wait_ge(hT_ready[ph], n - 1)
                at = bank16(u, F16)
                both = parts or hs[u]
                for s in range(2):
                    for k in range(KB):
                        blk = KB * s + k
                        nc.tensor.transpose(at[:, blk * P:(blk + 1) * P], both[:, s, k * P:(k + 1) * P], ident16[:])
                for i, part in enumerate((both[:, 0, KB * P:C], both[:, 1, KB * P:C], both[:, 0, KB * P:C],
                                          ones_blk[:])):
                    mm = nc.tensor.transpose(at[R * i:R * (i + 1), 4 * P:5 * P], part, ident16[:])
                mm.then_inc(turned[ph], 1)

            PRODUCTS = [(0, 0), (2, 0), (0, 2), (1, 1), (3, 1), (1, 3), (4, 4)]

            def qkv_mms(l, t, u, first):
                n = NT * l + t
                pe.wait_ge(hT_ready[0], n + 1)
                if not first:
                    pe.wait_ge(v_ready, n - 1)
                for i, (a, w) in enumerate(PRODUCTS):
                    for o in range(2):
                        mm = nc.tensor.matmul(bank(2 + 2 * u + o)[:, 0:HALF], hT[u][:, a, :],
                                              w_qkv[:, w, o * HALF:(o + 1) * HALF],
                                              start=(i == 0), stop=(i == len(PRODUCTS) - 1))
                mm.then_inc(qkv_mm, 1)

            def head_step(s, u):
                def inside(lag):
                    return not isinstance(s, int) or 0 <= s - lag < NT

                if inside(2):
                    qkv_mms(1, s - 2, u, isinstance(s, int) and s - 2 < 2)
                if inside(6):
                    t = s - 6
                    if not isinstance(s, int) or t:
                        pe.wait_ge(head_o, t)
                    for k in range(H // 2):
                        if k % (H // 4) == 0:
                            pe.wait_ge(ev_paired, 2 * t + 1 + k // (H // 4))
                        mm = nc.tensor.matmul(bank(7)[:, 0:C], ident[:], ev_low[:, k * C:(k + 1) * C],
                                              start=(k == 0), stop=(k == H // 2 - 1))
                    mm.then_inc(ev_summed, 1)
                if inside(0):
                    turn(0, u, NT + s, isinstance(s, int) and s < 2)
                if inside(3):
                    t = s - 3
                    if not isinstance(s, int) or t:
                        pe.wait_ge(head_sub, t)
                    pe.wait_ge(qk_paired, t + 1)
                    for d in range(D // 2):
                        mm = nc.tensor.matmul(bank(6)[:, 0:H * H], ident[:], qk_pair[:, d * H * H:(d + 1) * H * H],
                                              start=(d == 0), stop=(d == D // 2 - 1))
                    mm.then_inc(qk_summed, 1)

            def side_step(g, par, step, count, bk, freed):
                sem_freed, value = freed
                pe.wait_ge(sem_freed, value)
                if step[0] == "T":
                    _, m, j = step
                    k = count["T"]
                    if k == 0:
                        pe.wait_ge(part_step, 2 * PSTEPS * (g + 1))
                    for t in range(TB):
                        mm = nc.tensor.transpose(bank16(bk, BF16)[0:SK, t * P:(t + 1) * P],
                                                 stage[:, m, t, j, :], identb[:])
                    mm.then_inc(stack_turned, 1)
                    count["T"] += 1
                    return stack_ready, NT_STEPS * g + k + 1
                if step[0] == "S":
                    _, j, t, half = step
                    k = count["S"]
                    if k % (2 * TB) == 0:
                        pe.wait_ge(stack_ready, NT_STEPS * g + 2 * (j + 1))
                    nc.tensor.matmul(bank(bk), stacks[0:SK, par, 1, j, t * P:(t + 1) * P],
                                     stacks[0:SK, par, 0, j, half * 512:(half + 1) * 512],
                                     start=True, stop=True).then_inc(max_mm, 1)
                    count["S"] += 1
                    return max_done, NS_STEPS * g + k + 1
                pe.wait_ge(parts_ready, g + 1)
                for t in range(TB):
                    mm = nc.tensor.transpose(bank16(bk, BF16)[MR:MR + MROWS, t * P:(t + 1) * P],
                                             max_parts[:, t, :], identb[:])
                mm.then_inc(max_turned, 1)
                return max_row, HG * (g + 1)

            def scores(g, u, n, pair, first):
                c, kt = divmod(n, KT)
                s = SLOTS * g + n
                if not first:
                    pe.wait_ge(probs_ready, 2 * (s - 1) + pair + 1)
                if n == 0:
                    pe.wait_ge(max_row, HG * g + 2 * pair + 2)
                for j in (2 * pair, 2 * pair + 1):
                    mm = nc.tensor.matmul(bank(2 + j), stacks[0:SK, u, 0, j, kt * P:(kt + 1) * P],
                                          stacks[0:SK, u, 1, j, c * 512:(c + 1) * 512], start=True, stop=True)
                mm.then_inc(scores_ready, 1)

            def weigh(g, u, n, first):
                c, kt = divmod(n, KT)
                pe.wait_ge(probs_ready, 2 * (SLOTS * g + n) + 2)
                if n == 0:
                    pe.wait_ge(vg_ready, g + 1)
                if kt == 0 and not first:
                    pe.wait_ge(o_copied, QC * (g - 1) + c + 1)
                for j in range(HG):
                    mm = nc.tensor.matmul(bank(6 + c)[VW * j:VW * (j + 1), :], v_group[:, u, kt, j, :],
                                          probs[:, n % 2, j, :], start=(kt == 0), stop=(kt == KT - 1))
                mm.then_inc(pv_done, 1)

            def turn_o(g, c, bk, freed):
                sem_freed, value = freed
                pe.wait_ge(sem_freed, value)
                pe.wait_ge(o_copied, QC * g + c + 1)
                for q in range(TB // QC):
                    mm = nc.tensor.transpose(bank(bk)[:, q * P:(q + 1) * P], o_cols[:, c, q * P:(q + 1) * P],
                                             ident[:])
                mm.then_inc(o_turned, 1)
                return o_ready, QC * g + c + 1

            def attention_half(l, p, u, bk, recent, with_side, last, first):
                g, count = NG * l + 2 * p + u, {"T": 0, "S": 0}

                def side(steps, bk):
                    for step in steps:
                        freed = side_step(g + 1, 1 - u, step, count, bk % 2, recent.pop(0))
                        recent.append(freed)
                        bk += 1
                    return bk

                for n in range(SLOTS):
                    a, b = slot_side(n) if with_side else ([], [])
                    if n == O_SLOT:
                        recent.append(turn_o(g, 0, bk % 2, recent.pop(0)))
                        bk += 1
                    if n < SLOTS - 1:
                        scores(g, u, n + 1, 0, False)
                        bk = side(a, bk)
                        scores(g, u, n + 1, 1, False)
                        bk = side(b, bk)
                        weigh(g, u, n, first)
                    else:
                        if not last:
                            scores(g + 1, 1 - u, 0, 0, False)
                        weigh(g, u, n, first)
                        if not last:
                            scores(g + 1, 1 - u, 0, 1, False)
                recent.append(turn_o(g, 1, bk % 2, recent.pop(0)))
                return bk + 1

            def attention(l):
                g0, bk, count = NG * l, 0, {"T": 0, "S": 0}
                recent = [(hT_ready[0], NT * (l + 1) - 1), (hT_ready[0], NT * (l + 1))]
                for n in range(SLOTS):
                    for step in sum(slot_side(n), []):
                        recent.append(side_step(g0, 0, step, count, bk % 2, recent.pop(0)))
                        bk += 1
                pe.wait_ge(v_ready, NT * (l + 1))
                scores(g0, 0, 0, 0, True)
                scores(g0, 0, 0, 1, True)

                def at_start(p):
                    g = g0 + 2 * p
                    return [(max_row, HG * (g + 1)), (o_ready, QC * g)]

                recent = [(max_row, HG * (g0 + 1)), (max_row, HG * (g0 + 1))]
                bk = attention_half(l, 0, 0, 0, recent, True, False, l == 0)
                attention_half(l, 0, 1, bk, recent, True, False, False)
                with pe.Fori(1, HG - 1) as p:
                    recent = at_start(p)
                    bk = attention_half(l, p, 0, 0, recent, True, False, False)
                    attention_half(l, p, 1, bk, recent, True, False, False)
                recent = at_start(HG - 1)
                bk = attention_half(l, HG - 1, 0, 0, recent, True, False, False)
                attention_half(l, HG - 1, 1, bk, recent, False, True, False)

            def proj_mms(l, t, u, first):
                n = NT * l + t
                pe.wait_ge(hT_ready[1], n + 1)
                if not first:
                    pe.wait_ge(proj_y, n - 1)
                for i, (a, w) in enumerate(PRODUCTS):
                    mm = nc.tensor.matmul(bank(2 + u)[:, 0:C], hT[u][:, a, :], w_proj[:, w, :],
                                          start=(i == 0), stop=(i == len(PRODUCTS) - 1))
                mm.then_inc(proj_mm, 1)

            def mlp_chunk(l, c, last):
                pe.wait_ge(hT_ready[2], NT * l + 4 * (c + 1))
                for f in range(FT):
                    n = FT * (4 * l + c) + f
                    if l or not isinstance(c, int) or c or f > 1:
                        pe.wait_ge(g_ready, n if f == 0 else n - 1)
                    for i, (a, w) in enumerate(PRODUCTS):
                        mm = nc.tensor.matmul(bank(2 + f % 2), w_fc1[:, w, f * P:(f + 1) * P], h2T[:, a, :],
                                              start=(i == 0), stop=(i == len(PRODUCTS) - 1))
                    mm.then_inc(fc1_mm, 1)
                if not last:
                    for i in range(4):
                        turn(2, i % 2, NT * l + 4 * (c + 1) + i, False, hs4[i])
                pe.wait_ge(g_split, FT * (4 * l + c + 1))
                for i in range(4):
                    n = NT * l + 4 * c + i
                    if l or not isinstance(c, int) or c or i > 1:
                        pe.wait_ge(fc2_y, n - 1)
                    for f in range(FT):
                        for a, w in ((0, 0), (1, 0), (0, 1)):
                            mm = nc.tensor.matmul(bank(4 + i % 2)[:, 0:C], gs[:, f, a, i * P:(i + 1) * P],
                                                  w_fc2[:, w, f, :], start=(f == 0 and (a, w) == (0, 0)),
                                                  stop=(f == FT - 1 and (a, w) == (0, 1)))
                    mm.then_inc(fc2_mm, 1)

            def conditioning(l):
                pe.wait_ge(cond_ready, l + 1)
                pe.wait_ge(ada_in, 32 * (l + 1))
                for i in range(4 * B):
                    b, q = divmod(i, 4)
                    if i > 1:
                        pe.wait_ge(ada_sum, 4 * B * l + i - 1)
                    for k in range(3):
                        mm = nc.tensor.matmul(bank(6 + i % 2)[:, 0:6 * C // 4], cond_bc[:, k * B + b, :],
                                              ada_w_sb[:, k, q * 6 * C // 4:(q + 1) * 6 * C // 4],
                                              start=(k == 0), stop=(k == 2))
                    mm.then_inc(ada_mm, 1)

            pe.wait_ge(const_ready, 1)
            for l in range(2):
                conditioning(l)
                if l:
                    pe.wait_ge(fc2_y, NT * l)
                if l == 0:
                    turn(0, 0, 0, True)
                    turn(0, 1, 1, True)
                    pe.wait_ge(w_ready, QKV_JOBS)
                    qkv_mms(l, 0, 0, True)
                    turn(0, 0, 2, False)
                    qkv_mms(l, 1, 1, True)
                    turn(0, 1, 3, False)
                    with pe.Fori(2, TB) as i:
                        for u in range(2):
                            qkv_mms(l, 2 * i + u - 2, u, False)
                            turn(0, u, 2 * i + u, False)
                    for u in range(2):
                        qkv_mms(l, NT - 2 + u, u, False)
                    attention(l)
                else:
                    pe.wait_ge(w_ready, NJ + QKV_JOBS)
                    for s in range(FIRST):
                        head_step(s, s % 2)
                    with pe.Fori(FIRST // 2, LAST // 2) as i:
                        for u in range(2):
                            head_step(2 * i + u, u)
                    for s in range(LAST, NT + LAG + 1):
                        head_step(s, s % 2)
                pe.wait_ge(w_ready, NJ * l + PROJ_JOBS)
                for t in range(2):
                    turn(1, t, NT * l + t, True)
                for t in range(2):
                    proj_mms(l, t, t, True)
                    turn(1, t, NT * l + t + 2, False)
                with pe.Fori(2, TB) as i:
                    for u in range(2):
                        proj_mms(l, 2 * i + u - 2, u, False)
                        turn(1, u, NT * l + 2 * i + u, False)
                for u in range(2):
                    proj_mms(l, NT - 2 + u, u, False)
                pe.wait_ge(proj_y, NT * (l + 1))
                for i in range(4):
                    turn(2, i % 2, NT * l + i, i < 2, hs4[i])
                pe.wait_ge(w_ready, NJ * (l + 1))
                mlp_chunk(l, 0, False)
                with pe.Fori(1, 3) as c:
                    mlp_chunk(l, c, False)
                mlp_chunk(l, 3, True)


_LAYER = [("L0_cond_W_qkv", "L1_cond_qkv_w"), ("L0_cond_b_qkv", "L1_cond_qkv_b"),
          ("L0_cond_W_proj", "L1_cond_proj_w"), ("L0_cond_b_proj", "L1_cond_proj_b"),
          ("L0_cond_W_fc1", "L1_cond_fc1_w"), ("L0_cond_b_fc1", "L1_cond_fc1_b"),
          ("L0_cond_W_fc2", "L1_cond_fc2_w"), ("L0_cond_b_fc2", "L1_cond_fc2_b"),
          ("L0_cond_W_ada", "L1_cond_ada_w"), ("L0_cond_b_ada", "L1_cond_ada_b")]


def kernel(**inputs):
    import numpy as _np
    import concourse.bacc as _bacc
    from concourse import mybir as _mybir
    from concourse.bass_utils import run_bass_kernel_spmd as _run

    nc = _bacc.Bacc("TRN2", target_bir_lowering=False, num_devices=1)
    arrays = {}

    def given(name, a):
        a = _np.ascontiguousarray(a)
        arrays[name] = a
        return nc.dram_tensor(name, a.shape, _mybir.dt.from_np(a.dtype), kind="ExternalInput").ap()

    ones_rows = _np.zeros((P, R), _np.float32)
    ones_rows[:, 0:2] = HS
    lo_rows = _np.zeros((P, 1), _np.float32)
    lo_rows[2 * R:3 * R] = 1.0
    lo_rows[3 * R + 1] = 1.0
    max_rows = _np.zeros((P, HG, MROWS), _np.float32)
    for j in range(HG):
        max_rows[:, j, 3 * j:3 * j + 3] = 1.0
    args = [given("in_x", inputs["x"]), given("in_cond", inputs["cond_1152"])]
    for pair in _LAYER:
        args.append([given("in_" + name, inputs[name]) for name in pair])
    args += [given("c_identity", _np.eye(P, dtype=_np.float32)), given("c_ones_rows", ones_rows),
             given("c_lo_rows", lo_rows), given("c_max_rows", max_rows.reshape(P, HG * MROWS)),
             given("c_zeros", _np.zeros((R, FF), _np.float32))]
    out = nc.dram_tensor("out_0", (B, L, C), F32, kind="ExternalOutput").ap()
    hidden_blocks_kernel(nc, *args, out)
    r = _run(nc, [arrays], core_ids=[0])
    return r.results[0]["out_0"]
```

```python
from contextlib import ExitStack

import concourse.bass as bass
from concourse import mybir

F32 = mybir.dt.float32
F16 = mybir.dt.float16
BF16 = mybir.dt.bfloat16
ALU = mybir.AluOpType
ACT = mybir.ActivationFunctionType
AX = mybir.AxisListType

P = 128
B, L, C = 2, 1024, 288
H, D = 16, 18
FF = 4 * C
NT = B * L // P
TB = L // P
KB = 2
R = C - KB * P
EPS = 1e-6
HS, WS = 16.0, 64.0
UN = 1.0 / (HS * WS)
HG = 4
NG = B * H // HG
PARTS = 6
MR = 96
MROWS = 3 * HG
SK = PARTS * D + MROWS
KT = L // P
QC = 2
FT = FF // P
VW = 32
NW_QKV, NW_FC1, NW_FC2 = 3 * C, FF, C


def hidden_blocks_kernel(nc, x, cond, qkv_w, qkv_b, proj_w, proj_b, fc1_w, fc1_b, fc2_w, fc2_b,
                         ada_w, ada_b, identity, ones_rows, lo_rows, max_rows, zeros, out):
    gelus = [ACT.Gelu_apprx_tanh, ACT.Gelu]
    with ExitStack() as ctx:
        def sb(name, shape, dt=F32):
            return ctx.enter_context(nc.sbuf_tensor(name, shape, dt))

        def sem(name):
            return ctx.enter_context(nc.semaphore(name))

        x_sb = sb("x_sb", [P, NT, C])
        qk_sb = sb("qk_sb", [P, NT, 2 * C])
        v_sb = sb("v_sb", [P, NT, H, D + 1])
        stacks = sb("stacks", [P, 2, 2, HG, L], BF16)
        stage = sb("stage", [P, 2, TB, HG, SK], BF16)
        resid = sb("resid", [P, TB, HG * D])
        v_group = sb("v_group", [P, 2, KT, HG, VW])
        probs = sb("probs", [P, 2, HG, 512])
        w_qkv = sb("w_qkv", [P, 5, NW_QKV], F16)
        w_proj = sb("w_proj", [P, 5, C], F16)
        w_fc1 = sb("w_fc1", [P, 5, NW_FC1], F16)
        w_fc2 = sb("w_fc2", [P, 2, FT, NW_FC2], F16)
        w_raw = sb("w_raw", [P, FF])
        w_mask = sb("w_mask", [P, FF], F16)
        ada = sb("ada", [P, B, 6, C])
        o_cols = sb("o_cols", [P, QC, 512])
        fc2_bias = sb("fc2_bias", [P, C])
        ident = sb("ident", [P, P])
        ident16 = sb("ident16", [P, P], F16)
        identb = sb("identb", [P, P], BF16)
        ones_raw = sb("ones_raw", [P, R])
        ones_blk = sb("ones_blk", [P, R], F16)
        max_raw = sb("max_raw", [P, HG * MROWS])
        lo_row = sb("lo_row", [P, 1])
        zero_col = sb("zero_col", [P, 1])
        power = sb("power", [P, 1])
        eps_pair = sb("eps_pair", [P, 2])
        bn = sb("bn", [P, 2, 6])
        mv = sb("mv", [P, 2, 2])
        mean_var = sb("mean_var", [P, NT, 2])
        rstd = sb("rstd", [P, NT])
        carrier = sb("carrier", [P, 1])
        row_max = sb("row_max", [P, HG, TB, 2])
        neg_max = sb("neg_max", [P, HG * TB])
        max_rest = sb("max_rest", [P, HG * TB])
        max_parts = sb("max_parts", [P, TB, MROWS], BF16)
        o_recip = sb("o_recip", [P, QC, TB // QC * HG])
        cond_t = sb("cond_t", [96, 3 * B])
        silu_t = sb("silu_t", [96, 3 * B])

        free = probs[:].rearrange("p a h n -> p (a h n)")
        xn = [free[:, C * i:C * (i + 1)] for i in range(2)]
        hn = [free[:, 2 * C + C * i:2 * C + C * (i + 1)] for i in range(2)]
        hs = [free[:, 4 * C + C * i:5 * C + C * i].bitcast(F16).rearrange("p (s n) -> p s n", s=2)
              for i in range(2)]
        hT = [free[:, 6 * C + 320 * i:6 * C + 320 * (i + 1)].bitcast(F16).rearrange("p (k n) -> p k n", k=5)
              for i in range(2)]
        y_sb = free[:, 2560:2560 + 2 * C].rearrange("p (a n) -> p a n", a=2)
        free2 = stacks[:].rearrange("p a m h n -> p (a m h n)")
        h2T = free2[:, 0:2560].bitcast(F16).rearrange("p (k n) -> p k n", k=5)
        gs = free2[:, 2560:2560 + 2 * FT * 512].bitcast(F16).rearrange("p (f s n) -> p f s n", f=FT, s=2)
        mlp_hs = [free2[:, 13824 + 2 * C * i:13824 + 2 * C * (i + 1)].bitcast(F16).rearrange("p (s n) -> p s n", s=2)
                  for i in range(4)]
        g_sb = [free2[:, 11776 + 1024 * i:11776 + 1024 * (i + 1)].bitcast(F32) for i in range(2)]
        ada_next = v_sb[:].rearrange("p t h d -> p (t h d)")[:, 0:B * 6 * C].rearrange(
            "p (b s n) -> p b s n", b=B, s=6)
        free3 = qk_sb[:].rearrange("p t n -> p (t n)")
        ada_w_sb = free3[0:96, 0:3 * 6 * C].rearrange("p (k n) -> p k n", k=3)
        ada_b_sb = free3[:, 3 * 6 * C:4 * 6 * C]
        cond_bc = free3[0:96, 4 * 6 * C:4 * 6 * C + 6 * P].rearrange("p (k n) -> p k n", n=P)
        bn_first = free3[:, 4 * 6 * C + 6 * P:4 * 6 * C + 6 * P + 6 * NT].rearrange("p (t n) -> p t n", n=6)

        def parts_of(ph, i):
            return mlp_hs[i] if ph == 2 else hs[i]

        ps = ctx.enter_context(nc.psum_tensor("ps", [P, 8, 512], F32))

        def bank(i):
            return ps[:, i, :]

        HALF = 3 * C // 2

        def bank16(i, dt):
            return ps[:, i, :].bitcast(dt)

        def ada_bank(l, i):
            return 6 + i % 2 if l else i

        FIRST_BANKS = (4, 5, 6, 7)
        MLP_BANKS = (0, 1, 6, 7)

        def side_bank(i):
            return (0, 1, 7)[i % 3]

        free4 = stage[:].rearrange("p m t h s -> p (m t h s)").bitcast(F32)
        free5 = v_group[:].rearrange("p u k h d -> p (u k h d)")
        HH, PAIRS, POOLED = H * H, 7, 1
        SINGLES = D - 2 * PAIRS
        words = free2.bitcast(F32)
        qk_prod = words[:, 0:2 * PAIRS * HH]
        qk_pair = words[:, 2 * PAIRS * HH:3 * PAIRS * HH]
        qk_single = [words[:, (3 * PAIRS + SINGLES * i) * HH:(3 * PAIRS + SINGLES * (i + 1)) * HH] for i in range(2)]
        ev_low = free4[:, 0:H // 2 * C]
        ev_high = [free4[:, H // 2 * C:H // 2 * C + H // 4 * C],
                   free5[:, 0:H // 4 * C]]
        head_s = free5[:, H // 4 * C:H // 4 * C + H * H].rearrange("p (h k) -> p h k", h=H)
        head_e = [o_cols[:, i, 0:H * H].rearrange("p (h k) -> p h k", h=H) for i in range(2)]
        head_max = o_cols[:, 0, H * H:H * H + H]
        head_sum = [o_cols[:, 0, H * H + H * (i + 1):H * H + H * (i + 2)] for i in range(2)]
        head_rec = [o_cols[:, 1, H * H + H * i:H * H + H * (i + 1)] for i in range(2)]
        turned_out = nc.dram_tensor("turned_out", (B, H, L, D), F32, kind="Internal").ap()

        qk_mult, qk_paired, qk_summed = sem("qk_mult"), sem("qk_paired"), sem("qk_summed")
        head_top, head_sub, head_exp = sem("head_top"), sem("head_sub"), sem("head_exp")
        head_total, head_inv = sem("head_total"), sem("head_inv")
        ev_mult, ev_paired, ev_summed, head_o = sem("ev_mult"), sem("ev_paired"), sem("ev_summed"), sem("head_o")
        o_stored, o_loaded, o_loaded_1 = sem("o_stored"), sem("o_loaded"), sem("o_loaded_1")
        const_in, const_ready = sem("const_in"), sem("const_ready")
        x_in, cond_in, ada_in, fc2_bias_in = sem("x_in"), sem("cond_in"), sem("ada_in"), sem("fc2_bias_in")
        w_in, w_ready, w_step, w_scaled = sem("w_in"), sem("w_ready"), sem("w_step"), sem("w_scaled")
        w_high, w_masked = sem("w_high"), sem("w_masked")
        w_first = [sem(f"w_first{i}") for i in range(3)]
        silu_ready, cond_ready = sem("silu_ready"), sem("cond_ready")
        ada_mm, ada_sum, ada_ready = sem("ada_mm"), sem("ada_sum"), sem("ada_ready")
        gate_moved = sem("gate_moved")
        stat_raw, stat_agg, stat_ready, rstd_ready = (sem("stat_raw"), sem("stat_agg"), sem("stat_ready"),
                                                      sem("rstd_ready"))
        xn_done = [sem(f"xn_done{i}") for i in range(3)]
        h_ready = [sem(f"h_ready{i}") for i in range(3)]
        hi_ready = [sem(f"hi_ready{i}") for i in range(3)]
        lo_ready = [sem(f"lo_ready{i}") for i in range(3)]
        turned = [sem(f"turned{i}") for i in range(3)]
        hT_ready = [sem(f"hT_ready{i}") for i in range(3)]
        qkv_mm, qk_ready, v_ready = sem("qkv_mm"), sem("qk_ready"), sem("v_ready")
        part_step, vg_ready = sem("part_step"), sem("vg_ready")
        stack_turned, stack_by_act, stack_by_dve = sem("stack_turned"), sem("stack_by_act"), sem("stack_by_dve")
        max_mm, max_done, neg_done, split_done = (sem("max_mm"), sem("max_done"), sem("neg_done"),
                                                  sem("split_done"))
        parts_ready, max_turned, max_row = sem("parts_ready"), sem("max_turned"), sem("max_row")
        scores_ready, probs_ready, pv_done = sem("scores_ready"), sem("probs_ready"), sem("pv_done")
        o_copied, o_turned, recip_done, o_ready = (sem("o_copied"), sem("o_turned"), sem("recip_done"),
                                                   sem("o_ready"))
        proj_mm, proj_y, x_mid = sem("proj_mm"), sem("proj_y"), sem("x_mid")
        fc1_mm, g_ready, g_hi, g_split = sem("fc1_mm"), sem("g_ready"), sem("g_hi"), sem("g_split")
        fc2_mm, fc2_y, fc2_g, x_new = sem("fc2_mm"), sem("fc2_y"), sem("fc2_g"), sem("x_new")
        out_done = sem("out_done")

        CONSTS = 16 * 4
        FULL, MIXED = 1, 6

        def weight_jobs(l):
            jobs = []
            for w, b, dst, n, done in ((qkv_w[l], qkv_b[l], w_qkv, NW_QKV, (qkv_mm, NT * l)),
                                       (proj_w[l], proj_b[l], w_proj, C, (proj_mm, NT * l)),
                                       (fc1_w[l], fc1_b[l], w_fc1, NW_FC1, (fc1_mm, 4 * FT * l))):
                for k in range(KB):
                    jobs.append(([(slice(0, P), w[k * P:(k + 1) * P, :])], n, dst[:, k, :], dst[:, KB + k, :], done))
                src = [(slice(R * i, R * i + R), w[KB * P:C, :]) for i in range(3)]
                src += [(slice(3 * R + i, 3 * R + i + 1), b.rearrange("(a n) -> a n", a=1)) for i in range(2)]
                src += [(slice(3 * R + 2, P), zeros[0:R - 2, 0:n])]
                jobs.append((src, n, dst[:, 4, :], None, done))
            fc2_v = fc2_w[l].rearrange("(f p) n -> p f n", p=P)
            for f0, f1 in ((0, 4), (4, 8), (8, 9)):
                n = (f1 - f0) * C
                jobs.append(([(slice(0, P), fc2_v[:, f0:f1, :])], n,
                             w_fc2[:, 0, f0:f1, :].rearrange("p f n -> p (f n)"),
                             w_fc2[:, 1, f0:f1, :].rearrange("p f n -> p (f n)"), (fc2_mm, NT * l)))
            return jobs

        JOBS = [weight_jobs(l) for l in range(2)]
        NJ = len(JOBS[0])
        QKV_JOBS, PROJ_JOBS, FC1_JOBS = 3, 6, 9

        ACT_JOBS = [(0, i) for i in range(QKV_JOBS)]
        LAST_JOB_SLOTS = (2, 6, 10)
        JOBS_AT_FC2 = (0, 2)
        JOBS_AT_ADA = (1, 3, 5, 7)
        LAG = 6
        FIRST, LAST = 8, NT
        PEELED = [n for n in range(NT + LAG + 1) if n < FIRST or n >= LAST]
        JOB_AT = {NT + 1 + i: PROJ_JOBS + i for i in range(NJ - PROJ_JOBS)}

        def early_proj(s):
            first = NT + 2
            return (2 * (s - first), 2 * (s - first) + 1) if first <= s < first + TB // 2 else ()

        def raw(l, i):
            if (l, i) in ACT_JOBS[1:QKV_JOBS]:
                return stacks[:].rearrange("p a m h n -> p (a m h n)").bitcast(F32)[:, NW_QKV * (i - 1):NW_QKV * i]
            return w_raw[:, 0:JOBS[l][i][1]]

        def loaded(l, i):
            if (l, i) in ACT_JOBS[0:QKV_JOBS]:
                return w_first[i], 16 * len(JOBS[l][i][0])
            jobs = (JOBS[0] + JOBS[1])[QKV_JOBS:NJ * l + i + 1]
            return w_in, 16 * sum(len(job[0]) for job in jobs)

        def scaled(l, i):
            return sum(2 + (JOBS[a][b][3] is None) for a, b in ACT_JOBS[0:ACT_JOBS.index((l, i)) + 1])

        SLOTS = 2 * KT
        FIRST_SIDE, END_SIDE, M_SLOT = 1, SLOTS - 2, SLOTS - 2
        side = []
        for j in range(HG):
            for i in range(2 * TB):
                if i in (4, 8) and j + 1 < HG:
                    side.append(("T", i // 4 - 1, j + 1))
                side.append(("S", j, i // 2, i % 2))
        cut = [len(side) * n // (END_SIDE - FIRST_SIDE) for n in range(END_SIDE - FIRST_SIDE + 1)]

        def slot_side(n):
            if n == 0:
                return [("T", 0, 0), ("T", 1, 0)], [], []
            if n == M_SLOT:
                return [], [], [("M",)]
            if n > M_SLOT:
                return [], [], []
            steps = side[cut[n - FIRST_SIDE]:cut[n - FIRST_SIDE + 1]]
            between, after = len(steps) // 3, (len(steps) + 2) // 3
            before = len(steps) - between - after
            return steps[:before], steps[before:before + between], steps[before + between:]

        def steps_of(n):
            return sum(slot_side(n), [])

        BY_DVE = [(0, 0), (1, 0), (0, 1), (1, 1)]
        TURNS = [step[1:] for n in range(SLOTS) for step in steps_of(n) if step[0] == "T"]
        PSTEPS = 5
        NT_STEPS = 2 * HG
        NS_STEPS = 2 * TB * HG
        O_SLOTS = (SLOTS // QC + 1, 1)

        def multiply_slices(engine, t, dst, d0, d1, at=0):
            n = d1 - d0
            q = qk_sb[:, t, 0:C].rearrange("p (h d) -> p d h", d=D)[:, d0:d1]
            k = qk_sb[:, t, C:2 * C].rearrange("p (k d) -> p d k", d=D)[:, d0:d1]
            return engine.tensor_tensor(dst[:, at * HH:(at + n) * HH].rearrange("p (d h k) -> p d h k", d=n, h=H),
                                        q.unsqueeze(3).to_broadcast([P, n, H, H]),
                                        k.unsqueeze(2).to_broadcast([P, n, H, H]), ALU.mult)

        def attended(l, t):
            if l and (not isinstance(t, int) or t >= TB):
                return qk_sb[:, t - TB, 0:C].rearrange("p (h d) -> p h d", d=D)
            return v_sb[:, t, :, 0:D]

        block = ctx.enter_context(nc.Block())

        @block.sync
        def _(sp):
            def load_ada(l):
                if l:
                    sp.wait_ge(part_step, 2 * PSTEPS * NG * l)
                sp.dma_start(ada_w_sb, ada_w[l].rearrange("(k p) n -> p k n", p=96)).then_inc(ada_in, 16)
                sp.dma_start(ada_b_sb, ada_b[l].rearrange("(a n) -> a n", a=1).to_broadcast([P, 6 * C])
                             ).then_inc(ada_in, 16)

            with nc.allow_non_contiguous_dma(reason="576 numbers"):
                for b in range(B):
                    sp.dma_start(cond_t[:].rearrange("p (k b) -> p k b", b=B)[:, :, b],
                                 cond[b].rearrange("(k p) -> p k", p=96)).then_inc(cond_in, 16)
            sp.dma_start(ident[:], identity).then_inc(const_in, 16)
            sp.dma_start(ones_raw[:], ones_rows).then_inc(const_in, 16)
            sp.dma_start(max_raw[:], max_rows).then_inc(const_in, 16)
            sp.dma_start(lo_row[:], lo_rows).then_inc(const_in, 16)
            load_ada(0)
            x_v = x.rearrange("b (t p) n -> p (b t) n", p=P)
            for q in range(4):
                sp.dma_start(x_sb[:, 4 * q:4 * q + 4, :], x_v[:, 4 * q:4 * q + 4, :]).then_inc(x_in, 16)

            def load_weights(l, lo, hi):
                for i in range(lo, hi):
                    if NJ * l + i >= QKV_JOBS:
                        sp.wait_ge(w_ready, NJ * l + i)
                    for rows, src in JOBS[l][i][0]:
                        dst = raw(l, i)[rows, :]
                        if len(src.shape) == 3:
                            dst = dst.rearrange("p (f n) -> p f n", n=C)
                        sp.dma_start(dst, src).then_inc(loaded(l, i)[0], 16)

            load_weights(0, 0, 1)
            sp.dma_start(fc2_bias[:], fc2_b[0].rearrange("(a n) -> a n", a=1).to_broadcast([P, C])
                         ).then_inc(fc2_bias_in, 16)
            load_weights(0, 1, NJ)
            load_ada(1)
            load_weights(1, 0, QKV_JOBS)
            load_weights(1, QKV_JOBS, PROJ_JOBS)
            sp.wait_ge(fc2_y, NT)
            sp.dma_start(fc2_bias[:], fc2_b[1].rearrange("(a n) -> a n", a=1).to_broadcast([P, C])
                         ).then_inc(fc2_bias_in, 16)
            load_weights(1, PROJ_JOBS, PROJ_JOBS + 1)
            for b in range(B):
                for t in range(TB):
                    sp.wait_ge(head_o, TB * b + t + 1)
                    sp.dma_start(turned_out[b, :, t * P:(t + 1) * P, :].rearrange("h p d -> p h d"),
                                 v_sb[:, TB * b + t, :, 0:D]).then_inc(o_stored, 16)
                    if b:
                        sp.wait_ge(o_stored, 16 * (TB * b + t + 1))
                        rows = turned_out[b].rearrange("(T e) (a r) d -> e a T (r d)", e=2, r=H)
                        for e in range(2):
                            p0, n = P // 2 * e + P // H * t, P // H
                            sp.dma_start(qk_sb[p0:p0 + n, 0:TB, 0:C], rows[e, n * t:n * (t + 1)]
                                         ).then_inc(o_loaded_1, 16)
                    if b and t > 2:
                        load_weights(1, PROJ_JOBS + t - 2, PROJ_JOBS + t - 1)
                if b == 0:
                    sp.wait_ge(o_stored, 16 * TB)
                    rows = turned_out[b].rearrange("h (a r) d -> (h a) (r d)", r=H).rearrange(
                        "(t p) (h d) -> p t h d", p=P, h=H)
                    for t in range(TB):
                        sp.dma_start(v_sb[:, t, :, 0:D], rows[:, t]).then_inc(o_loaded, 16)
            o_v = out.rearrange("b (t p) n -> p (b t) n", p=P)
            for c in range(4):
                sp.wait_ge(x_new, NT + 4 * c + 4)
                sp.dma_start(o_v[:, 4 * c:4 * c + 4, :], x_sb[:, 4 * c:4 * c + 4, :]).then_inc(out_done, 16)
            sp.wait_ge(out_done, 64)

        @block.gpsimd
        def _(pool):
            steps = [0]

            def chain(ins):
                steps[0] += 1
                ins.then_inc(w_step, 1)
                pool.wait_ge(w_step, steps[0])

            def split_weights(l, first, end):
                for i in range(first, end):
                    _, n, dst_hi, dst_lo, _ = JOBS[l][i]
                    pool.wait_ge(*loaded(l, i))
                    chain(nc.gpsimd.tensor_scalar(w_raw[:, 0:n], w_raw[:, 0:n], WS, None, ALU.mult))
                    chain(nc.gpsimd.tensor_copy(dst_hi, w_raw[:, 0:n]))
                    if dst_lo is None:
                        chain(nc.gpsimd.tensor_scalar(w_mask[:, 0:n], dst_hi, lo_row[:, 0:1], None, ALU.mult))
                        last = nc.gpsimd.tensor_tensor(dst_hi, w_raw[:, 0:n], w_mask[:, 0:n], ALU.subtract)
                    else:
                        last = nc.gpsimd.tensor_tensor(dst_lo, w_raw[:, 0:n], dst_hi, ALU.subtract)
                    last.then_inc(w_ready, 1)

            def finish_weights(l, i):
                _, n, dst_hi, dst_lo, _ = JOBS[l][i]
                pool.wait_ge(w_scaled, scaled(l, i))
                if dst_lo is None:
                    last = nc.gpsimd.tensor_tensor(dst_hi, raw(l, i), w_mask[:, 0:n], ALU.subtract)
                else:
                    last = nc.gpsimd.tensor_tensor(dst_lo, raw(l, i), dst_hi, ALU.subtract)
                last.then_inc(w_ready, 1)

            def head_step(s, u):
                if not isinstance(s, int) or 0 <= s - 6 < NT:
                    t = s - 6
                    pool.wait_ge(ev_mult, t + 1)
                    for i in range(2):
                        low = ev_low[:, H // 4 * C * i:H // 4 * C * (i + 1)]
                        nc.gpsimd.tensor_tensor(low, low, ev_high[i], ALU.add).then_inc(ev_paired, 1)
                t = s - 3
                if not isinstance(s, int) or 0 <= t < NT:
                    pool.wait_ge(qk_ready, NT + t + 1)
                    if not isinstance(s, int) or t > 1:
                        pool.wait_ge(qk_summed, t - 1)
                if not isinstance(s, int) or 2 <= s < NT:
                    pool.wait_ge(hi_ready[0], NT + s + 1)
                    nc.gpsimd.tensor_tensor(hs[u][:, 1, :], hn[u], hs[u][:, 0, :], ALU.subtract
                                            ).then_inc(lo_ready[0], 1)
                if not isinstance(s, int) or 0 <= t < NT:
                    multiply_slices(nc.gpsimd, t, qk_single[1 - u], D - POOLED, D, SINGLES - POOLED)
                    if not isinstance(s, int) or t > 0:
                        pool.wait_ge(qk_summed, t)
                    pool.wait_ge(qk_mult, t + 1)
                    half = PAIRS * HH
                    nc.gpsimd.tensor_tensor(qk_pair, qk_prod[:, 0:half], qk_prod[:, half:2 * half], ALU.add
                                            ).then_inc(qk_paired, 1)

            def invert(t, n):
                pool.wait_ge(stat_ready, n + 1)
                nc.gpsimd.tensor_tensor(rstd[:, bass.ds(t, 1)], mean_var[:, t, 1:2],
                                        power[:], ALU.pow).then_inc(rstd_ready, 1)

            def cut_parts(src, m, order, n):
                st = stage[:, m].rearrange("p t h s -> p (t h) s")
                src4 = src.rearrange("p t (h d) -> p t h d", d=D)
                rs = resid[:].rearrange("p t (h d) -> p (t h) d", d=D)
                rs4 = resid[:].rearrange("p t (h d) -> p t h d", d=D)
                z4 = zero_col[:].unsqueeze(1).unsqueeze(1).to_broadcast([P, TB, HG, D])
                z3 = zero_col[:].unsqueeze(1).to_broadcast([P, TB * HG, D])
                first = [order.index(i) for i in (1, 2, 3)]

                def at(part, lo=0, hi=D):
                    off = part * D + lo + (MROWS if part * D + lo >= MR else 0)
                    return st[:, :, off:off + hi - lo]

                pool.wait_ge(part_step, PSTEPS * n)
                nc.gpsimd.tensor_tensor(rs4, src4, z4, ALU.add).then_inc(part_step, 1)
                pool.wait_ge(part_step, PSTEPS * n + 1)
                nc.gpsimd.tensor_tensor(at(first[0]), rs, z3, ALU.add).then_inc(part_step, 1)
                pool.wait_ge(part_step, PSTEPS * n + 2)
                nc.gpsimd.tensor_tensor(rs, rs, at(first[0]), ALU.subtract).then_inc(part_step, 1)
                pool.wait_ge(part_step, PSTEPS * n + 3)
                nc.gpsimd.tensor_tensor(at(first[1]), rs, z3, ALU.add).then_inc(part_step, 1)
                pool.wait_ge(part_step, PSTEPS * n + 4)
                last = nc.gpsimd.tensor_tensor(at(first[2]), rs, at(first[1]), ALU.subtract)
                for part in range(PARTS):
                    if part in first:
                        continue
                    f = first[order[part] - 1]
                    pieces = [(0, D)] if part < PARTS - 1 else [(0, MR - part * D), (MR - part * D, D)]
                    for lo, hi in pieces:
                        zeros_in = zero_col[:].unsqueeze(1).to_broadcast([P, TB * HG, hi - lo])
                        last = nc.gpsimd.tensor_tensor(at(part, lo, hi), at(f, lo, hi), zeros_in, ALU.add)
                last.then_inc(part_step, 1)

            def add_projection(l, t):
                pool.wait_ge(proj_y, NT * l + t + 1)
                nc.gpsimd.tensor_tensor(x_sb[:, t, :], x_sb[:, t, :], y_sb[:, t % 2, :], ALU.add
                                        ).then_inc(x_mid, 1)
                if l and isinstance(t, int) and t > 1:
                    invert(t - 2, 3 * NT + t - 2)

            def group_parts(l, p, u, first_round):
                n = NG * l + 2 * p + u
                if first_round:
                    pool.wait_ge(qk_ready, NT * l + TB * (u + 1))
                if first_round and l == 0 and u == 0:
                    pool.wait_ge(const_ready, 1)
                else:
                    pool.wait_ge(stack_turned, NT_STEPS * n)
                for m, order in ((0, (1, 1, 2, 1, 3, 2)), (1, (1, 2, 1, 3, 1, 2))):
                    cols = bass.ds(p * (HG * D) + (1 - m) * C, HG * D)
                    cut_parts(qk_sb[:, TB * u:TB * (u + 1), cols], m, order, 2 * n + m)
                if first_round:
                    pool.wait_ge(v_ready, NT * l + TB * (u + 1))
                else:
                    pool.wait_ge(pv_done, SLOTS * (n - 1))
                nc.gpsimd.tensor_tensor(v_group[:, u, :, :, 0:D + 1],
                                        v_sb[:, TB * u:TB * (u + 1), bass.ds(p * HG, HG), :],
                                        zero_col[:].unsqueeze(1).unsqueeze(1).to_broadcast([P, TB, HG, D + 1]),
                                        ALU.add).then_inc(vg_ready, 1)

            chain(nc.gpsimd.memset(power[:], -0.5))
            chain(nc.gpsimd.memset(zero_col[:], 0.0))
            pool.wait_ge(const_in, CONSTS)
            pool.wait_ge(stat_ready, NT)
            nc.gpsimd.tensor_tensor(rstd[:].unsqueeze(2), mean_var[:, :, 1:2],
                                    power[:].unsqueeze(1).to_broadcast([P, NT, 1]), ALU.pow).then_inc(rstd_ready, NT)
            for i in range(QKV_JOBS):
                finish_weights(0, i)
            for l in range(2):
                if l == 0:
                    for u in range(2):
                        group_parts(l, 0, u, True)
                    with pool.Fori(1, HG) as p:
                        for u in range(2):
                            group_parts(l, p, u, False)
                    split_weights(0, QKV_JOBS, FC1_JOBS)
                else:
                    for s in range(NT + LAG + 1):
                        if s == FIRST:
                            with pool.Fori(FIRST // 2, LAST // 2) as i:
                                for u in range(2):
                                    head_step(2 * i + u, u)
                        if s not in PEELED:
                            continue
                        head_step(s, s % 2)
                        for n in early_proj(s - 1):
                            if n > 2:
                                add_projection(1, n - 3)
                stats = 2 * NT * l + NT
                first = 2
                if l == 0:
                    add_projection(0, 0)
                    add_projection(0, 1)
                else:
                    first = TB - 3
                with pool.Fori(first, NT) as t:
                    add_projection(l, t)
                    invert(t - 2, stats + t - 2)
                for t in (NT - 2, NT - 1):
                    invert(t, stats + t)

                def add_mlp(t):
                    n = NT * l + t
                    pool.wait_ge(fc2_y, n + 1)
                    nc.gpsimd.tensor_tensor(y_sb[:, t % 2, :], y_sb[:, t % 2, :], ada[:, t // TB, 5, :],
                                            ALU.mult).then_inc(fc2_g, 1)
                    pool.wait_ge(fc2_g, n + 1)
                    nc.gpsimd.tensor_tensor(x_sb[:, t, :], x_sb[:, t, :], y_sb[:, t % 2, :],
                                            ALU.add).then_inc(x_new, 1)

                add_mlp(0)
                with pool.Fori(1, NT) as t:
                    add_mlp(t)
                    if l == 0:
                        invert(t - 1, stats + NT + t - 1)
                if l == 0:
                    invert(NT - 1, stats + 2 * NT - 1)

        @block.vector
        def _(dve):
            dve.wait_ge(const_in, CONSTS)
            nc.vector.tensor_copy(ident16[:], ident[:])
            nc.vector.tensor_copy(identb[:], ident[:])
            nc.vector.tensor_copy(ones_blk[:], ones_raw[:])
            nc.vector.memset(eps_pair[:, 0:1], 0.0)
            nc.vector.memset(eps_pair[:, 1:2], EPS)
            nc.vector.memset(v_sb[:, :, :, D:D + 1], 1.0)
            nc.vector.memset(v_group[:].rearrange("p u k h d -> p (u k h) d")[:, :, D + 1:VW], 0.0)
            nc.vector.memset(stage[:, 1, :, :, MR:MR + MROWS], 0.0)
            nc.vector.tensor_copy(stage[:, 0, :, :, MR:MR + MROWS],
                                  max_raw[:].rearrange("p (h s) -> p h s", h=HG).unsqueeze(1).to_broadcast(
                                      [P, TB, HG, MROWS])).then_inc(const_ready, 1)
            dve.wait_ge(const_ready, 1)

            def statistics(t, n):
                nc.vector.bn_stats(bn[:, 0, :], x_sb[:, t, :]).then_inc(stat_raw, 1)
                dve.wait_ge(stat_raw, n + 1)
                nc.vector.memset(carrier[:], 0.0)
                nc.vector.bn_aggr(mv[:, 0, :], bn[:, 0, :]).then_inc(stat_agg, 1)
                dve.wait_ge(stat_agg, n + 1)
                nc.vector.tensor_tensor(mean_var[:, t, :], mv[:, 0, :], eps_pair[:], ALU.add
                                        ).then_inc(stat_ready, 1)

            def normalise(ph, t, u, n, k, b, s):
                nc.vector.scalar_tensor_tensor(xn[u], x_sb[:, t, :], mean_var[:, t, 0:1], ada[:, b, s + 1, :],
                                               ALU.subtract, ALU.mult).then_inc(xn_done[ph], 1)
                dve.wait_ge(rstd_ready, k + 1)
                dve.wait_ge(xn_done[ph], n + 1)
                nc.vector.scalar_tensor_tensor(hn[u], xn[u], rstd[:, bass.ds(t, 1)], ada[:, b, s, :],
                                               ALU.mult, ALU.add).then_inc(h_ready[ph], 1)

            def low_part(ph, i, n):
                dve.wait_ge(hi_ready[ph], n + 1)
                nc.vector.tensor_tensor(parts_of(ph, i)[:, 1, :], hn[i % 2], parts_of(ph, i)[:, 0, :], ALU.subtract
                                        ).then_inc(lo_ready[ph], 1)

            def add_ada_bias(l):
                dst = ada_next if l else ada
                dve.wait_ge(ada_in, 32 * (l + 1))
                for i in range(4 * B):
                    b, q = divmod(i, 4)
                    cols = slice(q * 6 * C // 4, (q + 1) * 6 * C // 4)
                    dve.wait_ge(ada_mm, 4 * B * l + i + 1)
                    nc.vector.tensor_tensor(dst[:, b].rearrange("p s n -> p (s n)")[:, cols],
                                            bank(ada_bank(l, i))[:, 0:6 * C // 4], ada_b_sb[:, cols], ALU.add
                                            ).then_inc(ada_sum, 1)
                    if l and i in JOBS_AT_ADA:
                        split_weights(1, len(JOBS_AT_FC2) + JOBS_AT_ADA.index(i))

            def scale_ada(l):
                src = ada_next if l else ada
                dve.wait_ge(ada_sum, 4 * B * (l + 1))
                nc.vector.tensor_scalar(ada[:, :, 0:4:3, :], src[:, :, 0:4:3, :], HS, None, ALU.mult)
                last = nc.vector.tensor_scalar(ada[:, :, 1:5:3, :], src[:, :, 1:5:3, :], 1.0, HS,
                                               ALU.add, ALU.mult)
                if l:
                    last = nc.vector.tensor_copy(ada[:, :, 2, :], src[:, :, 2, :])
                last.then_inc(ada_ready, 1)
                dve.wait_ge(ada_ready, l + 1)

            def qkv_tile(l, t, u):
                normalise(0, t, u, NT * l + t, 2 * NT * l + t, t // TB, 0)
                low_part(0, u, NT * l + t)

            def reduce_scores(g, k, bk):
                j, i = divmod(k, 2 * TB)
                dve.wait_ge(max_mm, NS_STEPS * g + k + 1)
                nc.vector.reduce_max(row_max[:, j, i // 2, i % 2:i % 2 + 1], bank(bk), AX.X
                                     ).then_inc(max_done, 1)

            def split_maxima(g):
                at = max_parts[:].rearrange("p t (h s) -> p h t s", s=3)
                neg = neg_max[:].rearrange("p (h t) -> p h t", h=HG)
                rest = max_rest[:].rearrange("p (h t) -> p h t", h=HG)
                dve.wait_ge(max_done, NS_STEPS * (g + 1))
                nc.vector.tensor_reduce(neg_max[:], row_max[:].rearrange("p h t s -> p (h t) s"), AX.X,
                                        ALU.max, negate=True).then_inc(neg_done, 1)
                dve.wait_ge(neg_done, g + 1)
                nc.vector.tensor_copy(at[:, :, :, 0], neg).then_inc(split_done, 1)
                dve.wait_ge(split_done, 3 * g + 1)
                nc.vector.tensor_tensor(rest, neg, at[:, :, :, 0], ALU.subtract).then_inc(split_done, 1)
                dve.wait_ge(split_done, 3 * g + 2)
                nc.vector.tensor_copy(at[:, :, :, 1], rest).then_inc(split_done, 1)
                dve.wait_ge(split_done, 3 * g + 3)
                nc.vector.tensor_tensor(at[:, :, :, 2], rest, at[:, :, :, 1], ALU.subtract
                                        ).then_inc(parts_ready, 1)

            def place_maxima(g, par, bk):
                dve.wait_ge(max_turned, g + 1)
                for j in range(HG):
                    nc.vector.tensor_copy(stacks[MR:MR + MROWS, par, 1, j, :],
                                          bank16(bk, BF16)[MR:MR + MROWS, :]).then_inc(max_row, 1)

            def normalise_o(g, p, u, c, bk):
                o = bank(bk).rearrange("p (k d) -> p k d", d=VW)
                dve.wait_ge(o_turned, QC * g + c + 1)
                nc.vector.reciprocal(o_recip[:, c].unsqueeze(2), o[:, :, D:D + 1]).then_inc(recip_done, 1)
                dve.wait_ge(recip_done, QC * g + c + 1)
                t0, n = TB * u + TB // QC * c, TB // QC
                nc.vector.tensor_tensor(
                    v_sb[:, t0:t0 + n, bass.ds(p * HG, HG), 0:D],
                    o[:, :, 0:D].rearrange("p (t h) d -> p t h d", h=HG),
                    o_recip[:, c].rearrange("p (t h) -> p t h", h=HG).unsqueeze(3).to_broadcast([P, n, HG, D]),
                    ALU.mult).then_inc(o_ready, 1)

            def side_slot(g, par, n, bk, done):
                for step in steps_of(n):
                    if step[0] == "T" and step[1:] in BY_DVE:
                        _, m, j = step
                        dve.wait_ge(stack_turned, NT_STEPS * g + TURNS.index((m, j)) + 1)
                        nc.vector.tensor_copy(stacks[0:SK, par, m, j, :], bank16(side_bank(bk), BF16)[0:SK, :]
                                              ).then_inc(stack_by_dve, 1)
                    elif step[0] == "S":
                        reduce_scores(g, done, side_bank(bk))
                        done += 1
                        if done == NS_STEPS:
                            split_maxima(g)
                    elif step[0] == "M":
                        place_maxima(g, par, side_bank(bk))
                    bk += 1
                return bk, done

            jobs_done = {"high": 0, "masked": 0}

            def split_weights(l, i):
                src, n, dst_hi, dst_lo, (done, count) = JOBS[l][i]
                dve.wait_ge(*loaded(l, i))
                if l:
                    dve.wait_ge(done, count)
                nc.vector.tensor_scalar(dst_hi, raw(l, i), WS, None, ALU.mult).then_inc(w_high, 1)
                jobs_done["high"] += 1
                dve.wait_ge(w_high, jobs_done["high"])
                if dst_lo is None:
                    nc.vector.tensor_scalar(w_mask[:, 0:n], dst_hi, lo_row[:, 0:1], None, ALU.mult
                                            ).then_inc(w_masked, 1)
                    jobs_done["masked"] += 1
                    dve.wait_ge(w_masked, jobs_done["masked"])
                    dst_lo, dst_hi = dst_hi, w_mask[:, 0:n]
                nc.vector.scalar_tensor_tensor(dst_lo, raw(l, i), WS, dst_hi, ALU.mult, ALU.subtract
                                               ).then_inc(w_ready, 1)

            def attention_half(l, p, u, bk, with_side, first):
                g, done = NG * l + 2 * p + u, 0
                for n in range(SLOTS):
                    if not with_side and n in LAST_JOB_SLOTS:
                        split_weights(0, FC1_JOBS + LAST_JOB_SLOTS.index(n))
                    if n == O_SLOTS[0]:
                        normalise_o(g, p, u, 0, side_bank(bk))
                        bk += 1
                    if n == O_SLOTS[1] and not first:
                        normalise_o(g - 1, p if u else p - 1, 1 - u, 1, side_bank(bk))
                        bk += 1
                    if with_side:
                        bk, done = side_slot(g + 1, 1 - u, n, bk, done)
                return bk

            def attention():
                bk, done = 0, 0
                for n in range(SLOTS):
                    bk, done = side_slot(0, 0, n, bk, done)
                bk = attention_half(0, 0, 0, bk, True, True)
                attention_half(0, 0, 1, bk, True, False)
                with dve.Fori(1, HG - 1) as p:
                    bk = attention_half(0, p, 0, 0, True, False)
                    attention_half(0, p, 1, bk, True, False)
                bk = attention_half(0, HG - 1, 0, 0, True, False)
                bk = attention_half(0, HG - 1, 1, bk, False, False)
                normalise_o(NG - 1, HG - 1, 1, 1, side_bank(bk))

            def take_projection(l, t, u, peeled):
                n = NT * l + t
                dve.wait_ge(proj_mm, n + 1)
                if not peeled:
                    dve.wait_ge(x_mid, n - 1)
                nc.vector.scalar_tensor_tensor(y_sb[:, u, :], bank(2 + u)[:, 0:C], UN, ada[:, t // TB, 2, :],
                                               ALU.mult, ALU.mult).then_inc(proj_y, 1)

            def proj_low(l, t, u):
                dve.wait_ge(hi_ready[1], NT * l + t + 1)
                nc.vector.scalar_tensor_tensor(hs[u][:, 1, :].rearrange("p (h d) -> p h d", d=D),
                                               attended(l, t), HS,
                                               hs[u][:, 0, :].rearrange("p (h d) -> p h d", d=D),
                                               ALU.mult, ALU.subtract).then_inc(lo_ready[1], 1)

            def proj_step(l, s, u):
                def inside(lag):
                    return not isinstance(s, int) or 0 <= s - lag < NT

                n = 2 * NT * l + NT + s - 5
                if inside(5):
                    dve.wait_ge(x_mid, NT * l + s - 4)
                    nc.vector.bn_stats(bn[:, 0, :], x_sb[:, s - 5, :]).then_inc(stat_raw, 1)
                if inside(0):
                    proj_low(l, s, u)
                if inside(5):
                    dve.wait_ge(stat_raw, n + 1)
                if inside(3):
                    take_projection(l, s - 3, 1 - u, isinstance(s, int) and s - 3 < 2)
                elif inside(5):
                    nc.vector.memset(carrier[:], 0.0)
                if inside(5):
                    nc.vector.bn_aggr(mv[:, 0, :], bn[:, 0, :]).then_inc(stat_agg, 1)
                    dve.wait_ge(stat_agg, n + 1)
                    nc.vector.tensor_tensor(mean_var[:, s - 5, :], mv[:, 0, :], eps_pair[:], ALU.add
                                            ).then_inc(stat_ready, 1)

            def mlp_normalise(l, t, i):
                normalise(2, t, i % 2, NT * l + t, 2 * NT * l + NT + t, t // TB, 3)

            def new_statistics(t):
                dve.wait_ge(x_new, t + 1)
                statistics(t, 2 * NT + t)

            def mlp_chunk(l, c, last):
                for f in range(FT):
                    n = FT * (4 * l + c) + f
                    if l == 0 and f in (1, 3) and (not isinstance(c, int) or c):
                        new_statistics(4 * c - 2 + f // 2)
                    if not last and f % 2 == 0:
                        i = f // 2
                        if i:
                            low_part(2, i - 1, NT * l + 4 * (c + 1) + i - 1)
                        if i < 4:
                            mlp_normalise(l, 4 * (c + 1) + i, i)
                    dve.wait_ge(g_hi, n + 1)
                    nc.vector.scalar_tensor_tensor(gs[:, f, 1, :], g_sb[f % 2], HS, gs[:, f, 0, :],
                                                   ALU.mult, ALU.subtract).then_inc(g_split, 1)
                if last and l == 0:
                    scale_ada(1)
                    for t in range(2):
                        normalise(0, t, t, NT + t, 2 * NT + t, 0, 0)
                    for t in range(2):
                        low_part(0, t, NT + t)
                for i in range(6 if last else 4):
                    if i < 4:
                        n = NT * l + 4 * c + i
                        dve.wait_ge(fc2_mm, n + 1)
                        if i > 1 or l or not isinstance(c, int) or c:
                            dve.wait_ge(x_new, n - 1)
                        nc.vector.scalar_tensor_tensor(y_sb[:, i % 2, :], bank(4 + i % 2)[:, 0:C], UN,
                                                       fc2_bias[:], ALU.mult, ALU.add).then_inc(fc2_y, 1)
                    if l == 0 and isinstance(c, int) and c == 0 and i in JOBS_AT_FC2:
                        split_weights(1, JOBS_AT_FC2.index(i))
                    if l == 0 and 1 < i < (6 if last else 4):
                        new_statistics(4 * c + i - 2)

            def multiply_qk(t, u):
                if not isinstance(t, int) or t:
                    dve.wait_ge(qk_paired, t)
                dve.wait_ge(qk_ready, NT + t + 1)
                multiply_slices(nc.vector, t, qk_prod, 0, 2 * PAIRS)
                if not isinstance(t, int) or t > 1:
                    dve.wait_ge(qk_summed, t - 1)
                multiply_slices(nc.vector, t, qk_single[u], 2 * PAIRS, D - POOLED).then_inc(qk_mult, 1)

            def subtract_maxima(t):
                sums = bank(6)[:, 0:H * H].rearrange("p (h k) -> p h k", h=H)
                dve.wait_ge(qk_summed, t + 1)
                nc.vector.tensor_reduce(head_max, sums, AX.X, ALU.max).then_inc(head_top, 1)
                if not isinstance(t, int) or t:
                    dve.wait_ge(head_exp, t)
                dve.wait_ge(head_top, t + 1)
                nc.vector.tensor_tensor(head_s, sums, head_max.unsqueeze(2).to_broadcast([P, H, H]),
                                        ALU.subtract).then_inc(head_sub, 1)

            def weigh_v(t, u):
                e = head_e[u].rearrange("p h k -> p k h")
                dve.wait_ge(v_ready, NT + t + 1)
                dve.wait_ge(head_exp, t + 1)
                nc.vector.tensor_reduce(head_sum[u], head_e[u], AX.X, ALU.add).then_inc(head_total, 1)

                def part(dst, k0, k1):
                    n = k1 - k0
                    return nc.vector.tensor_tensor(
                        dst.rearrange("p (k h d) -> p k h d", k=n, h=H),
                        e[:, k0:k1].unsqueeze(3).to_broadcast([P, n, H, D]),
                        v_sb[:, t, k0:k1, 0:D].unsqueeze(2).to_broadcast([P, n, H, D]), ALU.mult)

                if not isinstance(t, int) or t:
                    dve.wait_ge(ev_paired, 2 * t)
                part(ev_high[0], H // 2, 3 * H // 4)
                part(ev_high[1], 3 * H // 4, H)
                dve.wait_ge(head_total, t + 1)
                nc.vector.reciprocal(head_rec[u], head_sum[u]).then_inc(head_inv, 1)
                if not isinstance(t, int) or t:
                    dve.wait_ge(ev_summed, t)
                part(ev_low, 0, H // 2).then_inc(ev_mult, 1)

            def normalise_heads(t, u):
                dve.wait_ge(head_inv, t + 1)
                dve.wait_ge(ev_summed, t + 1)
                nc.vector.tensor_tensor(v_sb[:, t, :, 0:D], bank(7)[:, 0:C].rearrange("p (h d) -> p h d", d=D),
                                        head_rec[u].unsqueeze(2).to_broadcast([P, H, D]), ALU.mult
                                        ).then_inc(head_o, 1)

            def head_step(s, u):
                def inside(lag):
                    return not isinstance(s, int) or 0 <= s - lag < NT

                if inside(0) and (not isinstance(s, int) or s > 1):
                    dve.wait_ge(lo_ready[0], NT + s - 1)
                    normalise(0, s, u, NT + s, 2 * NT + s, s // TB, 0)
                if inside(3):
                    multiply_qk(s - 3, 1 - u)
                if inside(4):
                    subtract_maxima(s - 4)
                if inside(5):
                    weigh_v(s - 5, 1 - u)
                if inside(6):
                    normalise_heads(s - 6, u)

            def spread_cond():
                nc.vector.tensor_copy(cond_bc, silu_t[:].unsqueeze(2).to_broadcast([96, 3 * B, P])
                                      ).then_inc(cond_ready, 1)

            dve.wait_ge(silu_ready, 1)
            spread_cond()
            dve.wait_ge(x_in, 16 * 4)
            for t in range(NT):
                nc.vector.bn_stats(bn_first[:, t, :], x_sb[:, t, :]).then_inc(stat_raw, 1)
            dve.wait_ge(stat_raw, NT)
            for t in range(NT):
                nc.vector.bn_aggr(mean_var[:, t, :], bn_first[:, t, :]).then_inc(stat_agg, 1)
            dve.wait_ge(stat_agg, NT)
            nc.vector.tensor_scalar(mean_var[:, :, 1:2], mean_var[:, :, 1:2], EPS, None, ALU.add
                                    ).then_inc(stat_ready, NT)
            add_ada_bias(0)
            scale_ada(0)
            for l in range(2):
                if l == 0:
                    for t in range(2):
                        qkv_tile(l, t, t)
                    with dve.Fori(1, TB) as i:
                        for u in range(2):
                            qkv_tile(l, 2 * i + u, u)
                    attention()
                    dve.wait_ge(part_step, 2 * PSTEPS * NG)
                    spread_cond()
                else:
                    dve.wait_ge(x_new, NT)
                    nc.vector.tensor_copy(ada[:, :, 5, :], ada_next[:, :, 5, :]).then_inc(gate_moved, 1)
                    dve.wait_ge(gate_moved, 1)
                    for s in range(FIRST):
                        head_step(s, s % 2)
                    with dve.Fori(FIRST // 2, LAST // 2) as i:
                        for u in range(2):
                            head_step(2 * i + u, u)
                    for s in range(LAST, NT + LAG + 1):
                        head_step(s, s % 2)
                        if s in JOB_AT:
                            split_weights(1, JOB_AT[s])
                        for n in early_proj(s):
                            if n == 0:
                                dve.wait_ge(o_loaded, 16 * TB)
                            proj_step(1, n, n % 2)
                    dve.wait_ge(o_loaded_1, 32 * TB)
                if l == 0:
                    for t in range(6):
                        proj_step(l, t, t % 2)
                with dve.Fori(TB // 2 if l else 3, TB - 2) as i:
                    for u in range(2):
                        proj_step(l, 2 * i + u, u)
                for t in range(NT - 4, NT + 5):
                    proj_step(l, t, t % 2)
                    i = t - (NT - 4)
                    if 1 < i < 6:
                        low_part(2, i - 2, NT * l + i - 2)
                    if i < 4:
                        mlp_normalise(l, i, i)
                dve.wait_ge(fc2_bias_in, 16 * (l + 1))
                mlp_chunk(l, 0, False)
                if l == 0:
                    add_ada_bias(1)
                with dve.Fori(1, 3) as c:
                    mlp_chunk(l, c, False)
                mlp_chunk(l, 3, True)

        @block.scalar
        def _(act):
            act.wait_ge(cond_in, 16 * B)
            nc.scalar.activation(silu_t[:], cond_t[:], ACT.Silu).then_inc(silu_ready, 1)

            steps = [0]

            def scale_weights(l, i):
                _, n, dst_hi, dst_lo, _ = JOBS[l][i]

                def chain(ins):
                    steps[0] += 1
                    ins.then_inc(w_scaled, 1)
                    act.wait_ge(w_scaled, steps[0])

                act.wait_ge(*loaded(l, i))
                chain(nc.scalar.activation(raw(l, i), raw(l, i), ACT.Copy, scale=WS))
                chain(nc.scalar.activation(dst_hi, raw(l, i), ACT.Copy))
                if dst_lo is None:
                    chain(nc.scalar.activation(w_mask[:, 0:n], dst_hi, ACT.Copy, scale=lo_row[:, 0:1]))

            def head_step(s, u):
                def inside(lag):
                    return not isinstance(s, int) or 0 <= s - lag < NT

                if isinstance(s, int) and s < 2:
                    if s == 0:
                        high_part(0, 0, NT, 2)
                        high_part(0, 1, NT + 1, 2)
                elif inside(0):
                    high_part(0, u, NT + s, 2)
                if inside(2):
                    take_qkv(1, s - 2, u)
                if inside(0):
                    take_hT(0, u, NT + s, hT[u])
                if inside(4):
                    t = s - 4
                    if not isinstance(s, int) or t > 1:
                        act.wait_ge(ev_mult, t - 1)
                    act.wait_ge(head_sub, t + 1)
                    nc.scalar.activation(head_e[u].rearrange("p h k -> p (h k)"),
                                         head_s.rearrange("p h k -> p (h k)"), ACT.Exp).then_inc(head_exp, 1)

            act.wait_ge(const_in, CONSTS)
            for i in range(QKV_JOBS):
                scale_weights(0, i)

            def high_part(ph, i, n, gap):
                act.wait_ge(h_ready[ph], n + 1)
                if gap:
                    act.wait_ge(turned[ph], n + 1 - gap)
                nc.scalar.activation(parts_of(ph, i)[:, 0, :], hn[i % 2], ACT.Copy).then_inc(hi_ready[ph], 1)

            def take_hT(ph, u, n, dst):
                act.wait_ge(turned[ph], n + 1)
                nc.scalar.activation(dst, bank16(u, F16)[:, 0:5 * P].rearrange("p (k n) -> p k n", k=5),
                                     ACT.Copy).then_inc(hT_ready[ph], 1)

            def take_qkv(l, t, u):
                act.wait_ge(qkv_mm, NT * l + t + 1)
                if l and isinstance(t, int) and t == 0:
                    act.wait_ge(gate_moved, 1)
                nc.scalar.activation(qk_sb[:, t, 0:C], bank(2 + 2 * u)[:, 0:C], ACT.Copy, scale=UN * D ** -0.5)
                k = ps[:, 2 + 2 * u:4 + 2 * u, :].rearrange("p b n -> p (b n)")[:, C:C + 2 * (512 - C)]
                nc.scalar.activation(qk_sb[:, t, C:2 * C].rearrange("p (x n) -> p x n", x=2),
                                     k.rearrange("p (x n) -> p x n", x=2)[:, :, 0:C // 2], ACT.Copy, scale=UN
                                     ).then_inc(qk_ready, 1)
                nc.scalar.activation(v_sb[:, t, :, 0:D], bank(3 + 2 * u)[:, C // 2:HALF].rearrange(
                    "p (h d) -> p h d", d=D), ACT.Copy, scale=UN).then_inc(v_ready, 1)

            def qkv_tile(l, t, u, peeled):
                high_part(0, u, NT * l + t, 0 if peeled and l == 0 else 2)
                if not peeled:
                    take_qkv(l, t - 2, u)
                take_hT(0, u, NT * l + t, hT[u])

            def take_stack(g, par, step, k, bk):
                act.wait_ge(stack_turned, NT_STEPS * g + k + 1)
                nc.scalar.activation(stacks[0:SK, par, step[1], step[2], :], bank16(bk, BF16)[0:SK, :],
                                     ACT.Copy).then_inc(stack_by_act, 1)

            def side_slot(g, par, n, bk, k):
                for step in steps_of(n):
                    if step[0] == "T":
                        if step[1:] not in BY_DVE:
                            take_stack(g, par, step, k, side_bank(bk))
                        k += 1
                    bk += 1
                return bk, k

            def exponents(g, n, first, u_first, after_first):
                s = SLOTS * g + n
                if not first:
                    act.wait_ge(pv_done, s - 1)
                for pair in range(2):
                    if pair and n == KT:
                        copy_o(g, 0, u_first)
                    if pair and n == 0 and not u_first:
                        copy_o(g - 1, 1, after_first)
                    act.wait_ge(scores_ready, 2 * s + pair + 1)
                    nc.scalar.activation(
                        probs[:, n % 2, 2 * pair:2 * pair + 2, :].rearrange("p h n -> p (h n)"),
                        ps[:, 2 + 2 * pair:4 + 2 * pair, :].rearrange("p b n -> p (b n)"),
                        ACT.Exp).then_inc(probs_ready, 1)

            def copy_o(g, c, first):
                act.wait_ge(pv_done, SLOTS * g + KT * (c + 1))
                if not first:
                    act.wait_ge(o_turned, QC * (g - 1) + c + 1)
                nc.scalar.activation(o_cols[:, c, :], bank(6), ACT.Copy).then_inc(o_copied, 1)

            def attention_half(l, p, u, bk, with_side, first):
                g, k = NG * l + 2 * p + u, 0
                for n in range(SLOTS):
                    exponents(g, n, first and n < 2, first, isinstance(g, int) and g == 1)
                    if n == O_SLOTS[0] or n == O_SLOTS[1] and not first:
                        bk += 1
                    if with_side:
                        bk, k = side_slot(g + 1, 1 - u, n, bk, k)
                return bk

            def attention():
                bk, k = 0, 0
                for n in range(SLOTS):
                    bk, k = side_slot(0, 0, n, bk, k)
                bk = attention_half(0, 0, 0, bk, True, True)
                attention_half(0, 0, 1, bk, True, False)
                with act.Fori(1, HG - 1) as p:
                    bk = attention_half(0, p, 0, 0, True, False)
                    attention_half(0, p, 1, bk, True, False)
                bk = attention_half(0, HG - 1, 0, 0, True, False)
                attention_half(0, HG - 1, 1, bk, False, False)
                copy_o(NG - 1, 1, False)

            def proj_step(l, s, u):
                if not isinstance(s, int) or s < NT:
                    if not isinstance(s, int) or l or s > 1:
                        act.wait_ge(turned[1], NT * l + s - 1)
                    nc.scalar.activation(hs[u][:, 0, :].rearrange("p (h d) -> p h d", d=D), attended(l, s),
                                         ACT.Copy, scale=HS).then_inc(hi_ready[1], 1)
                if not isinstance(s, int) or s:
                    take_hT(1, 1 - u, NT * l + s - 1, hT[1 - u])

            def mlp_chunk(l, c, last):
                t1 = 4 * (c + 1)
                for f in range(FT):
                    n = FT * (4 * l + c) + f
                    act.wait_ge(fc1_mm, n + 1)
                    if l or not isinstance(c, int) or c or f > 1:
                        act.wait_ge(g_split, n if f == 0 else n - 1)
                    nc.scalar.activation(g_sb[f % 2], bank(2 + f % 2), gelus[l], scale=UN).then_inc(g_ready, 1)
                    if f == 0 and (l or not isinstance(c, int) or c):
                        act.wait_ge(fc2_mm, NT * l + 4 * c)
                    act.wait_ge(g_ready, n + 1)
                    nc.scalar.activation(gs[:, f, 0, :], g_sb[f % 2], ACT.Copy, scale=HS).then_inc(g_hi, 1)
                    if not last and f % 2 == 1:
                        high_part(2, f // 2, NT * l + t1 + f // 2, 4)
                if not last:
                    for i in range(4):
                        take_hT(2, MLP_BANKS[i], NT * l + t1 + i, h2T[:, :, P * i:P * (i + 1)])

            for l in range(2):
                if l == 0:
                    for t in range(2):
                        qkv_tile(l, t, t, True)
                    with act.Fori(1, TB) as i:
                        for u in range(2):
                            qkv_tile(l, 2 * i + u, u, False)
                    for u in range(2):
                        take_qkv(l, NT - 2 + u, u)
                    attention()
                    act.wait_ge(o_ready, QC * NG)
                else:
                    for s in range(NT + LAG + 1):
                        if s == FIRST:
                            with act.Fori(FIRST // 2, LAST // 2) as i:
                                for u in range(2):
                                    head_step(2 * i + u, u)
                        if s not in PEELED:
                            continue
                        head_step(s, s % 2)
                        for n in early_proj(s):
                            if n == 0:
                                act.wait_ge(o_loaded, 16 * TB)
                            proj_step(1, n, n % 2)
                    act.wait_ge(o_loaded_1, 32 * TB)
                if l == 0:
                    for t in range(2):
                        proj_step(l, t, t)
                with act.Fori(TB // 2 if l else 1, TB - 2) as i:
                    for u in range(2):
                        proj_step(l, 2 * i + u, u)
                for i in range(6):
                    if i < 5:
                        proj_step(l, NT - 4 + i, i % 2)
                    if 0 < i < 5:
                        high_part(2, i - 1, NT * l + i - 1, 4 if l else 0)
                    if i > 1:
                        take_hT(2, FIRST_BANKS[i - 2], NT * l + i - 2, h2T[:, :, P * (i - 2):P * (i - 1)])
                mlp_chunk(l, 0, False)
                with act.Fori(1, 3) as c:
                    mlp_chunk(l, c, False)
                mlp_chunk(l, 3, True)

        @block.tensor
        def _(pe):
            def turn(ph, u, n, first, parts=None, banks=2):
                pe.wait_ge(lo_ready[ph], n + 1)
                if not first:
                    pe.wait_ge(hT_ready[ph], n + 1 - banks)
                at = bank16(u, F16)
                both = parts or hs[u]
                for s in range(2):
                    for k in range(KB):
                        blk = KB * s + k
                        nc.tensor.transpose(at[:, blk * P:(blk + 1) * P], both[:, s, k * P:(k + 1) * P], ident16[:])
                for i, part in enumerate((both[:, 0, KB * P:C], both[:, 1, KB * P:C], both[:, 0, KB * P:C],
                                          ones_blk[:])):
                    mm = nc.tensor.transpose(at[R * i:R * (i + 1), 4 * P:5 * P], part, ident16[:])
                mm.then_inc(turned[ph], 1)

            PRODUCTS = [(0, 0), (2, 0), (0, 2), (1, 1), (3, 1), (1, 3), (4, 4)]

            def qkv_mms(l, t, u, first):
                n = NT * l + t
                pe.wait_ge(hT_ready[0], n + 1)
                if not first:
                    pe.wait_ge(v_ready, n - 1)
                for i, (a, w) in enumerate(PRODUCTS):
                    for o in range(2):
                        mm = nc.tensor.matmul(bank(2 + 2 * u + o)[:, 0:HALF], hT[u][:, a, :],
                                              w_qkv[:, w, o * HALF:(o + 1) * HALF],
                                              start=(i == 0), stop=(i == len(PRODUCTS) - 1))
                mm.then_inc(qkv_mm, 1)

            def head_step(s, u):
                def inside(lag):
                    return not isinstance(s, int) or 0 <= s - lag < NT

                if inside(2):
                    qkv_mms(1, s - 2, u, isinstance(s, int) and s - 2 < 2)
                if inside(6):
                    t = s - 6
                    if not isinstance(s, int) or t:
                        pe.wait_ge(head_o, t)
                    for k in range(H // 2):
                        if k % (H // 4) == 0:
                            pe.wait_ge(ev_paired, 2 * t + 1 + k // (H // 4))
                        mm = nc.tensor.matmul(bank(7)[:, 0:C], ident[:], ev_low[:, k * C:(k + 1) * C],
                                              start=(k == 0), stop=(k == H // 2 - 1))
                    mm.then_inc(ev_summed, 1)
                if inside(0):
                    turn(0, u, NT + s, isinstance(s, int) and s < 2)
                if inside(3):
                    t = s - 3
                    if not isinstance(s, int) or t:
                        pe.wait_ge(head_sub, t)
                    pe.wait_ge(qk_paired, t + 1)
                    slices = [qk_single[1 - u][:, d * HH:(d + 1) * HH] for d in range(SINGLES)]
                    slices += [qk_pair[:, d * HH:(d + 1) * HH] for d in range(PAIRS)]
                    for i, part in enumerate(slices):
                        mm = nc.tensor.matmul(bank(6)[:, 0:HH], ident[:], part, start=(i == 0),
                                              stop=(i == len(slices) - 1))
                    mm.then_inc(qk_summed, 1)

            def stack_taken(g, m, j):
                mine = [turn for turn in TURNS if (turn in BY_DVE) == ((m, j) in BY_DVE)]
                return (stack_by_dve if (m, j) in BY_DVE else stack_by_act), len(mine) * g + mine.index((m, j)) + 1

            def side_step(g, par, step, count, bk, freed):
                sem_freed, value = freed
                pe.wait_ge(sem_freed, value)
                if step[0] == "T":
                    _, m, j = step
                    k = count["T"]
                    if k == 0:
                        pe.wait_ge(part_step, 2 * PSTEPS * (g + 1))
                    for t in range(TB):
                        mm = nc.tensor.transpose(bank16(bk, BF16)[0:SK, t * P:(t + 1) * P],
                                                 stage[:, m, t, j, :], identb[:])
                    mm.then_inc(stack_turned, 1)
                    count["T"] += 1
                    return stack_taken(g, m, j)
                if step[0] == "S":
                    _, j, t, half = step
                    k = count["S"]
                    if k % (2 * TB) == 0:
                        if ((0, j) in BY_DVE) != ((1, j) in BY_DVE):
                            pe.wait_ge(*stack_taken(g, 0, j))
                        pe.wait_ge(*stack_taken(g, 1, j))
                    nc.tensor.matmul(bank(bk), stacks[0:SK, par, 1, j, t * P:(t + 1) * P],
                                     stacks[0:SK, par, 0, j, half * 512:(half + 1) * 512],
                                     start=True, stop=True).then_inc(max_mm, 1)
                    count["S"] += 1
                    return max_done, NS_STEPS * g + k + 1
                pe.wait_ge(parts_ready, g + 1)
                for t in range(TB):
                    mm = nc.tensor.transpose(bank16(bk, BF16)[MR:MR + MROWS, t * P:(t + 1) * P],
                                             max_parts[:, t, :], identb[:])
                mm.then_inc(max_turned, 1)
                return max_row, HG * (g + 1)

            def scores(g, u, n, pair, first):
                c, kt = divmod(n, KT)
                s = SLOTS * g + n
                if not first:
                    pe.wait_ge(probs_ready, 2 * (s - 1) + pair + 1)
                if n == 0:
                    pe.wait_ge(max_row, HG * g + 2 * pair + 2)
                for j in (2 * pair, 2 * pair + 1):
                    mm = nc.tensor.matmul(bank(2 + j), stacks[0:SK, u, 0, j, kt * P:(kt + 1) * P],
                                          stacks[0:SK, u, 1, j, c * 512:(c + 1) * 512], start=True, stop=True)
                mm.then_inc(scores_ready, 1)

            def weigh(g, u, n, first):
                c, kt = divmod(n, KT)
                pe.wait_ge(probs_ready, 2 * (SLOTS * g + n) + 2)
                if n == 0:
                    pe.wait_ge(vg_ready, g + 1)
                if kt == 0 and (c or not first):
                    pe.wait_ge(o_copied, QC * g + c)
                for j in range(HG):
                    mm = nc.tensor.matmul(bank(6)[VW * j:VW * (j + 1), :], v_group[:, u, kt, j, :],
                                          probs[:, n % 2, j, :], start=(kt == 0), stop=(kt == KT - 1))
                mm.then_inc(pv_done, 1)

            def turn_o(g, c, bk, freed):
                sem_freed, value = freed
                pe.wait_ge(sem_freed, value)
                pe.wait_ge(o_copied, QC * g + c + 1)
                for q in range(TB // QC):
                    mm = nc.tensor.transpose(bank(bk)[:, q * P:(q + 1) * P], o_cols[:, c, q * P:(q + 1) * P],
                                             ident[:])
                mm.then_inc(o_turned, 1)
                return o_ready, QC * g + c + 1

            def attention_half(l, p, u, bk, recent, with_side, last, first):
                g, count = NG * l + 2 * p + u, {"T": 0, "S": 0}

                def side(steps, bk):
                    for step in steps:
                        freed = side_step(g + 1, 1 - u, step, count, side_bank(bk), recent.pop(0))
                        recent.append(freed)
                        bk += 1
                    return bk

                for n in range(SLOTS):
                    before, between, after = slot_side(n) if with_side else ([], [], [])
                    if n == O_SLOTS[0]:
                        recent.append(turn_o(g, 0, side_bank(bk), recent.pop(0)))
                        bk += 1
                    if n == O_SLOTS[1] and not first:
                        recent.append(turn_o(g - 1, 1, side_bank(bk), recent.pop(0)))
                        bk += 1
                    bk = side(before, bk)
                    if n < SLOTS - 1:
                        scores(g, u, n + 1, 0, False)
                        bk = side(between, bk)
                        scores(g, u, n + 1, 1, False)
                        bk = side(after, bk)
                        weigh(g, u, n, first)
                    else:
                        if not last:
                            scores(g + 1, 1 - u, 0, 0, False)
                        weigh(g, u, n, first)
                        if not last:
                            scores(g + 1, 1 - u, 0, 1, False)
                return bk

            def attention():
                bk, count = 0, {"T": 0, "S": 0}
                recent = [(hT_ready[0], NT - 1), (hT_ready[0], NT), (ada_sum, 4 * B)]
                for n in range(SLOTS):
                    for step in steps_of(n):
                        recent.append(side_step(0, 0, step, count, side_bank(bk), recent.pop(0)))
                        bk += 1
                pe.wait_ge(v_ready, NT)
                scores(0, 0, 0, 0, True)
                scores(0, 0, 0, 1, True)

                def at_start(p):
                    return [(max_done, NS_STEPS * (2 * p + 1) - 1), (max_done, NS_STEPS * (2 * p + 1)), (max_row, HG * (2 * p + 1))]

                recent = at_start(0)
                bk = attention_half(0, 0, 0, bk, recent, True, False, True)
                attention_half(0, 0, 1, bk, recent, True, False, False)
                with pe.Fori(1, HG - 1) as p:
                    recent = at_start(p)
                    bk = attention_half(0, p, 0, 0, recent, True, False, False)
                    attention_half(0, p, 1, bk, recent, True, False, False)
                recent = at_start(HG - 1)
                bk = attention_half(0, HG - 1, 0, 0, recent, True, False, False)
                bk = attention_half(0, HG - 1, 1, bk, recent, False, True, False)
                turn_o(NG - 1, 1, side_bank(bk), recent.pop(0))

            def proj_mms(l, t, u, first):
                n = NT * l + t
                pe.wait_ge(hT_ready[1], n + 1)
                if not first:
                    pe.wait_ge(proj_y, n - 1)
                for i, (a, w) in enumerate(PRODUCTS):
                    mm = nc.tensor.matmul(bank(2 + u)[:, 0:C], hT[u][:, a, :], w_proj[:, w, :],
                                          start=(i == 0), stop=(i == len(PRODUCTS) - 1))
                mm.then_inc(proj_mm, 1)

            def proj_step(l, s, u):
                if not isinstance(s, int) or s > 1:
                    proj_mms(l, s - 2, u, isinstance(s, int) and s < 4)
                turn(1, u, NT * l + s, isinstance(s, int) and s < 2)

            def mlp_chunk(l, c, last):
                pe.wait_ge(hT_ready[2], NT * l + 4 * (c + 1))
                for f in range(FT):
                    n = FT * (4 * l + c) + f
                    if l or not isinstance(c, int) or c or f > 1:
                        pe.wait_ge(g_ready, n if f == 0 else n - 1)
                    for i, (a, w) in enumerate(PRODUCTS):
                        mm = nc.tensor.matmul(bank(2 + f % 2), w_fc1[:, w, f * P:(f + 1) * P], h2T[:, a, :],
                                              start=(i == 0), stop=(i == len(PRODUCTS) - 1))
                    mm.then_inc(fc1_mm, 1)
                if not last:
                    for i in range(4):
                        turn(2, MLP_BANKS[i], NT * l + 4 * (c + 1) + i, False, mlp_hs[i], 4)
                pe.wait_ge(g_split, FT * (4 * l + c + 1))
                for i in range(4):
                    n = NT * l + 4 * c + i
                    if l or not isinstance(c, int) or c or i > 1:
                        pe.wait_ge(fc2_y, n - 1)
                    for f in range(FT):
                        for a, w in ((0, 0), (1, 0), (0, 1)):
                            mm = nc.tensor.matmul(bank(4 + i % 2)[:, 0:C], gs[:, f, a, i * P:(i + 1) * P],
                                                  w_fc2[:, w, f, :], start=(f == 0 and (a, w) == (0, 0)),
                                                  stop=(f == FT - 1 and (a, w) == (0, 1)))
                    mm.then_inc(fc2_mm, 1)

            def conditioning(l):
                pe.wait_ge(cond_ready, l + 1)
                pe.wait_ge(ada_in, 32 * (l + 1))
                if l:
                    pe.wait_ge(hT_ready[2], 8)
                for i in range(4 * B):
                    b, q = divmod(i, 4)
                    if l and i > 1:
                        pe.wait_ge(ada_sum, 4 * B * l + i - 1)
                    for k in range(3):
                        mm = nc.tensor.matmul(bank(ada_bank(l, i))[:, 0:6 * C // 4], cond_bc[:, k * B + b, :],
                                              ada_w_sb[:, k, q * 6 * C // 4:(q + 1) * 6 * C // 4],
                                              start=(k == 0), stop=(k == 2))
                    mm.then_inc(ada_mm, 1)

            pe.wait_ge(const_ready, 1)
            conditioning(0)
            for l in range(2):
                if l:
                    pe.wait_ge(fc2_y, NT * l)
                if l == 0:
                    pe.wait_ge(ada_sum, 4 * B)
                    turn(0, 0, 0, True)
                    turn(0, 1, 1, True)
                    pe.wait_ge(w_ready, QKV_JOBS)
                    qkv_mms(l, 0, 0, True)
                    turn(0, 0, 2, False)
                    qkv_mms(l, 1, 1, True)
                    turn(0, 1, 3, False)
                    with pe.Fori(2, TB) as i:
                        for u in range(2):
                            qkv_mms(l, 2 * i + u - 2, u, False)
                            turn(0, u, 2 * i + u, False)
                    for u in range(2):
                        qkv_mms(l, NT - 2 + u, u, False)
                    attention()
                else:
                    pe.wait_ge(w_ready, NJ + QKV_JOBS)
                    for s in range(FIRST):
                        head_step(s, s % 2)
                    with pe.Fori(FIRST // 2, LAST // 2) as i:
                        for u in range(2):
                            head_step(2 * i + u, u)
                    for s in range(LAST, NT + LAG + 1):
                        head_step(s, s % 2)
                        for n in early_proj(s):
                            if n == 0:
                                pe.wait_ge(w_ready, NJ + PROJ_JOBS)
                            proj_step(1, n, n % 2)
                if l == 0:
                    pe.wait_ge(w_ready, PROJ_JOBS)
                    for t in range(4):
                        proj_step(l, t, t % 2)
                with pe.Fori(TB // 2 if l else 2, TB - 2) as i:
                    for u in range(2):
                        proj_step(l, 2 * i + u, u)
                for i in range(4):
                    proj_step(l, NT - 4 + i, i % 2)
                    if i > 1:
                        turn(2, FIRST_BANKS[i - 2], NT * l + i - 2, True, mlp_hs[i - 2])
                for u in range(2):
                    proj_mms(l, NT - 2 + u, u, False)
                for i in (2, 3):
                    turn(2, FIRST_BANKS[i], NT * l + i, True, mlp_hs[i])
                pe.wait_ge(proj_y, NT * (l + 1))
                pe.wait_ge(w_ready, NJ * (l + 1))
                mlp_chunk(l, 0, False)
                if l == 0:
                    conditioning(1)
                    pe.wait_ge(ada_sum, 4 * B * 2)
                with pe.Fori(1, 3) as c:
                    mlp_chunk(l, c, False)
                mlp_chunk(l, 3, True)


_LAYER = [("L0_cond_W_qkv", "L1_cond_qkv_w"), ("L0_cond_b_qkv", "L1_cond_qkv_b"),
          ("L0_cond_W_proj", "L1_cond_proj_w"), ("L0_cond_b_proj", "L1_cond_proj_b"),
          ("L0_cond_W_fc1", "L1_cond_fc1_w"), ("L0_cond_b_fc1", "L1_cond_fc1_b"),
          ("L0_cond_W_fc2", "L1_cond_fc2_w"), ("L0_cond_b_fc2", "L1_cond_fc2_b"),
          ("L0_cond_W_ada", "L1_cond_ada_w"), ("L0_cond_b_ada", "L1_cond_ada_b")]


def kernel(**inputs):
    import numpy as _np
    import concourse.bacc as _bacc
    from concourse import mybir as _mybir
    from concourse.bass_utils import run_bass_kernel_spmd as _run

    nc = _bacc.Bacc("TRN2", target_bir_lowering=False, num_devices=1)
    arrays = {}

    def given(name, a):
        a = _np.ascontiguousarray(a)
        arrays[name] = a
        return nc.dram_tensor(name, a.shape, _mybir.dt.from_np(a.dtype), kind="ExternalInput").ap()

    ones_rows = _np.zeros((P, R), _np.float32)
    ones_rows[:, 0:2] = HS
    lo_rows = _np.zeros((P, 1), _np.float32)
    lo_rows[2 * R:3 * R] = 1.0
    lo_rows[3 * R + 1] = 1.0
    max_rows = _np.zeros((P, HG, MROWS), _np.float32)
    for j in range(HG):
        max_rows[:, j, 3 * j:3 * j + 3] = 1.0
    args = [given("in_x", inputs["x"]), given("in_cond", inputs["cond_1152"])]
    for pair in _LAYER:
        args.append([given("in_" + name, inputs[name]) for name in pair])
    args += [given("c_identity", _np.eye(P, dtype=_np.float32)), given("c_ones_rows", ones_rows),
             given("c_lo_rows", lo_rows), given("c_max_rows", max_rows.reshape(P, HG * MROWS)),
             given("c_zeros", _np.zeros((R, FF), _np.float32))]
    out = nc.dram_tensor("out_0", (B, L, C), F32, kind="ExternalOutput").ap()
    hidden_blocks_kernel(nc, *args, out)
    r = _run(nc, [arrays], core_ids=[0])
    return r.results[0]["out_0"]
```
